# Optimizing a Trainium2 kernel written in Bass

```python
import numpy as np
import jax
import jax.numpy as jnp

def _softmax(x, axis=-1):
    return jax.nn.softmax(x, axis=axis)

def _gelu(x):
    return jax.nn.gelu(x, approximate=True)

def _silu(x):
    return jax.nn.silu(x)

def _sigmoid(x):
    return jax.nn.sigmoid(x)

def _layernorm(x, axis=-1, eps=1e-05):
    m = jnp.mean(x, axis=axis, keepdims=True)
    v = jnp.var(x, axis=axis, keepdims=True)
    return (x - m) / jnp.sqrt(v + eps)

def _scatter_add(tgt, idx, src, axis=0):
    return tgt.at[idx].add(src)

def _segment_sum(src, seg, n):
    return jax.ops.segment_sum(src, seg, n)
kernel_name = 'mk_cond_seq_d1_seqx_r2_45b632'

def setup_inputs(seed: int=0):
    np.random.seed(seed)
    _w = jnp.asarray

    def _rec_inputs():
        import jax
        import jax.numpy as jnp
        _rk = jax.random.key(seed)
        x = -0.0002928 + 1 * jax.random.normal(jax.random.fold_in(_rk, 1), (2, 2048, 512), jnp.float32)
        _lenS = 2048 - jax.random.randint(jax.random.fold_in(_rk, 7), (2,), 0, max(1, 2048 // 4) + 1, jnp.int32)
        _lenS2 = 2048 - jax.random.randint(jax.random.fold_in(_rk, 8), (2,), 0, max(1, 2048 // 4) + 1, jnp.int32)
        cond_1024 = 0.0061147 + 1.02565 * jax.random.normal(jax.random.fold_in(_rk, 11), (2, 512), jnp.float32)
        return (x, cond_1024)
    x, cond_1024 = _rec_inputs()

    def _L0_cond_setup():
        import jax, jax.numpy as jnp
        import numpy as np
        D = 512
        H = 16
        HD = 4 * D
        B, T = (4, 512)
        EPS = 1e-05

        def _layernorm(x, g, b):
            mu = jnp.mean(x, axis=-1, keepdims=True)
            var = jnp.mean(jnp.square(x - mu), axis=-1, keepdims=True)
            return (x - mu) * jax.lax.rsqrt(var + EPS) * g + b

        def _attention(x, Wqkv, Wproj, bproj):
            b, t, c = x.shape
            hd = c // H
            qkv = (x @ Wqkv).reshape(b, t, 3, H, hd).transpose(2, 0, 3, 1, 4)
            q, k, v = (qkv[0], qkv[1], qkv[2])
            scale = hd ** (-0.5)
            scores = jnp.einsum('bhqd,bhkd->bhqk', q, k) * scale
            causal = jnp.tril(jnp.ones((t, t), bool))
            scores = jnp.where(causal, scores, -jnp.inf)
            attn = jax.nn.softmax(scores, axis=-1)
            out = jnp.einsum('bhqk,bhkd->bhqd', attn, v)
            out = out.transpose(0, 2, 1, 3).reshape(b, t, c)
            return out @ Wproj + bproj
        key = jax.random.key(seed)
        ks = jax.random.split(key, 12)
        s = 0.02
        return {'x': jax.random.normal(ks[0], (B, T, D), jnp.float32), 'condition': jax.random.normal(ks[1], (B, D), jnp.float32), 'Wqkv': jax.random.normal(ks[2], (D, 3 * D), jnp.float32) * s, 'Wproj': jax.random.normal(ks[3], (D, D), jnp.float32) * s, 'bproj': jnp.zeros((D,), jnp.float32), 'W1': jax.random.normal(ks[4], (D, HD), jnp.float32) * s, 'b1': jnp.zeros((HD,), jnp.float32), 'W2': jax.random.normal(ks[5], (HD, D), jnp.float32) * s, 'b2': jnp.zeros((D,), jnp.float32), 'g1': jnp.ones((D,), jnp.float32), 'be1': jnp.zeros((D,), jnp.float32), 'g2': jnp.ones((D,), jnp.float32), 'be2': jnp.zeros((D,), jnp.float32), 'Wada': jax.random.normal(ks[6], (D, 6 * D), jnp.float32) * s, 'bada': jax.random.normal(ks[7], (6 * D,), jnp.float32) * s}
    _L0_cond_all = _L0_cond_setup()
    _L0_cond_in = {k: v for k, v in _L0_cond_all.items() if k in ('Wqkv', 'Wproj', 'bproj', 'W1', 'b1', 'W2', 'b2', 'g1', 'be1', 'g2', 'be2', 'Wada', 'bada')}
    del _L0_cond_all
    return {'x': x, 'cond_1024': cond_1024, 'L0_cond_Wqkv': _L0_cond_in['Wqkv'], 'L0_cond_Wproj': _L0_cond_in['Wproj'], 'L0_cond_bproj': _L0_cond_in['bproj'], 'L0_cond_W1': _L0_cond_in['W1'], 'L0_cond_b1': _L0_cond_in['b1'], 'L0_cond_W2': _L0_cond_in['W2'], 'L0_cond_b2': _L0_cond_in['b2'], 'L0_cond_g1': _L0_cond_in['g1'], 'L0_cond_be1': _L0_cond_in['be1'], 'L0_cond_g2': _L0_cond_in['g2'], 'L0_cond_be2': _L0_cond_in['be2'], 'L0_cond_Wada': _L0_cond_in['Wada'], 'L0_cond_bada': _L0_cond_in['bada']}

def reference(x, cond_1024, L0_cond_Wqkv, L0_cond_Wproj, L0_cond_bproj, L0_cond_W1, L0_cond_b1, L0_cond_W2, L0_cond_b2, L0_cond_g1, L0_cond_be1, L0_cond_g2, L0_cond_be2, L0_cond_Wada, L0_cond_bada):
    import jax
    import jax.numpy as jnp

    def _L0_cond_ref(x, condition, Wqkv, Wproj, bproj, W1, b1, W2, b2, g1, be1, g2, be2, Wada, bada):
        import jax, jax.numpy as jnp
        import numpy as np
        D = 512
        H = 16
        HD = 4 * D
        B, T = (4, 512)
        EPS = 1e-05

        def _layernorm(x, g, b):
            mu = jnp.mean(x, axis=-1, keepdims=True)
            var = jnp.mean(jnp.square(x - mu), axis=-1, keepdims=True)
            return (x - mu) * jax.lax.rsqrt(var + EPS) * g + b

        def _attention(x, Wqkv, Wproj, bproj):
            b, t, c = x.shape
            hd = c // H
            qkv = (x @ Wqkv).reshape(b, t, 3, H, hd).transpose(2, 0, 3, 1, 4)
            q, k, v = (qkv[0], qkv[1], qkv[2])
            scale = hd ** (-0.5)
            scores = jnp.einsum('bhqd,bhkd->bhqk', q, k) * scale
            causal = jnp.tril(jnp.ones((t, t), bool))
            scores = jnp.where(causal, scores, -jnp.inf)
            attn = jax.nn.softmax(scores, axis=-1)
            out = jnp.einsum('bhqk,bhkd->bhqd', attn, v)
            out = out.transpose(0, 2, 1, 3).reshape(b, t, c)
            return out @ Wproj + bproj
        mod = jax.nn.silu(condition) @ Wada + bada
        sh_a, sc_a, gt_a, sh_m, sc_m, gt_m = jnp.split(mod, 6, axis=1)
        xn = _layernorm(x, g1, be1)
        xm = xn * (1.0 + sc_a[:, None, :]) + sh_a[:, None, :]
        x = x + gt_a[:, None, :] * _attention(xm, Wqkv, Wproj, bproj)
        xn = _layernorm(x, g2, be2)
        xm = xn * (1.0 + sc_m[:, None, :]) + sh_m[:, None, :]
        h = jax.nn.gelu(xm @ W1 + b1, approximate=False)
        x = x + gt_m[:, None, :] * (h @ W2 + b2)
        return x
    x = _L0_cond_ref(x, cond_1024, L0_cond_Wqkv, L0_cond_Wproj, L0_cond_bproj, L0_cond_W1, L0_cond_b1, L0_cond_W2, L0_cond_b2, L0_cond_g1, L0_cond_be1, L0_cond_g2, L0_cond_be2, L0_cond_Wada, L0_cond_bada)
    return x

_drawn_inputs = setup_inputs


def setup_inputs(seed=0):
    import zlib

    import numpy as np

    out = dict(_drawn_inputs(seed))
    spreads = {'L0_cond_bproj': (0.0, 0.29),
     'L0_cond_b1': (0.0, 0.536),
     'L0_cond_b2': (0.0, 0.315),
     'L0_cond_g1': (1.0, 0.6),
     'L0_cond_be1': (0.0, 0.8),
     'L0_cond_g2': (1.0, 0.6),
     'L0_cond_be2': (0.0, 0.8)}
    factors = {'L0_cond_Wqkv': 3.22, 'L0_cond_Wproj': 3.374, 'L0_cond_bada': 8.0}
    for name, (base, spread) in spreads.items():
        noise = np.random.default_rng([zlib.crc32(name.encode()), seed]).standard_normal(out[name].shape)
        drawn = base * np.exp(spread * noise) if base else spread * noise
        out[name] = jnp.asarray(drawn.astype(out[name].dtype))
    for name, factor in factors.items():
        out[name] = (out[name] * factor).astype(out[name].dtype)
    return out
```

```python
from contextlib import ExitStack

import concourse.bass as bass
from concourse import mybir

F32 = mybir.dt.float32
F32R = mybir.dt.float32r
BF16 = mybir.dt.bfloat16
ACT = mybir.ActivationFunctionType
ALU = mybir.AluOpType
AX = mybir.AxisListType

P = 128
BATCH, SEQ, D = 2, 2048, 512
HEADS, HD = 16, 32
HID = 4 * D
TOK = BATCH * SEQ
KT = D // P
HT = HID // P
CH = 512
NCH = TOK // CH
TT = CH // P
GH = P // HD
NG = BATCH * HEADS // GH
KEYT = SEQ // P
QC = SEQ // CH
SCALE = float(HD) ** -0.5
EPS = 1e-5
NEG = -1e30
LOWEST = -3e38

V_BADA, V_G1, V_BE1, V_G2, V_BE2, V_B1 = 0, 24, 28, 32, 36, 40
V_ROWS = 56
M_SHA, M_SCA, M_GTA, M_SHM, M_SCM, M_GTM = 0, 4, 8, 12, 16, 20


def raw(ap):
    return ap.bitcast(F32)


def terms(a_hi, a_lo, b_hi, b_lo):
    return ((a_hi, b_hi), (a_lo, b_hi), (a_hi, b_lo))


def await_count(eng, carrier, sem, value):
    eng.wait_ge(sem, value)
    eng.sem_inc(carrier, 1)


class Common:

    def __init__(self, nc, ctx):
        def sb(name, shape, dt=F32):
            return ctx.enter_context(nc.sbuf_tensor(name, shape, dt))

        def dram(name, shape):
            return nc.dram_tensor(name, shape, F32, kind="Internal").ap()

        self.ident = sb("ident", [P, P])
        self.ident_bf = sb("ident_bf", [P, P], BF16)
        self.mask_qk = sb("mask_qk", [P, P], BF16)
        self.mask_kq = sb("mask_kq", [P, P], BF16)
        self.ones = sb("ones", [P, P])
        self.vcol = sb("vcol", [P, V_ROWS])
        self.cond_t = sb("cond_t", [P, KT, BATCH])
        self.mod = sb("mod", [P, BATCH, 24])
        self.aff1 = sb("aff1", [P, BATCH, 2, KT])
        self.aff2 = sb("aff2", [P, BATCH, 2, KT])
        self.gate = sb("gate", [P, 2, BATCH, D])
        self.qk = dram("qk_scratch", (2, 2, D, TOK))
        self.v = dram("v_scratch", (TOK, D))
        self.m = dram("m_scratch", (NG, 2, GH * KEYT, P))
        self.o = dram("o_scratch", (NG, P, SEQ))
        self.x2 = dram("x2_scratch", (TOK, D))
        self.xm2 = dram("xm2_scratch", (2, D, TOK))


def wave(eng, body, pairs, last_differs=True):
    with eng.Fori(0, pairs - 1) as i:
        for u in range(2):
            body(2 * i + u, u, True)
    for u in range(2):
        body(2 * (pairs - 1) + u, u, u == 0)


def newton_rstd(nc, dve, link, ve, sd, r, t):
    link(nc.vector.reciprocal(r, sd))
    link(nc.vector.tensor_tensor(t, r, r, ALU.mult))
    link(nc.vector.tensor_tensor(t, t, ve, ALU.mult))
    link(nc.vector.tensor_scalar(t, t, -0.5, 1.5, ALU.mult, ALU.add))
    link(nc.vector.tensor_tensor(r, r, t, ALU.mult))


def phase_qkv(nc, K, x, cond, wada, bada, vecs, wqkv):
    with ExitStack() as ctx:
        def sb(name, shape, dt=F32):
            return ctx.enter_context(nc.sbuf_tensor(name, shape, dt))

        def pb(name, shape):
            return ctx.enter_context(nc.psum_tensor(name, shape, F32))

        def sem(name):
            return ctx.enter_context(nc.semaphore(name))

        AHEAD = 5
        NT = 3 * D // P
        w_raw = sb("w_raw", [P, KT, 3 * D])
        w_hi = sb("w_hi", [P, KT, 3 * D], F32R)
        w_lo = sb("w_lo", [P, KT, 3 * D], F32R)
        ada = sb("ada", [P, KT, 2 * D])
        vrow = sb("vrow", [V_ROWS, P])
        cnd = sb("cnd", [BATCH, 3, D])
        xs = sb("xs", [P, 2, TT, D])
        xn = sb("xn", [P, TT, D])
        y32 = sb("y32", [P, 2, CH])
        xm_hi = sb("xm_hi", [P, 2, KT, CH], F32R)
        xm_lo = sb("xm_lo", [P, 2, KT, CH], F32R)
        st_hi = sb("st_hi", [P, 2, KT, CH], F32R)
        st_lo = sb("st_lo", [P, 2, KT, CH], F32R)
        st_v = sb("st_v", [P, TT, D])
        bst = sb("bst", [P, TT, 6])
        mv = sb("mv", [P, TT, 2])
        ve = sb("ve", [P, TT])
        sd = sb("sd", [P, TT])
        rstd = sb("rstd", [P, TT])
        tmp = sb("tmp", [P, TT])
        one_sc = sb("one_sc", [P, BATCH, KT])
        tp = [pb(f"tp{i}", [P, CH]) for i in range(2)]
        acc = [pb(f"acc{i}", [P, CH]) for i in range(4)]
        misc = pb("misc", [P, CH])

        c_ready = sem("a_constants_ready")
        v_loaded = sem("a_vectors_loaded")
        ada_loaded = sem("a_ada_loaded")
        w_loaded = sem("a_w_loaded")
        w_hi_ready = sem("a_w_hi_ready")
        w_split = sem("a_w_split")
        silu_e = sem("a_silu_exp_ready")
        silu_r = sem("a_silu_ready")
        small_pe = sem("a_small_pe")
        small_dve = sem("a_small_dve")
        x_loaded = [sem(f"a_x_loaded{u}") for u in range(2)]
        x_free = sem("a_x_free")
        var_ready = sem("a_var_ready")
        sd_ready = sem("a_sd_ready")
        xn_ready = sem("a_xn_ready")
        tp_ready = sem("a_tp_ready")
        tp_free = sem("a_tp_free")
        xm_ready = sem("a_xm_ready")
        acc_ready = sem("a_acc_ready")
        acc_free = sem("a_acc_free")
        hi_ready = sem("a_hi_ready")
        v_ready = sem("a_v_ready")
        qk_stored = [sem(f"a_{n}_stored") for n in "qk"]
        v_stored = sem("a_v_stored")
        chain = sem("a_dve_chain")
        held = sem("a_wait_carrier")
        block = ctx.enter_context(nc.Block())

        @block.sync
        def _(sp):
            sp.dma_start(cnd[:, 0, :], cond).then_inc(v_loaded, 16)
            for at, v in vecs:
                n = v.shape[0] // P
                sp.dma_start(vrow[at:at + n, :], v.rearrange("(t p) -> t p", p=P)).then_inc(v_loaded, 16)
            sp.dma_start(ada[:, :, :], wada[:, 0:2 * D].rearrange("(t p) n -> p t n", p=P)).then_inc(ada_loaded, 16)
            for t in range(KT):
                sp.dma_start(w_raw[:, t, :], wqkv[t * P:(t + 1) * P, :]).then_inc(w_loaded, 16)
            with nc.sync.Fori(0, NCH // 2) as i:
                for u in range(2):
                    n = 2 * i + u
                    await_count(sp, held, x_free, n + 1)
                    sp.dma_start(xs[:, u, :, :],
                                 x[bass.ds(n * CH, CH), :].rearrange("(t p) d -> p t d", p=P)).then_inc(x_loaded[u], 16)

        @block.gpsimd
        def _(pool):
            nc.gpsimd.memset(K.ident[:, :], 0.0).then_inc(c_ready, 1)
            nc.gpsimd.memset(K.ident_bf[:, :], 0.0).then_inc(c_ready, 1)
            nc.gpsimd.memset(K.mask_qk[:, :], 0.0).then_inc(c_ready, 1)
            nc.gpsimd.memset(K.mask_kq[:, :], 0.0).then_inc(c_ready, 1)
            nc.gpsimd.memset(K.ones[:, :], 1.0).then_inc(c_ready, 1)
            pool.wait_ge(c_ready, 5)
            for m in (K.ident, K.ident_bf):
                nc.gpsimd.affine_select(out=m[:, :], in_=m[:, :], compare_op=ALU.not_equal, fill=1.0, base=0,
                                        pattern=[[-1, P]], channel_multiplier=1).then_inc(c_ready, 1)
            for m, step in ((K.mask_qk, 1), (K.mask_kq, -1)):
                nc.gpsimd.affine_select(out=m[:, :], in_=m[:, :], compare_op=ALU.is_ge, fill=NEG, base=0,
                                        pattern=[[-step, P]], channel_multiplier=step).then_inc(c_ready, 1)

        @block.scalar
        def _(act):
            act.wait_ge(v_loaded, 16 * (1 + len(vecs)))
            nc.scalar.activation(cnd[:, 1, :], cnd[:, 0, :], ACT.Exp, scale=-1.0).then_inc(silu_e, 1)
            act.wait_ge(w_loaded, 16 * KT)
            for t in range(KT):
                nc.scalar.activation(w_hi[:, t, :], w_raw[:, t, :], ACT.Copy).then_inc(w_hi_ready, 1)

            def std(n):
                act.wait_ge(var_ready, n + 1)
                nc.scalar.activation(sd[:, :], ve[:, :], ACT.Sqrt).then_inc(sd_ready, 1)

            def body(n, u, more):
                if more:
                    std(n + 1)
                for j in range(2 * KT):
                    act.wait_ge(acc_ready, NT * n + j + 1 + 1)
                    nc.scalar.activation(st_hi[:, j // KT, j % KT, :], acc[j % 4][:, :], ACT.Copy).then_inc(hi_ready, 1)
                    if j == KT:
                        store_qk(n, 0)
                store_qk(n, 1)
                act.wait_ge(v_ready, n + 1)
                act.dma_start(K.v[bass.ds(n * CH, CH), :].rearrange("(t p) d -> p t d", p=P),
                              st_v[:, :, :]).then_inc(v_stored, 16)
                for half in range(2):
                    act.wait_ge(qk_stored[half], 32 * (n + 1))
                act.wait_ge(v_stored, 16 * (n + 1))

            def store_qk(n, half):
                act.wait_ge(acc_free, NT * n + KT * (half + 1) + 4)
                for part, st in enumerate((st_hi, st_lo)):
                    act.dma_start(K.qk[half, part, :, bass.ds(n * CH, CH)].rearrange("(t p) n -> p t n", p=P),
                                  raw(st[:, half, :, :])).then_inc(qk_stored[half], 16)

            std(0)
            wave(nc.scalar, body, NCH // 2)

        @block.vector
        def _(dve):
            links = [0]

            def link(ins):
                links[0] += 1
                ins.then_inc(chain, 1)
                dve.wait_ge(chain, links[0])

            dve.wait_ge(silu_e, 1)
            link(nc.vector.tensor_scalar(cnd[:, 2, :], cnd[:, 1, :], 1.0, None, ALU.add))
            link(nc.vector.reciprocal(cnd[:, 1, :], cnd[:, 2, :]))
            nc.vector.tensor_tensor(cnd[:, 2, :], cnd[:, 1, :], cnd[:, 0, :], ALU.mult).then_inc(silu_r, 1)
            dve.wait_ge(small_pe, 1)
            nc.vector.tensor_copy(K.vcol[:, :], misc[:, 0:V_ROWS]).then_inc(small_dve, 1)
            dve.wait_ge(small_pe, 2)
            nc.vector.tensor_copy(K.cond_t[:, :, :], misc[:, 64:64 + KT * BATCH].rearrange("p (t b) -> p t b", b=BATCH)).then_inc(small_dve, 1)
            dve.wait_ge(small_dve, 1)
            dve.wait_ge(small_pe, 3)
            mod_ps = misc[:, 128:128 + 8 * BATCH].rearrange("p (m b) -> p b m", b=BATCH)
            for b in range(BATCH):
                link(nc.vector.tensor_tensor(K.mod[:, b, 0:8], mod_ps[:, b, :], K.vcol[:, V_BADA:V_BADA + 8], ALU.add))
                link(nc.vector.tensor_scalar(one_sc[:, b, :], K.mod[:, b, M_SCA:M_SCA + KT], 1.0, None, ALU.add))
                link(nc.vector.tensor_tensor(K.aff1[:, b, 0, :], one_sc[:, b, :], K.vcol[:, V_G1:V_G1 + KT], ALU.mult))
                link(nc.vector.tensor_tensor(K.aff1[:, b, 1, :], one_sc[:, b, :], K.vcol[:, V_BE1:V_BE1 + KT], ALU.mult))
                link(nc.vector.tensor_tensor(K.aff1[:, b, 1, :], K.aff1[:, b, 1, :], K.mod[:, b, M_SHA:M_SHA + KT], ALU.add))
            for t in range(KT):
                dve.wait_ge(w_hi_ready, t + 1)
                nc.vector.tensor_tensor(w_lo[:, t, :], w_raw[:, t, :], raw(w_hi[:, t, :]), ALU.subtract).then_inc(w_split, 1)
            dve.sem_inc(x_free, 2)
            dve.sem_inc(tp_free, 2)
            dve.sem_inc(acc_free, 4)
            base = links[0]
            CHAINS = 7

            def norm(n, u):
                at = [0]

                def lk(ins):
                    at[0] += 1
                    ins.then_inc(chain, 1)
                    dve.wait_ge(chain, n * CHAINS + base + at[0])

                dve.wait_ge(x_loaded[u], (n // 2) * 16 + 16)
                for t in range(TT - 1):
                    nc.vector.bn_stats(bst[:, t, :], xs[:, u, t, :])
                lk(nc.vector.bn_stats(bst[:, TT - 1, :], xs[:, u, TT - 1, :]))
                dve.sem_inc(held, 1)
                for t in range(TT - 1):
                    nc.vector.bn_aggr(mv[:, t, :], bst[:, t, :])
                lk(nc.vector.bn_aggr(mv[:, TT - 1, :], bst[:, TT - 1, :]))
                nc.vector.tensor_scalar(ve[:, :], mv[:, :, 1], EPS, None, ALU.add).then_inc(var_ready, 1)
                dve.wait_ge(sd_ready, n + 1)
                newton_rstd(nc, dve, lk, ve[:, :], sd[:, :], rstd[:, :], tmp[:, :])
                dve.wait_ge(tp_ready, n * KT + 1)
                for t in range(TT):
                    nc.vector.tensor_scalar(xn[:, t, :], xs[:, u, t, :], mv[:, t, 0:1], rstd[:, t:t + 1],
                                            ALU.subtract, ALU.mult).then_inc(xn_ready, 1)
                dve.wait_ge(xn_ready, TT * (n + 1))
                dve.sem_inc(x_free, 1)

            def modulate(n, u, t):
                b = n // (NCH // BATCH)
                dve.wait_ge(tp_ready, n * KT + t + 1 + 1)
                nc.vector.tensor_scalar(y32[:, t % 2, :], tp[t % 2][:, :], aff(b, 0, t), aff(b, 1, t),
                                        ALU.mult, ALU.add).then_inc(tp_free, 1)
                dve.wait_ge(tp_free, n * KT + t + 1 + 2)
                nc.vector.tensor_copy(xm_hi[:, u, t, :], y32[:, t % 2, :]).then_inc(xm_ready, 1)
                dve.wait_ge(xm_ready, 2 * (n * KT + t) + 1)
                nc.vector.tensor_tensor(xm_lo[:, u, t, :], y32[:, t % 2, :], raw(xm_hi[:, u, t, :]),
                                        ALU.subtract).then_inc(xm_ready, 1)

            def aff(b, which, t):
                if isinstance(b, int):
                    return K.aff1[:, b, which, t:t + 1]
                return K.aff1[:, bass.ds(b, 1), which, t:t + 1]

            def body(n, u, more):
                if more:
                    norm(n + 1, 1 - u)
                    dve.wait_ge(acc_ready, NT * n + 1)
                for j in range(NT):
                    if more and 0 <= j - AHEAD < KT:
                        modulate(n + 1, 1 - u, j - AHEAD)
                    if j < 2 * KT:
                        dve.wait_ge(hi_ready, 2 * KT * n + j + 1)
                        nc.vector.tensor_tensor(st_lo[:, j // KT, j % KT, :], acc[j % 4][:, :],
                                                raw(st_hi[:, j // KT, j % KT, :]), ALU.subtract).then_inc(acc_free, 1)
                    else:
                        dve.wait_ge(acc_ready, NT * n + j + 1 + 1)
                        ins = nc.vector.tensor_copy(st_v[:, j - 2 * KT, :], acc[j % 4][:, :])
                        ins.then_inc(acc_free, 1)
                dve.wait_ge(acc_free, NT * (n + 1) + 4)
                dve.sem_inc(v_ready, 1)

            norm(0, 0)
            for t in range(KT):
                modulate(0, 0, t)
            wave(nc.vector, body, NCH // 2)

        @block.tensor
        def _(pe):
            pe.wait_ge(c_ready, 9)
            pe.wait_ge(v_loaded, 16 * (1 + len(vecs)))
            nc.tensor.transpose(misc[:, 0:V_ROWS], vrow[:, :], K.ident[0:V_ROWS, 0:V_ROWS]).then_inc(small_pe, 1)
            pe.wait_ge(silu_r, 1)
            pe.wait_ge(small_dve, 1)
            for t in range(KT):
                ins = nc.tensor.transpose(misc[:, 64 + t * BATCH:64 + (t + 1) * BATCH], cnd[:, 2, t * P:(t + 1) * P],
                                          K.ident[0:BATCH, 0:BATCH])
            ins.then_inc(small_pe, 1)
            pe.wait_ge(small_dve, 2)
            pe.wait_ge(ada_loaded, 16)
            for m in range(8):
                for t in range(KT):
                    ins = nc.tensor.matmul(misc[:, 128 + m * BATCH:128 + (m + 1) * BATCH], ada[:, t, m * P:(m + 1) * P],
                                           K.cond_t[:, t, :], start=(t == 0), stop=(t == KT - 1))
            ins.then_inc(small_pe, 1)
            pe.sem_inc(tp_ready, 1)
            pe.sem_inc(acc_ready, 1)

            def turn(n, t):
                pe.wait_ge(tp_free, n * KT + t + 1)
                if t == 0:
                    pe.wait_ge(xn_ready, TT * (n + 1))
                for s in range(TT):
                    ins = nc.tensor.transpose(tp[t % 2][:, s * P:(s + 1) * P], xn[:, s, t * P:(t + 1) * P], K.ident[:, :])
                ins.then_inc(tp_ready, 1)

            def body(n, u, more):
                pe.wait_ge(xm_ready, 2 * KT * (n + 1))
                for j in range(NT):
                    if more and 0 <= j - AHEAD < KT:
                        turn(n + 1, j - AHEAD)
                    pe.wait_ge(acc_free, NT * n + j + 1)
                    for t in range(KT):
                        if j < 2 * KT:
                            cols = slice(j * P, (j + 1) * P)
                            ops = terms(w_hi[:, t, cols], w_lo[:, t, cols], xm_hi[:, u, t, :], xm_lo[:, u, t, :])
                        else:
                            cols = slice((j - 2 * KT) * P, (j - 2 * KT + 1) * P)
                            ops = terms(xm_hi[:, u, t, cols], xm_lo[:, u, t, cols], w_hi[:, t, 2 * D:], w_lo[:, t, 2 * D:])
                        for k, (a, b) in enumerate(ops):
                            ins = nc.tensor.matmul(acc[j % 4][:, :], a, b, start=(t == 0 and k == 0),
                                                   stop=(t == KT - 1 and k == 2))
                    ins.then_inc(acc_ready, 1)

            for t in range(KT):
                turn(0, t)
            pe.wait_ge(w_split, KT)
            wave(nc.tensor, body, NCH // 2)


class Plan:

    def __init__(self):
        self.steps = [(c, kt) for c in range(QC) for kt in range((c + 1) * TT)]
        self.NS = len(self.steps)
        self.first = [self.steps.index((c, 0)) for c in range(QC)]
        self.last = [self.steps.index((c, (c + 1) * TT - 1)) for c in range(QC)]
        self.jobs = [(h, qt, kc, min(CH, (qt + 1) * P - kc * CH))
                     for h in range(GH) for qt in range(KEYT) for kc in range(qt // TT + 1)]
        self.NJ = len(self.jobs)
        self.JOBS = self.NJ + 2
        self.adds, done = [], 0
        self.released = []
        for s, (c, kt) in enumerate(self.steps):
            if c >= 1 and kt >= 2:
                done += 1
                self.adds.append(s)
            self.released.append(done + 1 if c >= 1 and kt == 1 else done)
        self.NA = done
        weight = [CH - max(0, kt - c * TT) * P for c, kt in self.steps]
        FROM, TO = 2, self.NS - 4
        span = sum(weight[FROM:TO])
        cost = sum(w + 64 for *_, w in self.jobs)
        self.jobs_at, at, spent, passed = [[] for _ in self.steps], 0, 0, 0
        for s in range(FROM, TO):
            passed += weight[s]
            while at < self.NJ and (spent + (self.jobs[at][3] + 64) / 2) * span <= passed * cost:
                self.jobs_at[s].append(at)
                spent += self.jobs[at][3] + 64
                at += 1
        while at < self.NJ:
            self.jobs_at[TO - 1].append(at)
            at += 1
        self.turns_at = TO + 1

    def mid(self, s):
        c, kt = self.steps[s]
        return max(0, kt - c * TT) * P


def phase_attention(nc, K):
    L = Plan()
    ROWS, MROWS = 3 * HD, 3 * HD + 2
    BUF = 4
    with ExitStack() as ctx:
        def sb(name, shape, dt=F32):
            return ctx.enter_context(nc.sbuf_tensor(name, shape, dt))

        def pb(name, shape):
            return ctx.enter_context(nc.psum_tensor(name, shape, F32))

        def sem(name):
            return ctx.enter_context(nc.semaphore(name))

        k_st = sb("k_st", [P, 2, GH, SEQ], F32R)
        q_st = sb("q_st", [P, 2, GH, CH], F32R)
        qx_st = sb("qx_st", [P, 2, SEQ], F32R)
        v_sb = sb("v_sb", [P, 2, KEYT, P])
        prob = sb("prob", [P, BUF, GH, CH])
        psum_k = sb("psum_k", [P, 2, GH, CH])
        rinv = sb("rinv", [P, CH])
        o_sb = sb("o_sb", [P, 2, CH])
        part = sb("part", [P, GH, KEYT, QC])
        mcol = sb("mcol", [P, GH * KEYT])
        m_hi = sb("m_hi", [GH * KEYT // 2, 2, P], F32R)
        m_lo = sb("m_lo", [GH * KEYT // 2, 2, P], F32R)
        st = [pb(f"st{i}", [P, 2, CH]) for i in range(2)]
        mx = [pb(f"mx{i}", [P, CH]) for i in range(2)]
        o_ps = pb("o_ps", [P, CH])
        r_ps = pb("r_ps", [P, CH])

        ones_ready = sem("b_ones_ready")
        part_ready = sem("b_part_ready")
        k_loaded = [[sem(f"b_k_loaded{u}{h}") for h in range(GH)] for u in range(2)]
        v_loaded = [sem(f"b_v_loaded{u}") for u in range(2)]
        q_loaded = [sem(f"b_q_loaded{u}") for u in range(2)]
        qx_loaded = [sem(f"b_qx_loaded{u}") for u in range(2)]
        m_ready = sem("b_m_ready")
        m_stored = sem("b_m_stored")
        mx_ready = sem("b_mx_ready")
        mx_free = sem("b_mx_free")
        mcol_ready = sem("b_mcol_ready")
        st_ready = sem("b_st_ready")
        exp_done = sem("b_exp_done")
        pv_done = sem("b_pv_done")
        pool_added = sem("b_pool_added")
        dve_added = sem("b_dve_added")
        o_ready = sem("b_o_ready")
        o_free = sem("b_o_free")
        rinv_ready = sem("b_rinv_ready")
        o_stored = [sem(f"b_o_stored{u}") for u in range(2)]
        o_sb_free = sem("b_o_sb_free")
        held = sem("b_wait_carrier")
        block = ctx.enter_context(nc.Block())

        def st_count(g, pairs):
            return 2 * L.NS * g + pairs + 1

        def exp_count(g, pairs):
            return 2 * L.NS * g + pairs + 2

        def pv_count(g, steps):
            return L.NS * g + steps + BUF

        def add_count(g, n):
            return L.NA * g + n + L.NA

        def o_reuse(g, c):
            return QC * g + 1 + (2 if c == 3 else 0)

        def per_group(eng, body):
            with eng.Fori(0, NG // 2 - 1) as i:
                for u in range(2):
                    body(2 * i + u, u, True)
            body(NG - 2, 0, True)
            body(NG - 1, 1, False)

        @block.sync
        def _(sp):
            def place(g):
                return g // (HEADS // GH), g % (HEADS // GH)

            def load_k(g, u, h):
                b, gg = place(g)
                for row, hl in enumerate((0, 1, 0)):
                    sp.dma_start(raw(k_st[row * HD:(row + 1) * HD, u, h, :]),
                                 K.qk[1, hl, bass.ds(gg * P + h * HD, HD), bass.ds(b * SEQ, SEQ)]).then_inc(k_loaded[u][h], 16)

            def load_qx(g, h):
                b, gg = place(g)
                for row, hl in enumerate((0, 0, 1)):
                    sp.dma_start(raw(qx_st[row * HD:(row + 1) * HD, h % 2, :]),
                                 K.qk[0, hl, bass.ds(gg * P + h * HD, HD), bass.ds(b * SEQ, SEQ)]).then_inc(qx_loaded[h % 2], 16)

            def load_v(g, u):
                b, gg = place(g)
                sp.dma_start(v_sb[:, u, :, :],
                             K.v[bass.ds(b * SEQ, SEQ), bass.ds(gg * P, P)].rearrange("(t p) d -> p t d", p=P)).then_inc(v_loaded[u], 16)

            def load_q(g, c):
                b, gg = place(g)
                for row, hl in enumerate((0, 0, 1)):
                    sp.dma_start(raw(q_st[row * HD:(row + 1) * HD, c % 2, :, :]),
                                 K.qk[0, hl, bass.ds(gg * P, P), bass.ds(b * SEQ + c * CH, CH)]
                                 .rearrange("(h r) n -> r h n", r=HD)).then_inc(q_loaded[c % 2], 16)
                m = K.m[g, :, :, :] if isinstance(g, int) else K.m[bass.ds(g, 1), :, :, :].rearrange("g a r n -> (g a) r n")
                sp.dma_start(raw(q_st[ROWS:MROWS, c % 2, :, :]),
                             m.rearrange("a (h c t) n -> a h c (t n)", h=GH, c=QC)[:, :, c, :]).then_inc(q_loaded[c % 2], 16)

            def store_m(g):
                await_count(sp, held, m_ready, 4 * (g + 1))
                for half in range(2):
                    rows = slice(half * GH * KEYT // 2, (half + 1) * GH * KEYT // 2)
                    for hl, t in enumerate((m_hi, m_lo)):
                        dst = K.m[g, hl, rows, :] if isinstance(g, int) else K.m[bass.ds(g, 1), hl, rows, :].rearrange("g r n -> (g r) n")
                        sp.dma_start(dst, raw(t[:, half, :])).then_inc(m_stored, 16)
                await_count(sp, held, m_stored, 64 * (g + 1))

            def store_o(g, c):
                await_count(sp, held, rinv_ready, 2 * (QC * g + c + 1))
                dst = K.o[g, :, c * CH:(c + 1) * CH] if isinstance(g, int) else \
                    K.o[bass.ds(g, 1), :, c * CH:(c + 1) * CH].rearrange("g r n -> (g r) n")
                sp.dma_start(dst, o_sb[:, c % 2, :]).then_inc(o_stored[c % 2], 16)

            def stored_o(g, c):
                await_count(sp, held, o_stored[c % 2], 16 * (2 * g + c // 2 + 1))
                sp.sem_inc(o_sb_free, 1)

            for h in range(GH):
                load_k(0, 0, h)
                if h < 2:
                    load_qx(0, h)
            load_v(0, 0)
            for h in range(2, GH):
                await_count(sp, held, mx_ready, (h - 1) * L.NJ // GH)
                load_qx(0, h)
            store_m(0)
            load_q(0, 0)

            def body(g, u, more):
                await_count(sp, held, st_ready, st_count(g, 0))
                load_q(g, 1)
                if more:
                    for h in range(2):
                        load_qx(g + 1, h)
                        load_k(g + 1, 1 - u, h)
                    for h in range(2, GH):
                        load_k(g + 1, 1 - u, h)
                    await_count(sp, held, pv_done, pv_count(g, 0))
                    load_v(g + 1, 1 - u)
                await_count(sp, held, st_ready, st_count(g, 2 * (L.last[0] + 1)))
                load_q(g, 2)
                store_o(g, 0)
                await_count(sp, held, st_ready, st_count(g, 2 * (L.last[1] + 1)))
                load_q(g, 3)
                stored_o(g, 0)
                if more:
                    await_count(sp, held, mx_ready, L.JOBS * (g + 1) + L.NJ // GH)
                    load_qx(g + 1, 2)
                store_o(g, 1)
                if more:
                    await_count(sp, held, mx_ready, L.JOBS * (g + 1) + 2 * L.NJ // GH)
                    load_qx(g + 1, 3)
                stored_o(g, 1)
                store_o(g, 2)
                if more:
                    store_m(g + 1)
                    await_count(sp, held, st_ready, st_count(g, 2 * (L.last[2] + 1)))
                    load_q(g + 1, 0)
                stored_o(g, 2)
                store_o(g, 3)
                stored_o(g, 3)

            per_group(nc.sync, body)

        @block.gpsimd
        def _(pool):
            nc.gpsimd.memset(raw(k_st[ROWS:MROWS, :, :, :]), 1.0).then_inc(ones_ready, 1)
            pool.sem_inc(pool_added, L.NA)

            def body(g, u, more):
                n = 0
                for s in L.adds:
                    c, kt = L.steps[s]
                    m = L.mid(s)
                    n += 1
                    dst = psum_k[:, c % 2, 0:GH - 1, m:]
                    pool.wait_ge(exp_done, exp_count(g, 2 * s + 2))
                    if kt == 2:
                        pool.wait_ge(o_ready, o_reuse(g, c))
                        src = prob[:, (s - 1) % BUF, 0:GH - 1, m:]
                    else:
                        pool.wait_ge(pool_added, add_count(g, n - 1))
                        src = dst
                    nc.gpsimd.tensor_tensor(dst, src, prob[:, s % BUF, 0:GH - 1, m:], ALU.add).then_inc(pool_added, 1)

            per_group(nc.gpsimd, body)

        @block.scalar
        def _(act):
            act.sem_inc(exp_done, 2)

            def body(g, u, more):
                for s in range(L.NS):
                    m = L.mid(s)
                    for p in range(2):
                        if p == 0:
                            act.wait_ge(pv_done, pv_count(g, s + 1 - BUF))
                            n = L.released[s - BUF] if s >= BUF else L.released[s - BUF] - L.NA
                            act.wait_ge(pool_added, add_count(g, n))
                            act.wait_ge(dve_added, add_count(g, n))
                        act.wait_ge(st_ready, st_count(g, 2 * s + p + 1))
                        nc.scalar.activation(prob[:, s % BUF, 2 * p:2 * p + 2, m:], st[p][:, :, m:], ACT.Exp,
                                             scale=SCALE).then_inc(exp_done, 1)

            per_group(nc.scalar, body)

        @block.vector
        def _(dve):
            dve.sem_inc(dve_added, L.NA)
            dve.sem_inc(mx_free, 2)
            dve.sem_inc(o_free, 1)
            nc.vector.memset(part[:, :, :, :], LOWEST).then_inc(part_ready, 1)
            dve.wait_ge(part_ready, 1)

            def job(g, j):
                h, qt, kc, w = L.jobs[j]
                dve.wait_ge(mx_ready, L.JOBS * g + j + 1)
                nc.vector.tensor_reduce(part[:, h, qt, kc:kc + 1], mx[j % 2][:, 0:w], AX.X, ALU.max).then_inc(mx_free, 1)

            def turns(g):
                dve.wait_ge(mx_free, L.JOBS * g + L.NJ + 2)
                nc.vector.tensor_reduce(mcol[:, :], part[:, :, :, :].rearrange("p h q k -> p (h q) k"),
                                        AX.X, ALU.max).then_inc(mcol_ready, 1)
                for half in range(2):
                    j = L.NJ + half
                    dve.wait_ge(mx_ready, L.JOBS * g + j + 1)
                    m = mx[j % 2][0:GH * KEYT // 2, 0:P]
                    nc.vector.tensor_scalar(m_hi[:, half, :], m, -1.0, None, ALU.mult).then_inc(m_ready, 1)
                    dve.wait_ge(m_ready, 4 * g + 2 * half + 1)
                    nc.vector.scalar_tensor_tensor(out=m_lo[:, half, :], in0=m, scalar=-1.0, in1=raw(m_hi[:, half, :]),
                                                   op0=ALU.mult, op1=ALU.subtract).then_inc(m_ready, 1)
                    dve.wait_ge(m_ready, 4 * g + 2 * half + 2)
                    dve.sem_inc(mx_free, 1)

            def finish(g, c):
                dve.wait_ge(o_ready, QC * g + c + 1 + 1)
                nc.vector.reciprocal(rinv[:, :], r_ps[:, :]).then_inc(rinv_ready, 1)
                dve.wait_ge(rinv_ready, 2 * (QC * g + c) + 1)
                dve.wait_ge(o_sb_free, QC * g + c + 1)
                nc.vector.tensor_tensor(o_sb[:, c % 2, :], o_ps[:, :], rinv[:, :], ALU.mult).then_inc(rinv_ready, 1)
                dve.wait_ge(rinv_ready, 2 * (QC * g + c) + 2)
                dve.sem_inc(o_free, 1)

            def add(g, s):
                c, kt = L.steps[s]
                if s not in L.adds:
                    return
                m, n = L.mid(s), L.adds.index(s) + 1
                dst = psum_k[:, c % 2, GH - 1, m:]
                dve.wait_ge(exp_done, exp_count(g, 2 * s + 2))
                if kt == 2:
                    dve.wait_ge(o_ready, o_reuse(g, c))
                    src = prob[:, (s - 1) % BUF, GH - 1, m:]
                else:
                    dve.wait_ge(dve_added, add_count(g, n - 1))
                    src = dst
                nc.vector.tensor_tensor(dst, src, prob[:, s % BUF, GH - 1, m:], ALU.add).then_inc(dve_added, 1)

            def body(g, u, more):
                for s in range(L.NS + 2):
                    if s - 2 in L.last:
                        finish(g, L.last.index(s - 2))
                    if more and s < L.NS:
                        for j in L.jobs_at[s]:
                            job(g + 1, j)
                        if s == L.turns_at:
                            turns(g + 1)
                    if 1 <= s <= L.NS:
                        add(g, s - 1)

            dve.sem_inc(o_sb_free, 2)
            for j in range(L.NJ):
                job(0, j)
            turns(0)
            per_group(nc.vector, body)

        @block.tensor
        def _(pe):
            pe.sem_inc(st_ready, 1)
            pe.sem_inc(pv_done, BUF)
            pe.sem_inc(o_ready, 1)
            pe.wait_ge(ones_ready, 1)

            def job(g, u, j):
                h, qt, kc, w = L.jobs[j]
                if j % (L.NJ // GH) == 0:
                    pe.wait_ge(k_loaded[u][h], 48 * (g // 2 + 1))
                    pe.wait_ge(qx_loaded[h % 2], 48 * (2 * g + h // 2 + 1))
                pe.wait_ge(mx_free, L.JOBS * g + j + 1)
                out = mx[j % 2]
                diagonal = (qt + 1) * P <= (kc + 1) * CH
                ins = nc.tensor.matmul(out[:, 0:w], qx_st[0:ROWS, h % 2, qt * P:(qt + 1) * P],
                                       k_st[0:ROWS, u, h, kc * CH:kc * CH + w], start=True, stop=not diagonal)
                if diagonal:
                    ins = nc.tensor.matmul(out[:, w - P:w], K.ident_bf[:, :], K.mask_qk[:, :], start=False, stop=True)
                ins.then_inc(mx_ready, 1)

            def turns(g):
                pe.wait_ge(mcol_ready, g + 1)
                for half in range(2):
                    j = L.NJ + half
                    pe.wait_ge(mx_free, L.JOBS * g + j + 1)
                    nc.tensor.transpose(mx[j % 2][0:GH * KEYT // 2, 0:P], mcol[:, half * GH * KEYT // 2:(half + 1) * GH * KEYT // 2],
                                        K.ident[:, :]).then_inc(mx_ready, 1)

            def scores(g, u, s):
                c, kt = L.steps[s]
                m = L.mid(s)
                if kt == 0:
                    pe.wait_ge(q_loaded[c % 2], 64 * (2 * g + c // 2 + 1))
                for p in range(2):
                    pe.wait_ge(exp_done, exp_count(g, 2 * s + p - 1))
                    for h in (2 * p, 2 * p + 1):
                        out = st[p][:, h % 2, :]
                        ins = nc.tensor.matmul(out[:, m:], k_st[0:MROWS, u, h, kt * P:(kt + 1) * P],
                                               q_st[0:MROWS, c % 2, h, m:], start=True, stop=kt < c * TT)
                        if kt >= c * TT:
                            ins = nc.tensor.matmul(out[:, m:m + P], K.ident_bf[:, :], K.mask_kq[:, :], start=False, stop=True)
                    ins.then_inc(st_ready, 1)

            def product(g, u, s):
                c, kt = L.steps[s]
                m = L.mid(s)
                end = s == L.last[c]
                if s == 0:
                    pe.wait_ge(v_loaded[u], 16 * (g // 2 + 1))
                if kt == 0:
                    pe.wait_ge(o_free, QC * g + c + 1)
                pe.wait_ge(exp_done, exp_count(g, 2 * s + 2))
                for h in range(GH):
                    rows = slice(h * HD, (h + 1) * HD)
                    ins = nc.tensor.matmul(o_ps[rows, m:], v_sb[:, u, kt, rows], prob[:, s % BUF, h, m:],
                                           start=(kt == 0), stop=end)
                if c == 0 or kt == 0:
                    for h in range(GH):
                        ins = nc.tensor.matmul(r_ps[h * HD:(h + 1) * HD, m:], K.ones[:, 0:HD], prob[:, s % BUF, h, m:],
                                               start=(kt == 0), stop=end)
                ins.then_inc(pv_done, 1)
                if end and c == 0:
                    pe.wait_ge(pv_done, pv_count(g, s + 1))
                    pe.sem_inc(o_ready, 1)

            def total(g, c):
                n = L.adds.index(L.last[c]) + 1
                pe.wait_ge(pool_added, add_count(g, n))
                pe.wait_ge(dve_added, add_count(g, n))
                for h in range(GH):
                    ins = nc.tensor.matmul(r_ps[h * HD:(h + 1) * HD, :], K.ones[:, 0:HD], psum_k[:, c % 2, h, :],
                                           start=False, stop=True)
                ins.then_inc(o_ready, 1)

            def body(g, u, more):
                for s in range(L.NS + 2):
                    if s - 2 in L.last[1:]:
                        total(g, L.last.index(s - 2))
                    if s < L.NS:
                        scores(g, u, s)
                        if more:
                            for j in L.jobs_at[s]:
                                job(g + 1, 1 - u, j)
                            if s == L.turns_at:
                                turns(g + 1)
                    if 1 <= s <= L.NS:
                        product(g, u, s - 1)

            for j in range(L.NJ):
                job(0, 0, j)
            turns(0)
            per_group(nc.tensor, body)


def phase_project(nc, K, x, wada, wproj, bproj):
    with ExitStack() as ctx:
        def sb(name, shape, dt=F32):
            return ctx.enter_context(nc.sbuf_tensor(name, shape, dt))

        def pb(name, shape):
            return ctx.enter_context(nc.psum_tensor(name, shape, F32))

        def sem(name):
            return ctx.enter_context(nc.semaphore(name))

        M0, M1 = M_GTA, M_GTM + KT
        ada = sb("ada2", [P, KT, (M1 - M0) * P])
        w_raw = sb("p_raw", [P, KT, D])
        w_hi = sb("p_hi", [P, KT, D], F32R)
        w_lo = sb("p_lo", [P, KT, D], F32R)
        bias = sb("p_bias", [1, D])
        bias_hi = sb("p_bias_hi", [1, D], F32R)
        bias_lo = sb("p_bias_lo", [1, D], F32R)
        one_row = sb("p_one_row", [1, P], F32R)
        one_sc = sb("p_one_sc", [P, BATCH, KT])
        diag = sb("p_diag", [P, 2, P])
        gate = K.gate
        o_in = sb("o_in", [P, 2, KT, CH])
        o_hi = sb("o_hi", [P, KT, CH], F32R)
        o_lo = sb("o_lo", [P, KT, CH], F32R)
        xs = sb("p_xs", [P, 2, TT, D])
        gated = sb("p_gated", [P, 2, D])
        xn = sb("p_xn", [P, TT, D])
        y32 = sb("p_y32", [P, 2, CH])
        xm_hi = sb("p_xm_hi", [P, KT, CH], F32R)
        xm_lo = sb("p_xm_lo", [P, KT, CH], F32R)
        bst = sb("p_bst", [P, TT, 6])
        mv = sb("p_mv", [P, TT, 2])
        ve = sb("p_ve", [P, TT])
        sd = sb("p_sd", [P, TT])
        rstd = sb("p_rstd", [P, TT])
        tmp = sb("p_tmp", [P, TT])
        tp = [pb(f"p_tp{i}", [P, CH]) for i in range(2)]
        acc = [pb(f"p_acc{i}", [P, D]) for i in range(TT)]
        misc = pb("p_misc", [P, CH])
        gps = pb("p_gps", [P, D])

        w_loaded = sem("p_w_loaded")
        ada_loaded = sem("p_ada_loaded")
        w_hi_ready = sem("p_w_hi_ready")
        w_split = sem("p_w_split")
        mod_ready = sem("p_mod_ready")
        diag_ready = sem("p_diag_ready")
        gate_ready = sem("p_gate_ready")
        gate_done = sem("p_gate_done")
        chain = sem("p_dve_chain")
        o_loaded = [sem(f"p_o_loaded{u}") for u in range(2)]
        x_loaded = [sem(f"p_x_loaded{u}") for u in range(2)]
        o_free = sem("p_o_free")
        hi_ready = sem("p_hi_ready")
        lo_ready = sem("p_lo_ready")
        acc_ready = sem("p_acc_ready")
        acc_free = sem("p_acc_free")
        x2_ready = sem("p_x2_ready")
        x2_stored = [sem(f"p_x2_stored{u}") for u in range(2)]
        x_free = sem("p_x_free")
        var_ready = sem("p_var_ready")
        sd_ready = sem("p_sd_ready")
        xn_ready = sem("p_xn_ready")
        tp_ready = sem("p_tp_ready")
        tp_free = sem("p_tp_free")
        xm_ready = sem("p_xm_ready")
        xm_stored = sem("p_xm_stored")
        xm_free = sem("p_xm_free")
        held = sem("c_wait_carrier")
        block = ctx.enter_context(nc.Block())

        @block.sync
        def _(sp):
            sp.dma_start(bias[:, :], bproj.rearrange("(a n) -> a n", a=1)).then_inc(w_loaded, 16)
            sp.dma_start(w_raw[:, :, :], wproj.rearrange("(t p) n -> p t n", p=P)).then_inc(w_loaded, 16)
            with nc.sync.Fori(0, NCH // 2) as i:
                for u in range(2):
                    n = 2 * i + u
                    b = n // (NCH // BATCH)
                    await_count(sp, held, o_free, n + 1)
                    sp.dma_start(o_in[:, u, :, :],
                                 K.o[bass.ds(b * KT, KT), :, bass.ds((n % (NCH // BATCH)) * CH, CH)].rearrange("g p n -> p g n")).then_inc(o_loaded[u], 16)
                    await_count(sp, held, x_free, n + 1)
                    sp.dma_start(xs[:, u, :, :],
                                 x[bass.ds(n * CH, CH), :].rearrange("(t p) d -> p t d", p=P)).then_inc(x_loaded[u], 16)

        @block.gpsimd
        def _(pool):
            pool.dma_start(ada[:, :, :], wada[:, M0 * P:M1 * P].rearrange("(t p) n -> p t n", p=P)).then_inc(ada_loaded, 16)

            def body(n, u):
                for t in range(KT):
                    pool.wait_ge(hi_ready, KT * n + t + 1)
                    if t == 0:
                        pool.wait_ge(acc_ready, TT * n + 1)
                    nc.gpsimd.tensor_tensor(o_lo[:, t, :], o_in[:, u, t, :], raw(o_hi[:, t, :]), ALU.subtract).then_inc(lo_ready, 1)
                pool.wait_ge(lo_ready, KT * (n + 1))
                pool.sem_inc(o_free, 1)

            pool.sem_inc(o_free, 2)
            with nc.gpsimd.Fori(0, NCH // 2) as i:
                for u in range(2):
                    body(2 * i + u, u)

        @block.scalar
        def _(act):
            act.wait_ge(w_loaded, 32)
            nc.scalar.activation(bias_hi[:, :], bias[:, :], ACT.Copy).then_inc(w_hi_ready, 1)
            nc.scalar.activation(w_hi[:, :, :], w_raw[:, :, :], ACT.Copy).then_inc(w_hi_ready, 1)

            def high(n, u):
                act.wait_ge(o_loaded[u], 16 * (n // 2) + 16)
                act.wait_ge(acc_ready, TT * n + 1)
                for t in range(KT):
                    nc.scalar.activation(o_hi[:, t, :], o_in[:, u, t, :], ACT.Copy).then_inc(hi_ready, 1)

            def body(n, u, more):
                if more:
                    high(n + 1, 1 - u)
                act.wait_ge(var_ready, n + 1)
                nc.scalar.activation(sd[:, :], ve[:, :], ACT.Sqrt).then_inc(sd_ready, 1)
                act.wait_ge(x2_ready, n + 1)
                act.dma_start(K.x2[bass.ds(n * CH, CH), :].rearrange("(t p) d -> p t d", p=P),
                              xs[:, u, :, :]).then_inc(x2_stored[u], 16)
                act.wait_ge(xm_ready, 2 * KT * (n + 1))
                for hl, t in enumerate((xm_hi, xm_lo)):
                    act.dma_start(K.xm2[hl, :, bass.ds(n * CH, CH)].rearrange("(t p) n -> p t n", p=P),
                                  raw(t[:, :, :])).then_inc(xm_stored, 16)
                act.wait_ge(x2_stored[u], 16 * (n // 2) + 16)
                act.sem_inc(x_free, 1)
                act.wait_ge(xm_stored, 32 * (n + 1))
                act.sem_inc(xm_free, 1)

            act.sem_inc(x_free, 2)
            act.sem_inc(xm_free, 1)
            high(0, 0)
            wave(nc.scalar, body, NCH // 2)

        @block.vector
        def _(dve):
            links = [0]

            def link(ins):
                links[0] += 1
                ins.then_inc(chain, 1)
                dve.wait_ge(chain, links[0])

            link(nc.vector.memset(raw(one_row[:, :]), 1.0))
            dve.wait_ge(w_hi_ready, 1)
            link(nc.vector.tensor_tensor(bias_lo[:, :], bias[:, :], raw(bias_hi[:, :]), ALU.subtract))
            dve.wait_ge(w_hi_ready, 2)
            nc.vector.tensor_tensor(w_lo[:, :, :], w_raw[:, :, :], raw(w_hi[:, :, :]), ALU.subtract).then_inc(w_split, 1)
            dve.wait_ge(mod_ready, 1)
            mod_ps = misc[:, 0:(M1 - M0) * BATCH].rearrange("p (m b) -> p b m", b=BATCH)
            for b in range(BATCH):
                link(nc.vector.tensor_tensor(K.mod[:, b, M0:M1], mod_ps[:, b, :], K.vcol[:, V_BADA + M0:V_BADA + M1], ALU.add))
                link(nc.vector.tensor_scalar(one_sc[:, b, :], K.mod[:, b, M_SCM:M_SCM + KT], 1.0, None, ALU.add))
                link(nc.vector.tensor_tensor(K.aff2[:, b, 0, :], one_sc[:, b, :], K.vcol[:, V_G2:V_G2 + KT], ALU.mult))
                link(nc.vector.tensor_tensor(K.aff2[:, b, 1, :], one_sc[:, b, :], K.vcol[:, V_BE2:V_BE2 + KT], ALU.mult))
                link(nc.vector.tensor_tensor(K.aff2[:, b, 1, :], K.aff2[:, b, 1, :], K.mod[:, b, M_SHM:M_SHM + KT], ALU.add))
            n = 0
            for which, m in enumerate((M_GTA, M_GTM)):
                for b in range(BATCH):
                    for t in range(KT):
                        if n >= 2:
                            dve.wait_ge(gate_ready, n - 1)
                        nc.vector.tensor_scalar(diag[:, n % 2, :], K.ident[:, :], K.mod[:, b, m + t:m + t + 1], None,
                                                ALU.mult).then_inc(diag_ready, 1)
                        n += 1
                    dve.wait_ge(gate_ready, n)
                    nc.vector.tensor_copy(gate[:, which, b, :], gps[:, :]).then_inc(gate_done, 1)
            dve.wait_ge(gate_done, 2 * BATCH)
            dve.sem_inc(tp_free, 2)
            dve.sem_inc(acc_free, TT)
            base = links[0]
            CHAINS = 2 + 5

            def body(n, u, more):
                at = [0]
                b = n // (NCH // BATCH)

                def lk(ins):
                    at[0] += 1
                    ins.then_inc(chain, 1)
                    dve.wait_ge(chain, n * CHAINS + base + at[0])

                def of_batch(t, *rest):
                    return t[(slice(None), *((b if isinstance(b, int) else bass.ds(b, 1)) if r is None else r for r in rest))]

                dve.wait_ge(x_loaded[u], 16 * (n // 2) + 16)
                for t in range(TT):
                    dve.wait_ge(acc_ready, TT * n + t + 1 + 1)
                    nc.vector.tensor_tensor(gated[:, t % 2, :], acc[t][:, :], of_batch(gate, 0, None, slice(None)),
                                            ALU.mult).then_inc(acc_free, 1)
                    dve.wait_ge(acc_free, TT * n + t + 1 + TT)
                    ins = nc.vector.tensor_tensor(xs[:, u, t, :], gated[:, t % 2, :], xs[:, u, t, :], ALU.add)
                ins.then_inc(x2_ready, 1)
                dve.wait_ge(x2_ready, n + 1)
                for t in range(TT - 1):
                    nc.vector.bn_stats(bst[:, t, :], xs[:, u, t, :])
                lk(nc.vector.bn_stats(bst[:, TT - 1, :], xs[:, u, TT - 1, :]))
                dve.sem_inc(held, 1)
                for t in range(TT - 1):
                    nc.vector.bn_aggr(mv[:, t, :], bst[:, t, :])
                lk(nc.vector.bn_aggr(mv[:, TT - 1, :], bst[:, TT - 1, :]))
                nc.vector.tensor_scalar(ve[:, :], mv[:, :, 1], EPS, None, ALU.add).then_inc(var_ready, 1)
                dve.wait_ge(sd_ready, n + 1)
                newton_rstd(nc, dve, lk, ve[:, :], sd[:, :], rstd[:, :], tmp[:, :])
                for t in range(TT):
                    nc.vector.tensor_scalar(xn[:, t, :], xs[:, u, t, :], mv[:, t, 0:1], rstd[:, t:t + 1],
                                            ALU.subtract, ALU.mult).then_inc(xn_ready, 1)
                for t in range(KT):
                    dve.wait_ge(tp_ready, n * KT + t + 1)
                    nc.vector.tensor_scalar(y32[:, t % 2, :], tp[t % 2][:, :], of_batch(K.aff2, None, 0, slice(t, t + 1)),
                                            of_batch(K.aff2, None, 1, slice(t, t + 1)), ALU.mult, ALU.add).then_inc(tp_free, 1)
                    dve.wait_ge(tp_free, n * KT + t + 1 + 2)
                    if t == 0:
                        dve.wait_ge(xm_free, n + 1)
                    nc.vector.tensor_copy(xm_hi[:, t, :], y32[:, t % 2, :]).then_inc(xm_ready, 1)
                    dve.wait_ge(xm_ready, 2 * (n * KT + t) + 1)
                    nc.vector.tensor_tensor(xm_lo[:, t, :], y32[:, t % 2, :], raw(xm_hi[:, t, :]),
                                            ALU.subtract).then_inc(xm_ready, 1)

            wave(nc.vector, body, NCH // 2)

        @block.tensor
        def _(pe):
            pe.sem_inc(acc_ready, 1)
            pe.wait_ge(ada_loaded, 16)
            for m in range(M1 - M0):
                for t in range(KT):
                    ins = nc.tensor.matmul(misc[:, m * BATCH:(m + 1) * BATCH], ada[:, t, m * P:(m + 1) * P],
                                           K.cond_t[:, t, :], start=(t == 0), stop=(t == KT - 1))
            ins.then_inc(mod_ready, 1)
            for n in range(2 * BATCH * KT):
                pe.wait_ge(diag_ready, n + 1)
                if n % KT == 0 and n:
                    pe.wait_ge(gate_done, n // KT)
                nc.tensor.matmul(gps[:, (n % KT) * P:(n % KT + 1) * P], K.ones[:, :], diag[:, n % 2, :],
                                 start=True, stop=True).then_inc(gate_ready, 1)
            pe.wait_ge(w_split, 1)

            def project(n):
                for s in range(TT):
                    pe.wait_ge(acc_free, TT * n + s + 1)
                    if s == 0:
                        pe.wait_ge(lo_ready, KT * (n + 1))
                    cols = slice(s * P, (s + 1) * P)
                    nc.tensor.matmul(acc[s][:, :], one_row[:, :], bias_hi[:, :], start=True, stop=False)
                    nc.tensor.matmul(acc[s][:, :], one_row[:, :], bias_lo[:, :], start=False, stop=False)
                    for t in range(KT):
                        for k, (a, b) in enumerate(terms(o_hi[:, t, cols], o_lo[:, t, cols], w_hi[:, t, :], w_lo[:, t, :])):
                            ins = nc.tensor.matmul(acc[s][:, :], a, b, start=False, stop=(t == KT - 1 and k == 2))
                    ins.then_inc(acc_ready, 1)

            def body(n, u, more):
                if more:
                    project(n + 1)
                for t in range(KT):
                    pe.wait_ge(tp_free, n * KT + t + 1)
                    if t == 0:
                        pe.wait_ge(xn_ready, TT * (n + 1))
                    for s in range(TT):
                        ins = nc.tensor.transpose(tp[t % 2][:, s * P:(s + 1) * P], xn[:, s, t * P:(t + 1) * P], K.ident[:, :])
                    ins.then_inc(tp_ready, 1)

            project(0)
            wave(nc.tensor, body, NCH // 2)


def phase_mlp(nc, K, w1, w2, b2, out):
    with ExitStack() as ctx:
        def sb(name, shape, dt=F32):
            return ctx.enter_context(nc.sbuf_tensor(name, shape, dt))

        def pb(name, shape):
            return ctx.enter_context(nc.psum_tensor(name, shape, F32))

        def sem(name):
            return ctx.enter_context(nc.semaphore(name))

        PIECE = CH
        NP = HID // PIECE
        LAG = 2
        w1_hi = sb("w1_hi", [P, NP, KT, PIECE], F32R)
        w1_lo = sb("w1_lo", [P, NP, KT, PIECE], F32R)
        w2_hi = sb("w2_hi", [P, NP, KT, D], F32R)
        w2_lo = sb("w2_lo", [P, NP, KT, D], F32R)
        w_raw = sb("m_raw", [P, KT, CH])
        bias = sb("m_bias", [1, D])
        bias_hi = sb("m_bias_hi", [1, D], F32R)
        bias_lo = sb("m_bias_lo", [1, D], F32R)
        one_row = sb("m_one_row", [1, P], F32R)
        xm = sb("m_xm", [P, 2, KT, CH], F32R)
        xs = sb("m_xs", [P, TT, D])
        g32 = sb("m_g32", [P, 2, CH])
        g_hi = sb("m_g_hi", [P, 4, CH], F32R)
        g_lo = sb("m_g_lo", [P, 4, CH], F32R)
        gated = sb("m_gated", [P, 1, D])
        hid = [pb(f"m_hid{i}", [P, CH]) for i in range(4)]
        acc = [pb(f"m_acc{i}", [P, D]) for i in range(TT)]

        b_loaded = sem("m_b_loaded")
        w_loaded = sem("m_w_loaded")
        w_hi_ready = sem("m_w_hi_ready")
        w_split = sem("m_w_split")
        bias_ready = sem("m_bias_ready")
        xm_loaded = sem("m_xm_loaded")
        x_loaded = sem("m_x_loaded")
        hid_ready = sem("m_hid_ready")
        hid_free = sem("m_hid_free")
        g_hi_ready = sem("m_g_hi_ready")
        g_ready = sem("m_g_ready")
        used = sem("m_used")
        acc_ready = sem("m_acc_ready")
        acc_free = sem("m_acc_free")
        out_ready = sem("m_out_ready")
        out_stored = sem("m_out_stored")
        held = sem("m_wait_carrier")
        block = ctx.enter_context(nc.Block())

        @block.sync
        def _(sp):
            sp.dma_start(bias[:, :], b2.rearrange("(a n) -> a n", a=1)).then_inc(b_loaded, 16)
            for i in range(2 * NP):
                k = i // 2
                src = w1[:, k * PIECE:(k + 1) * PIECE] if i % 2 == 0 else w2[k * CH:(k + 1) * CH, :]
                if i:
                    await_count(sp, held, w_split, i)
                sp.dma_start(w_raw[:, :, :], src.rearrange("(t p) n -> p t n", p=P)).then_inc(w_loaded, 16)
            with nc.sync.Fori(0, NCH) as n:
                await_count(sp, held, used, HT * n + 1)
                sp.dma_start(raw(xm[:, :, :, :]), K.xm2[:, :, bass.ds(n * CH, CH)].rearrange("a (t p) n -> p a t n", p=P)).then_inc(xm_loaded, 16)
                sp.dma_start(xs[:, :, :], K.x2[bass.ds(n * CH, CH), :].rearrange("(t p) d -> p t d", p=P)).then_inc(x_loaded, 16)
                await_count(sp, held, out_ready, TT * (n + 1))
                sp.dma_start(out[bass.ds(n * CH, CH), :].rearrange("(t p) d -> p t d", p=P), xs[:, :, :]).then_inc(out_stored, 16)
                await_count(sp, held, out_stored, 16 * (n + 1))

        @block.gpsimd
        def _(pool):
            pass

        @block.scalar
        def _(act):
            act.wait_ge(b_loaded, 16)
            nc.scalar.activation(bias_hi[:, :], bias[:, :], ACT.Copy).then_inc(bias_ready, 1)
            for i in range(2 * NP):
                act.wait_ge(w_loaded, 16 * (i + 1))
                dst = (w1_hi if i % 2 == 0 else w2_hi)[:, i // 2, :, :]
                nc.scalar.activation(dst, w_raw[:, :, :], ACT.Copy).then_inc(w_hi_ready, 1)
            with nc.scalar.Fori(0, NCH) as n:
                for j in range(HT):
                    act.wait_ge(hid_ready, HT * n + j + 1)
                    act.wait_ge(g_ready, HT * n + j + 1)
                    nc.scalar.activation(g32[:, j % 2, :], hid[j % 4][:, :], ACT.Gelu,
                                         bias=K.vcol[:, V_B1 + j:V_B1 + j + 1]).then_inc(hid_free, 1)
                    act.wait_ge(hid_free, HT * n + j + 1 + 4)
                    act.wait_ge(used, HT * n + j + 1)
                    nc.scalar.activation(g_hi[:, j % 4, :], g32[:, j % 2, :], ACT.Copy).then_inc(g_hi_ready, 1)

        @block.vector
        def _(dve):
            nc.vector.memset(raw(one_row[:, :]), 1.0).then_inc(bias_ready, 1)
            dve.wait_ge(bias_ready, 2)
            nc.vector.tensor_tensor(bias_lo[:, :], bias[:, :], raw(bias_hi[:, :]), ALU.subtract).then_inc(bias_ready, 1)
            for i in range(2 * NP):
                dve.wait_ge(w_hi_ready, i + 1)
                hi, lo = ((w1_hi, w1_lo) if i % 2 == 0 else (w2_hi, w2_lo))
                nc.vector.tensor_tensor(lo[:, i // 2, :, :], w_raw[:, :, :], raw(hi[:, i // 2, :, :]), ALU.subtract).then_inc(w_split, 1)
            dve.sem_inc(hid_free, 4)
            dve.sem_inc(g_ready, 2)
            dve.sem_inc(acc_free, TT)
            with nc.vector.Fori(0, NCH) as n:
                b = n // (NCH // BATCH)
                for j in range(HT):
                    dve.wait_ge(g_hi_ready, HT * n + j + 1)
                    nc.vector.tensor_tensor(g_lo[:, j % 4, :], g32[:, j % 2, :], raw(g_hi[:, j % 4, :]),
                                            ALU.subtract).then_inc(g_ready, 1)
                dve.wait_ge(x_loaded, 16 * (n + 1))
                for s in range(TT):
                    dve.wait_ge(acc_ready, TT * n + s + 1)
                    nc.vector.tensor_tensor(gated[:, 0, :], acc[s][:, :], K.gate[:, 1, bass.ds(b, 1), :],
                                            ALU.mult).then_inc(acc_free, 1)
                    dve.wait_ge(acc_free, TT * n + s + 1 + TT)
                    nc.vector.tensor_tensor(xs[:, s, :], gated[:, 0, :], xs[:, s, :], ALU.add).then_inc(out_ready, 1)
                    dve.wait_ge(out_ready, TT * n + s + 1)

        @block.tensor
        def _(pe):
            pe.sem_inc(used, 4)
            pe.wait_ge(bias_ready, 3)
            pe.wait_ge(w_split, 2 * NP)

            def multiply(n, j):
                if j == 0:
                    for s in range(TT):
                        pe.wait_ge(acc_free, TT * n + s + 1)
                        nc.tensor.matmul(acc[s][:, :], one_row[:, :], bias_hi[:, :], start=True, stop=False)
                        nc.tensor.matmul(acc[s][:, :], one_row[:, :], bias_lo[:, :], start=False, stop=False)
                pe.wait_ge(g_ready, HT * n + j + 1 + 2)
                for s in range(TT):
                    cols = slice(s * P, (s + 1) * P)
                    for k, (a, b) in enumerate(terms(g_hi[:, j % 4, cols], g_lo[:, j % 4, cols],
                                                     w2_hi[:, j // KT, j % KT, :], w2_lo[:, j // KT, j % KT, :])):
                        ins = nc.tensor.matmul(acc[s][:, :], a, b, start=False, stop=(j == HT - 1 and k == 2))
                    if j == HT - 1:
                        ins.then_inc(acc_ready, 1)
                if j < HT - 1:
                    ins.then_inc(used, 1)
                else:
                    pe.wait_ge(acc_ready, TT * (n + 1))
                    pe.sem_inc(used, 1)

            with nc.tensor.Fori(0, NCH) as n:
                pe.wait_ge(xm_loaded, 16 * (n + 1))
                for j in range(HT + LAG):
                    if j < HT:
                        pe.wait_ge(hid_free, HT * n + j + 1)
                        cols = slice((j % KT) * P, (j % KT + 1) * P)
                        for t in range(KT):
                            for k, (a, b) in enumerate(terms(w1_hi[:, j // KT, t, cols], w1_lo[:, j // KT, t, cols],
                                                             xm[:, 0, t, :], xm[:, 1, t, :])):
                                ins = nc.tensor.matmul(hid[j % 4][:, :], a, b, start=(t == 0 and k == 0),
                                                       stop=(t == KT - 1 and k == 2))
                        ins.then_inc(hid_ready, 1)
                    if j >= LAG:
                        multiply(n, j - LAG)


def build(nc, x, cond, wqkv, wproj, bproj, w1, b1, w2, b2, g1, be1, g2, be2, wada, bada, out, phases="abcd"):
    x = x.rearrange("b t d -> (b t) d")
    out = out.rearrange("b t d -> (b t) d")
    vecs = [(V_BADA, bada), (V_G1, g1), (V_BE1, be1), (V_G2, g2), (V_BE2, be2), (V_B1, b1)]
    with ExitStack() as ctx:
        K = Common(nc, ctx)
        phase_qkv(nc, K, x, cond, wada, bada, vecs, wqkv)
        if "b" in phases:
            phase_attention(nc, K)
        if "c" in phases:
            phase_project(nc, K, x, wada, wproj, bproj)
        if "d" in phases:
            phase_mlp(nc, K, w1, w2, b2, out)


_INS = ['x', 'cond_1024', 'L0_cond_Wqkv', 'L0_cond_Wproj', 'L0_cond_bproj', 'L0_cond_W1', 'L0_cond_b1',
        'L0_cond_W2', 'L0_cond_b2', 'L0_cond_g1', 'L0_cond_be1', 'L0_cond_g2', 'L0_cond_be2',
        'L0_cond_Wada', 'L0_cond_bada']
_OUTS = [((2, 2048, 512), 'float32')]


def kernel(**inputs):
    import numpy as _np
    import concourse.bacc as _bacc
    from concourse import mybir as _mybir
    from concourse.bass_utils import run_bass_kernel_spmd as _run

    nc = _bacc.Bacc("TRN2", target_bir_lowering=False, num_devices=1)
    arrays, args = {}, []
    for name in _INS:
        a = _np.ascontiguousarray(inputs[name])
        arrays[f"in_{name}_dram"] = a
        args.append(nc.dram_tensor(f"in_{name}_dram", a.shape, _mybir.dt.from_np(a.dtype), kind="ExternalInput").ap())
    for i, (shape, dtype) in enumerate(_OUTS):
        dt = _mybir.dt.from_np(_np.dtype(dtype))
        args.append(nc.dram_tensor(f"out_{i}_dram", shape, dt, kind="ExternalOutput").ap())
    build(nc, *args)
    r = _run(nc, [arrays], core_ids=[0])
    return r.results[0]["out_0_dram"]
```

```python
from contextlib import ExitStack

import concourse.bass as bass
from concourse import mybir

F32 = mybir.dt.float32
F32R = mybir.dt.float32r
BF16 = mybir.dt.bfloat16
ACT = mybir.ActivationFunctionType
ALU = mybir.AluOpType
AX = mybir.AxisListType

P = 128
BATCH, SEQ, D = 2, 2048, 512
HEADS, HD = 16, 32
HID = 4 * D
TOK = BATCH * SEQ
KT = D // P
HT = HID // P
CH = 512
NCH = TOK // CH
TT = CH // P
GH = P // HD
NG = BATCH * HEADS // GH
KEYT = SEQ // P
QC = SEQ // CH
SCALE = float(HD) ** -0.5
EPS = 1e-5
NEG = -1e30
LOWEST = -3e38

V_BADA, V_G1, V_BE1, V_G2, V_BE2, V_B1 = 0, 24, 28, 32, 36, 40
V_ROWS = 56
M_SHA, M_SCA, M_GTA, M_SHM, M_SCM, M_GTM = 0, 4, 8, 12, 16, 20


def raw(ap):
    return ap.bitcast(F32)


def terms(a_hi, a_lo, b_hi, b_lo):
    return ((a_hi, b_hi), (a_lo, b_hi), (a_hi, b_lo))


def await_count(eng, carrier, sem, value):
    eng.wait_ge(sem, value)
    eng.sem_inc(carrier, 1)


class Common:

    def __init__(self, nc, ctx):
        def sb(name, shape, dt=F32):
            return ctx.enter_context(nc.sbuf_tensor(name, shape, dt))

        def dram(name, shape):
            return nc.dram_tensor(name, shape, F32, kind="Internal").ap()

        self.ident = sb("ident", [P, P])
        self.ident_bf = sb("ident_bf", [P, P], BF16)
        self.mask_qk = sb("mask_qk", [P, P], BF16)
        self.mask_kq = sb("mask_kq", [P, P], BF16)
        self.ones = sb("ones", [P, P])
        self.vcol = sb("vcol", [P, V_ROWS])
        self.cond_t = sb("cond_t", [P, KT, BATCH])
        self.mod = sb("mod", [P, BATCH, 24])
        self.aff1 = sb("aff1", [P, BATCH, 2, KT])
        self.aff2 = sb("aff2", [P, BATCH, 2, KT])
        self.gate = sb("gate", [P, 2, BATCH, D])
        self.qk = dram("qk_scratch", (2, 2, D, TOK))
        self.v = dram("v_scratch", (TOK, D))
        self.m = dram("m_scratch", (QC, 2, GH * CH))
        self.o = dram("o_scratch", (NG, P, SEQ))
        self.x2 = dram("x2_scratch", (TOK, D))
        self.xm2 = dram("xm2_scratch", (2, D, TOK))


def wave(eng, body, pairs, last_differs=True):
    with eng.Fori(0, pairs - 1) as i:
        for u in range(2):
            body(2 * i + u, u, True)
    for u in range(2):
        body(2 * (pairs - 1) + u, u, u == 0)


def newton_rstd(nc, dve, link, ve, sd, r, t):
    link(nc.vector.reciprocal(r, sd))
    link(nc.vector.tensor_tensor(t, r, r, ALU.mult))
    link(nc.vector.tensor_tensor(t, t, ve, ALU.mult))
    link(nc.vector.tensor_scalar(t, t, -0.5, 1.5, ALU.mult, ALU.add))
    link(nc.vector.tensor_tensor(r, r, t, ALU.mult))


def phase_qkv(nc, K, x, cond, wada, bada, vecs, wqkv):
    with ExitStack() as ctx:
        def sb(name, shape, dt=F32):
            return ctx.enter_context(nc.sbuf_tensor(name, shape, dt))

        def pb(name, shape):
            return ctx.enter_context(nc.psum_tensor(name, shape, F32))

        def sem(name):
            return ctx.enter_context(nc.semaphore(name))

        AHEAD = 5
        NT = 3 * D // P
        w_raw = sb("w_raw", [P, KT, 3 * D])
        w_hi = sb("w_hi", [P, KT, 3 * D], F32R)
        w_lo = sb("w_lo", [P, KT, 3 * D], F32R)
        ada = sb("ada", [P, KT, 2 * D])
        vrow = sb("vrow", [V_ROWS, P])
        cnd = sb("cnd", [BATCH, 3, D])
        xs = sb("xs", [P, 2, TT, D])
        xn = sb("xn", [P, TT, D])
        y32 = sb("y32", [P, 2, CH])
        xm_hi = sb("xm_hi", [P, 2, KT, CH], F32R)
        xm_lo = sb("xm_lo", [P, 2, KT, CH], F32R)
        st_hi = sb("st_hi", [P, 2, KT, CH], F32R)
        st_lo = sb("st_lo", [P, 2, KT, CH], F32R)
        st_v = sb("st_v", [P, TT, D])
        bst = sb("bst", [P, TT, 6])
        mv = sb("mv", [P, TT, 2])
        ve = sb("ve", [P, TT])
        sd = sb("sd", [P, TT])
        rstd = sb("rstd", [P, TT])
        tmp = sb("tmp", [P, TT])
        one_sc = sb("one_sc", [P, BATCH, KT])
        tp = [pb(f"tp{i}", [P, CH]) for i in range(2)]
        acc = [pb(f"acc{i}", [P, CH]) for i in range(4)]
        misc = pb("misc", [P, CH])

        c_ready = sem("a_constants_ready")
        v_loaded = sem("a_vectors_loaded")
        ada_loaded = sem("a_ada_loaded")
        w_loaded = sem("a_w_loaded")
        w_hi_ready = sem("a_w_hi_ready")
        w_split = sem("a_w_split")
        silu_e = sem("a_silu_exp_ready")
        silu_r = sem("a_silu_ready")
        small_pe = sem("a_small_pe")
        small_dve = sem("a_small_dve")
        x_loaded = [sem(f"a_x_loaded{u}") for u in range(2)]
        x_free = sem("a_x_free")
        var_ready = sem("a_var_ready")
        sd_ready = sem("a_sd_ready")
        xn_ready = sem("a_xn_ready")
        tp_ready = sem("a_tp_ready")
        tp_free = sem("a_tp_free")
        xm_ready = sem("a_xm_ready")
        acc_ready = sem("a_acc_ready")
        acc_free = sem("a_acc_free")
        hi_ready = sem("a_hi_ready")
        v_ready = sem("a_v_ready")
        qk_stored = [sem(f"a_{n}_stored") for n in "qk"]
        v_stored = sem("a_v_stored")
        chain = sem("a_dve_chain")
        held = sem("a_wait_carrier")
        block = ctx.enter_context(nc.Block())

        @block.sync
        def _(sp):
            sp.dma_start(cnd[:, 0, :], cond).then_inc(v_loaded, 16)
            for at, v in vecs:
                n = v.shape[0] // P
                sp.dma_start(vrow[at:at + n, :], v.rearrange("(t p) -> t p", p=P)).then_inc(v_loaded, 16)
            sp.dma_start(ada[:, :, :], wada[:, 0:2 * D].rearrange("(t p) n -> p t n", p=P)).then_inc(ada_loaded, 16)
            for t in range(KT):
                sp.dma_start(w_raw[:, t, :], wqkv[t * P:(t + 1) * P, :]).then_inc(w_loaded, 16)
            with nc.sync.Fori(0, NCH // 2) as i:
                for u in range(2):
                    n = 2 * i + u
                    await_count(sp, held, x_free, n + 1)
                    sp.dma_start(xs[:, u, :, :],
                                 x[bass.ds(n * CH, CH), :].rearrange("(t p) d -> p t d", p=P)).then_inc(x_loaded[u], 16)

        @block.gpsimd
        def _(pool):
            nc.gpsimd.memset(K.ident[:, :], 0.0).then_inc(c_ready, 1)
            nc.gpsimd.memset(K.ident_bf[:, :], 0.0).then_inc(c_ready, 1)
            nc.gpsimd.memset(K.mask_qk[:, :], 0.0).then_inc(c_ready, 1)
            nc.gpsimd.memset(K.mask_kq[:, :], 0.0).then_inc(c_ready, 1)
            nc.gpsimd.memset(K.ones[:, :], 1.0).then_inc(c_ready, 1)
            pool.wait_ge(c_ready, 5)
            for m in (K.ident, K.ident_bf):
                nc.gpsimd.affine_select(out=m[:, :], in_=m[:, :], compare_op=ALU.not_equal, fill=1.0, base=0,
                                        pattern=[[-1, P]], channel_multiplier=1).then_inc(c_ready, 1)
            for m, step in ((K.mask_qk, 1), (K.mask_kq, -1)):
                nc.gpsimd.affine_select(out=m[:, :], in_=m[:, :], compare_op=ALU.is_ge, fill=NEG, base=0,
                                        pattern=[[-step, P]], channel_multiplier=step).then_inc(c_ready, 1)

        @block.scalar
        def _(act):
            act.wait_ge(v_loaded, 16 * (1 + len(vecs)))
            nc.scalar.activation(cnd[:, 1, :], cnd[:, 0, :], ACT.Exp, scale=-1.0).then_inc(silu_e, 1)
            act.wait_ge(w_loaded, 16 * KT)
            for t in range(KT):
                nc.scalar.activation(w_hi[:, t, :], w_raw[:, t, :], ACT.Copy).then_inc(w_hi_ready, 1)

            def std(n):
                act.wait_ge(var_ready, n + 1)
                nc.scalar.activation(sd[:, :], ve[:, :], ACT.Sqrt).then_inc(sd_ready, 1)

            def body(n, u, more):
                if more:
                    std(n + 1)
                for j in range(2 * KT):
                    act.wait_ge(acc_ready, NT * n + j + 1 + 1)
                    nc.scalar.activation(st_hi[:, j // KT, j % KT, :], acc[j % 4][:, :], ACT.Copy).then_inc(hi_ready, 1)
                    if j == KT:
                        store_qk(n, 0)
                store_qk(n, 1)
                act.wait_ge(v_ready, n + 1)
                act.dma_start(K.v[bass.ds(n * CH, CH), :].rearrange("(t p) d -> p t d", p=P),
                              st_v[:, :, :]).then_inc(v_stored, 16)
                for half in range(2):
                    act.wait_ge(qk_stored[half], 32 * (n + 1))
                act.wait_ge(v_stored, 16 * (n + 1))

            def store_qk(n, half):
                act.wait_ge(acc_free, NT * n + KT * (half + 1) + 4)
                for part, st in enumerate((st_hi, st_lo)):
                    act.dma_start(K.qk[half, part, :, bass.ds(n * CH, CH)].rearrange("(t p) n -> p t n", p=P),
                                  raw(st[:, half, :, :])).then_inc(qk_stored[half], 16)

            std(0)
            wave(nc.scalar, body, NCH // 2)

        @block.vector
        def _(dve):
            links = [0]

            def link(ins):
                links[0] += 1
                ins.then_inc(chain, 1)
                dve.wait_ge(chain, links[0])

            dve.wait_ge(silu_e, 1)
            link(nc.vector.tensor_scalar(cnd[:, 2, :], cnd[:, 1, :], 1.0, None, ALU.add))
            link(nc.vector.reciprocal(cnd[:, 1, :], cnd[:, 2, :]))
            nc.vector.tensor_tensor(cnd[:, 2, :], cnd[:, 1, :], cnd[:, 0, :], ALU.mult).then_inc(silu_r, 1)
            dve.wait_ge(small_pe, 1)
            nc.vector.tensor_copy(K.vcol[:, :], misc[:, 0:V_ROWS]).then_inc(small_dve, 1)
            dve.wait_ge(small_pe, 2)
            nc.vector.tensor_copy(K.cond_t[:, :, :], misc[:, 64:64 + KT * BATCH].rearrange("p (t b) -> p t b", b=BATCH)).then_inc(small_dve, 1)
            dve.wait_ge(small_dve, 1)
            dve.wait_ge(small_pe, 3)
            mod_ps = misc[:, 128:128 + 8 * BATCH].rearrange("p (m b) -> p b m", b=BATCH)
            for b in range(BATCH):
                link(nc.vector.tensor_tensor(K.mod[:, b, 0:8], mod_ps[:, b, :], K.vcol[:, V_BADA:V_BADA + 8], ALU.add))
                link(nc.vector.tensor_scalar(one_sc[:, b, :], K.mod[:, b, M_SCA:M_SCA + KT], 1.0, None, ALU.add))
                link(nc.vector.tensor_tensor(K.aff1[:, b, 0, :], one_sc[:, b, :], K.vcol[:, V_G1:V_G1 + KT], ALU.mult))
                link(nc.vector.tensor_tensor(K.aff1[:, b, 1, :], one_sc[:, b, :], K.vcol[:, V_BE1:V_BE1 + KT], ALU.mult))
                link(nc.vector.tensor_tensor(K.aff1[:, b, 1, :], K.aff1[:, b, 1, :], K.mod[:, b, M_SHA:M_SHA + KT], ALU.add))
            for t in range(KT):
                dve.wait_ge(w_hi_ready, t + 1)
                nc.vector.tensor_tensor(w_lo[:, t, :], w_raw[:, t, :], raw(w_hi[:, t, :]), ALU.subtract).then_inc(w_split, 1)
            dve.sem_inc(x_free, 2)
            dve.sem_inc(tp_free, 2)
            dve.sem_inc(acc_free, 4)
            base = links[0]
            CHAINS = 7

            def norm(n, u):
                at = [0]

                def lk(ins):
                    at[0] += 1
                    ins.then_inc(chain, 1)
                    dve.wait_ge(chain, n * CHAINS + base + at[0])

                dve.wait_ge(x_loaded[u], (n // 2) * 16 + 16)
                for t in range(TT - 1):
                    nc.vector.bn_stats(bst[:, t, :], xs[:, u, t, :])
                lk(nc.vector.bn_stats(bst[:, TT - 1, :], xs[:, u, TT - 1, :]))
                dve.sem_inc(held, 1)
                for t in range(TT - 1):
                    nc.vector.bn_aggr(mv[:, t, :], bst[:, t, :])
                lk(nc.vector.bn_aggr(mv[:, TT - 1, :], bst[:, TT - 1, :]))
                nc.vector.tensor_scalar(ve[:, :], mv[:, :, 1], EPS, None, ALU.add).then_inc(var_ready, 1)
                dve.wait_ge(sd_ready, n + 1)
                newton_rstd(nc, dve, lk, ve[:, :], sd[:, :], rstd[:, :], tmp[:, :])
                dve.wait_ge(tp_ready, n * KT + 1)
                for t in range(TT):
                    nc.vector.tensor_scalar(xn[:, t, :], xs[:, u, t, :], mv[:, t, 0:1], rstd[:, t:t + 1],
                                            ALU.subtract, ALU.mult).then_inc(xn_ready, 1)
                dve.wait_ge(xn_ready, TT * (n + 1))
                dve.sem_inc(x_free, 1)

            def modulate(n, u, t):
                b = n // (NCH // BATCH)
                dve.wait_ge(tp_ready, n * KT + t + 1 + 1)
                nc.vector.tensor_scalar(y32[:, t % 2, :], tp[t % 2][:, :], aff(b, 0, t), aff(b, 1, t),
                                        ALU.mult, ALU.add).then_inc(tp_free, 1)
                dve.wait_ge(tp_free, n * KT + t + 1 + 2)
                nc.vector.tensor_copy(xm_hi[:, u, t, :], y32[:, t % 2, :]).then_inc(xm_ready, 1)
                dve.wait_ge(xm_ready, 2 * (n * KT + t) + 1)
                nc.vector.tensor_tensor(xm_lo[:, u, t, :], y32[:, t % 2, :], raw(xm_hi[:, u, t, :]),
                                        ALU.subtract).then_inc(xm_ready, 1)

            def aff(b, which, t):
                if isinstance(b, int):
                    return K.aff1[:, b, which, t:t + 1]
                return K.aff1[:, bass.ds(b, 1), which, t:t + 1]

            def body(n, u, more):
                if more:
                    norm(n + 1, 1 - u)
                    dve.wait_ge(acc_ready, NT * n + 1)
                for j in range(NT):
                    if more and 0 <= j - AHEAD < KT:
                        modulate(n + 1, 1 - u, j - AHEAD)
                    if j < 2 * KT:
                        dve.wait_ge(hi_ready, 2 * KT * n + j + 1)
                        nc.vector.tensor_tensor(st_lo[:, j // KT, j % KT, :], acc[j % 4][:, :],
                                                raw(st_hi[:, j // KT, j % KT, :]), ALU.subtract).then_inc(acc_free, 1)
                    else:
                        dve.wait_ge(acc_ready, NT * n + j + 1 + 1)
                        ins = nc.vector.tensor_copy(st_v[:, j - 2 * KT, :], acc[j % 4][:, :])
                        ins.then_inc(acc_free, 1)
                dve.wait_ge(acc_free, NT * (n + 1) + 4)
                dve.sem_inc(v_ready, 1)

            norm(0, 0)
            for t in range(KT):
                modulate(0, 0, t)
            wave(nc.vector, body, NCH // 2)

        @block.tensor
        def _(pe):
            pe.wait_ge(c_ready, 9)
            pe.wait_ge(v_loaded, 16 * (1 + len(vecs)))
            nc.tensor.transpose(misc[:, 0:V_ROWS], vrow[:, :], K.ident[0:V_ROWS, 0:V_ROWS]).then_inc(small_pe, 1)
            pe.wait_ge(silu_r, 1)
            pe.wait_ge(small_dve, 1)
            for t in range(KT):
                ins = nc.tensor.transpose(misc[:, 64 + t * BATCH:64 + (t + 1) * BATCH], cnd[:, 2, t * P:(t + 1) * P],
                                          K.ident[0:BATCH, 0:BATCH])
            ins.then_inc(small_pe, 1)
            pe.wait_ge(small_dve, 2)
            pe.wait_ge(ada_loaded, 16)
            for m in range(8):
                for t in range(KT):
                    ins = nc.tensor.matmul(misc[:, 128 + m * BATCH:128 + (m + 1) * BATCH], ada[:, t, m * P:(m + 1) * P],
                                           K.cond_t[:, t, :], start=(t == 0), stop=(t == KT - 1))
            ins.then_inc(small_pe, 1)
            pe.sem_inc(tp_ready, 1)
            pe.sem_inc(acc_ready, 1)

            def turn(n, t):
                pe.wait_ge(tp_free, n * KT + t + 1)
                if t == 0:
                    pe.wait_ge(xn_ready, TT * (n + 1))
                for s in range(TT):
                    ins = nc.tensor.transpose(tp[t % 2][:, s * P:(s + 1) * P], xn[:, s, t * P:(t + 1) * P], K.ident[:, :])
                ins.then_inc(tp_ready, 1)

            def body(n, u, more):
                pe.wait_ge(xm_ready, 2 * KT * (n + 1))
                for j in range(NT):
                    if more and 0 <= j - AHEAD < KT:
                        turn(n + 1, j - AHEAD)
                    pe.wait_ge(acc_free, NT * n + j + 1)
                    for t in range(KT):
                        if j < 2 * KT:
                            cols = slice(j * P, (j + 1) * P)
                            ops = terms(w_hi[:, t, cols], w_lo[:, t, cols], xm_hi[:, u, t, :], xm_lo[:, u, t, :])
                        else:
                            cols = slice((j - 2 * KT) * P, (j - 2 * KT + 1) * P)
                            ops = terms(xm_hi[:, u, t, cols], xm_lo[:, u, t, cols], w_hi[:, t, 2 * D:], w_lo[:, t, 2 * D:])
                        for k, (a, b) in enumerate(ops):
                            ins = nc.tensor.matmul(acc[j % 4][:, :], a, b, start=(t == 0 and k == 0),
                                                   stop=(t == KT - 1 and k == 2))
                    ins.then_inc(acc_ready, 1)

            for t in range(KT):
                turn(0, t)
            pe.wait_ge(w_split, KT)
            wave(nc.tensor, body, NCH // 2)


class Plan:

    DIRECT = 3

    def __init__(self):
        self.order = list(range(QC))[::-1]
        self.steps = [(pos, kt) for pos, c in enumerate(self.order) for kt in range((c + 1) * TT)]
        self.NS = len(self.steps)
        self.last = [self.steps.index((pos, (c + 1) * TT - 1)) for pos, c in enumerate(self.order)]
        LATER = 3
        self.batch = [[(pos, h, t, kc, min(CH, (c * TT + t + 1) * P - kc * CH))
                       for kc in range(c + 1)[::-1] for h in range(GH) for t in range(TT)]
                      for pos, c in enumerate(self.order)]
        self.opening = self.batch[0] + [0]
        self.items = []
        for pos in (*range(1, QC), 0):
            start = len(self.items)
            self.items += self.batch[pos]
            if pos != 1:
                self.items.insert(start + (LATER if pos else 0), (pos or QC) - 1)
        self.items.append(0)
        self.NI = len(self.items)
        self.adds, self.opens, done, held = [], set(), 0, None
        self.released = []
        for s, (pos, kt) in enumerate(self.steps):
            if self.direct(s):
                self.released.append(done)
                continue
            if kt == 1:
                self.released.append(done + 1)
            else:
                done += 1
                self.adds.append(s)
                self.released.append(done)
        self.NA = done
        weight = [self.width(s) for s in range(self.NS)]
        FROM, TO = 1, self.NS - 4
        span = sum(weight[FROM:TO])
        price = [P if isinstance(it, int) else it[4] + 64 for it in self.items]
        total, spent, at, passed = sum(price), 0, 0, 0
        self.items_at = [[] for _ in self.steps]
        for s in range(FROM, TO):
            passed += weight[s]
            while at < self.NI - 1 and (spent + price[at] / 2) * span <= passed * total:
                self.items_at[s].append(at)
                spent += price[at]
                at += 1
        self.items_at[TO - 1] += range(at, self.NI - 1)
        self.items_at[TO + 1].append(self.NI - 1)

    def direct(self, s):
        pos, kt = self.steps[s]
        return pos == QC - 1 or kt % self.DIRECT == 0

    def mid(self, s):
        pos, kt = self.steps[s]
        return max(0, kt - self.order[pos] * TT) * P

    def width(self, s):
        return CH - self.mid(s)

    def places(self, n, k):
        return [(i * k + k - 1) // n if n > k else i for i in range(n)]

    def stream(self, s, more):
        if s >= self.NS:
            return []
        return [i for i in self.items_at[s] if more or self.group(0, i) == 0]

    def group(self, g, i):
        it = self.items[i]
        return g + (1 if (it if isinstance(it, int) else it[0]) == 0 else 0)

    def through(self, pos):
        return self.items.index(self.batch[pos][-1]) + 1


def phase_attention(nc, K):
    L = Plan()
    ROWS, MROWS = 3 * HD, 3 * HD + 2
    BUF = 5
    INV = 4
    MROW = GH * TT
    with ExitStack() as ctx:
        def sb(name, shape, dt=F32):
            return ctx.enter_context(nc.sbuf_tensor(name, shape, dt))

        def pb(name, shape):
            return ctx.enter_context(nc.psum_tensor(name, shape, F32))

        def sem(name):
            return ctx.enter_context(nc.semaphore(name))

        k_st = sb("k_st", [P, 2, GH, SEQ], F32R)
        q_st = sb("q_st", [P, 2, GH, CH], F32R)
        qx_st = sb("qx_st", [P, 2, GH, CH], F32R)
        v_sb = sb("v_sb", [P, 2, KEYT, P])
        prob = sb("prob", [P, BUF, GH, CH])
        psum_k = sb("psum_k", [P, 2, GH, CH])
        o_raw = sb("o_raw", [P, 2, 2, CH])
        o_sb = sb("o_sb", [P, 2, CH])
        part = sb("part", [P, 2, MROW, QC])
        mcol = sb("mcol", [P, 2, MROW])
        m_hi = sb("m_hi", [MROW, 2, P], F32R)
        m_lo = sb("m_lo", [MROW, 2, P], F32R)
        st = [pb(f"st{i}", [P, 2, CH]) for i in range(2)]
        mx = [pb(f"mx{i}", [P, CH]) for i in range(2)]
        o_ps = pb("o_ps", [P, CH])
        r_ps = pb("r_ps", [P, CH])

        ones_ready = sem("b_ones_ready")
        k_loaded = [[sem(f"b_k_loaded{u}{kc}") for kc in range(QC)] for u in range(2)]
        v_loaded = [sem(f"b_v_loaded{u}") for u in range(2)]
        q_loaded = [sem(f"b_q_loaded{u}") for u in range(2)]
        qx_loaded = [sem(f"b_qx_loaded{u}") for u in range(2)]
        m_ready = sem("b_m_ready")
        m_stored = sem("b_m_stored")
        mx_ready = sem("b_mx_ready")
        mx_free = sem("b_mx_free")
        mcol_ready = sem("b_mcol_ready")
        st_ready = sem("b_st_ready")
        exp_done = sem("b_exp_done")
        pv_done = sem("b_pv_done")
        pool_added = sem("b_pool_added")
        o_ready = sem("b_o_ready")
        o_copied = sem("b_o_copied")
        inverted = sem("b_inverted")
        o_done = sem("b_o_done")
        o_stored = [sem(f"b_o_stored{u}") for u in range(2)]
        o_sb_free = sem("b_o_sb_free")
        held = sem("b_wait_carrier")
        block = ctx.enter_context(nc.Block())

        def st_count(g, pairs):
            return 2 * L.NS * g + pairs + 1

        def exp_count(g, pairs):
            return 2 * L.NS * g + pairs + 2

        def pv_count(g, steps):
            return L.NS * g + steps + BUF

        def add_count(g, n):
            return L.NA * g + n + L.NA

        def item_count(g, n):
            return len(L.opening) + L.NI * g + n

        def slot(i):
            return (len(L.opening) + i) % 2

        def o_reuse(g, pos):
            return QC * g + 1 + (1 if pos == 2 else 0)

        def per_group(eng, body):
            with eng.Fori(0, NG // 2 - 1) as i:
                for u in range(2):
                    body(2 * i + u, u, True)
            body(NG - 2, 0, True)
            body(NG - 1, 1, False)

        @block.sync
        def _(sp):
            def place(g):
                return g // (HEADS // GH), g % (HEADS // GH)

            def load_k(g, u, kc):
                b, gg = place(g)
                cols = slice(kc * CH, (kc + 1) * CH)
                for row, hl in enumerate((0, 1, 0)):
                    sp.dma_start(raw(k_st[row * HD:(row + 1) * HD, u, :, cols]),
                                 K.qk[1, hl, bass.ds(gg * P, P), bass.ds(b * SEQ + kc * CH, CH)]
                                 .rearrange("(h r) n -> r h n", r=HD)).then_inc(k_loaded[u][kc], 16)

            def load_queries(g, pos, dst, loaded):
                b, gg = place(g)
                for row, hl in enumerate((0, 0, 1)):
                    sp.dma_start(raw(dst[row * HD:(row + 1) * HD, pos % 2, :, :]),
                                 K.qk[0, hl, bass.ds(gg * P, P), bass.ds(b * SEQ + L.order[pos] * CH, CH)]
                                 .rearrange("(h r) n -> r h n", r=HD)).then_inc(loaded[pos % 2], 16)

            def load_qx(g, pos):
                load_queries(g, pos, qx_st, qx_loaded)

            def load_v(g, u):
                b, gg = place(g)
                sp.dma_start(v_sb[:, u, :, :],
                             K.v[bass.ds(b * SEQ, SEQ), bass.ds(gg * P, P)].rearrange("(t p) d -> p t d", p=P)).then_inc(v_loaded[u], 16)

            def store_m_load_q(g, pos):
                load_queries(g, pos, q_st, q_loaded)
                await_count(sp, held, m_ready, 2 * (QC * g + pos + 1))
                for hl, t in enumerate((m_hi, m_lo)):
                    sp.dma_start(K.m[pos, hl, :].rearrange("(r n) -> r n", n=P), raw(t[:, pos % 2, :])).then_inc(m_stored, 16)
                await_count(sp, held, m_stored, 32 * (QC * g + pos + 1) + 64)
                sp.dma_start(raw(q_st[ROWS:MROWS, pos % 2, :, :]),
                             K.m[pos, :, :].rearrange("a (h n) -> a h n", h=GH)).then_inc(q_loaded[pos % 2], 16)

            def jobs_done(g, pos):
                await_count(sp, held, mx_ready, item_count(g, L.through(pos)))

            def steps_done(g, pos):
                await_count(sp, held, st_ready, st_count(g, 2 * (L.last[pos] + 1)))

            def store_o(g, pos):
                await_count(sp, held, o_done, QC * g + pos + 1 + 2)
                c = L.order[pos]
                sp.dma_start(K.o[bass.ds(g, 1), :, c * CH:(c + 1) * CH].rearrange("g r n -> (g r) n"),
                             o_sb[:, pos % 2, :]).then_inc(o_stored[pos % 2], 16)

            def stored_o(g, pos):
                await_count(sp, held, o_stored[pos % 2], 16 * (2 * g + pos // 2 + 1))
                sp.sem_inc(o_sb_free, 1)

            sp.sem_inc(m_stored, 64)
            load_qx(0, 0)
            for kc in range(QC)[::-1]:
                load_k(0, 0, kc)
            load_qx(0, 1)
            load_v(0, 0)
            await_count(sp, held, mx_ready, len(L.batch[0]))
            load_qx(0, 2)
            store_m_load_q(0, 0)

            def body(g, u, more):
                if more:
                    await_count(sp, held, st_ready, st_count(g, 0))
                    for kc in range(QC)[::-1]:
                        load_k(g + 1, 1 - u, kc)
                    await_count(sp, held, pv_done, pv_count(g, 0))
                    load_v(g + 1, 1 - u)
                jobs_done(g, 1)
                load_qx(g, 3)
                store_m_load_q(g, 1)
                jobs_done(g, 2)
                if more:
                    load_qx(g + 1, 0)
                steps_done(g, 0)
                store_m_load_q(g, 2)
                store_o(g, 0)
                jobs_done(g, 3)
                if more:
                    load_qx(g + 1, 1)
                stored_o(g, 0)
                steps_done(g, 1)
                store_m_load_q(g, 3)
                store_o(g, 1)
                if more:
                    jobs_done(g, 0)
                    load_qx(g + 1, 2)
                    steps_done(g, 2)
                    store_m_load_q(g + 1, 0)
                stored_o(g, 1)
                store_o(g, 2)
                stored_o(g, 2)
                store_o(g, 3)
                stored_o(g, 3)

            per_group(nc.sync, body)

        @block.gpsimd
        def _(pool):
            nc.gpsimd.memset(raw(k_st[ROWS:MROWS, :, :, :]), 1.0).then_inc(ones_ready, 1)
            pool.sem_inc(pool_added, L.NA)

            def body(g, u, more):
                for n, s in enumerate(L.adds):
                    pos, kt = L.steps[s]
                    m = L.mid(s)
                    dst = psum_k[:, pos % 2, :, m:]
                    pool.wait_ge(exp_done, exp_count(g, 2 * s + 2))
                    if kt == 2:
                        pool.wait_ge(o_ready, o_reuse(g, pos))
                        src = prob[:, (s - 1) % BUF, :, m:]
                    else:
                        pool.wait_ge(pool_added, add_count(g, n))
                        src = dst
                    nc.gpsimd.tensor_tensor(dst, src, prob[:, s % BUF, :, m:], ALU.add).then_inc(pool_added, 1)

            per_group(nc.gpsimd, body)

        @block.scalar
        def _(act):
            act.sem_inc(exp_done, 2)
            act.sem_inc(o_done, 2)
            act.sem_inc(o_copied, 1)

            def exps(g, s):
                m = L.mid(s)
                act.wait_ge(pv_done, pv_count(g, s + 1 - BUF))
                n = L.released[s - BUF] if s >= BUF else L.released[s - BUF] - L.NA
                act.wait_ge(pool_added, add_count(g, n))
                for p in range(2):
                    act.wait_ge(st_ready, st_count(g, 2 * s + p + 1))
                    nc.scalar.activation(prob[:, s % BUF, 2 * p:2 * p + 2, m:], st[p][:, :, m:], ACT.Exp,
                                         scale=SCALE).then_inc(exp_done, 1)

            def copy(g, pos):
                act.wait_ge(pv_done, pv_count(g, L.last[pos] + 1))
                act.wait_ge(o_done, QC * g + pos + 1)
                nc.scalar.activation(o_raw[:, pos % 2, 0, :], o_ps[:, :], ACT.Copy).then_inc(o_copied, 1)
                act.wait_ge(o_ready, QC * g + pos + 1 + 1)
                nc.scalar.activation(o_raw[:, pos % 2, 1, :], r_ps[:, :], ACT.Copy).then_inc(o_copied, 1)

            def body(g, u, more):
                for s in range(1, L.NS + 1):
                    if s < L.NS:
                        exps(g, s)
                    elif more:
                        exps(g + 1, 0)
                    if s - 1 in L.last:
                        copy(g, L.last.index(s - 1))

            exps(0, 0)
            per_group(nc.scalar, body)

        @block.vector
        def _(dve):
            dve.sem_inc(mx_free, 2)

            def item(g, pre, it, bank):
                if isinstance(it, int):
                    return turn(g, pre, it, bank)
                pos, h, t, kc, w = it
                dve.wait_ge(mx_ready, pre + 1)
                nc.vector.tensor_reduce(part[:, pos % 2, h * TT + t, kc:kc + 1], mx[bank][:, 0:w], AX.X, ALU.max).then_inc(mx_free, 1)
                if it is L.batch[pos][-1]:
                    dve.wait_ge(mx_free, pre + 1 + 2)
                    nc.vector.tensor_reduce(mcol[:, pos % 2, :], part[:, pos % 2, :, 0:L.order[pos] + 1],
                                            AX.X, ALU.max).then_inc(mcol_ready, 1)

            def turn(g, pre, pos, bank):
                n = QC * g + pos
                dve.wait_ge(mx_ready, pre + 1)
                dve.wait_ge(m_stored, 32 * n + 32)
                m = mx[bank][0:MROW, 0:P]
                nc.vector.tensor_scalar(m_hi[:, pos % 2, :], m, -1.0, None, ALU.mult).then_inc(m_ready, 1)
                dve.wait_ge(m_ready, 2 * n + 1)
                nc.vector.scalar_tensor_tensor(out=m_lo[:, pos % 2, :], in0=m, scalar=-1.0, in1=raw(m_hi[:, pos % 2, :]),
                                               op0=ALU.mult, op1=ALU.subtract).then_inc(m_ready, 1)
                dve.wait_ge(m_ready, 2 * n + 2)
                dve.sem_inc(mx_free, 1)

            def invert(g, pos, j):
                r = o_raw[:, pos % 2, 1, j * CH // INV:(j + 1) * CH // INV]
                dve.wait_ge(o_copied, 2 * (QC * g + pos) + 2 + 1)
                nc.vector.reciprocal(r, r).then_inc(inverted, 1)

            def finish(g, pos):
                dve.wait_ge(inverted, INV * (QC * g + pos + 1))
                dve.wait_ge(o_sb_free, QC * g + pos + 1)
                nc.vector.tensor_tensor(o_sb[:, pos % 2, :], o_raw[:, pos % 2, 0, :], o_raw[:, pos % 2, 1, :],
                                        ALU.mult).then_inc(o_done, 1)

            def body(g, u, more):
                for s in range(1, L.NS + 2):
                    for pos in range(QC - 1):
                        j = s - 2 - L.last[pos]
                        if 0 <= j < INV:
                            invert(g, pos, j)
                        if j == INV:
                            finish(g, pos)
                    items = L.stream(s, more)
                    for i in items:
                        item(L.group(g, i), item_count(g, i), L.items[i], slot(i))
                for j in range(INV):
                    invert(g, QC - 1, j)
                finish(g, QC - 1)

            dve.sem_inc(o_sb_free, 2)
            for j, it in enumerate(L.opening):
                item(0, j, it, j % 2)
            per_group(nc.vector, body)

        @block.tensor
        def _(pe):
            pe.sem_inc(st_ready, 1)
            pe.sem_inc(pv_done, BUF)
            pe.sem_inc(o_ready, 1)
            pe.wait_ge(ones_ready, 1)

            def item(g, u, pre, it, bank):
                pe.wait_ge(mx_free, pre + 1)
                out = mx[bank]
                if isinstance(it, int):
                    pe.wait_ge(mcol_ready, QC * g + it + 1)
                    nc.tensor.transpose(out[0:MROW, 0:P], mcol[:, it % 2, :], K.ident[:, :]).then_inc(mx_ready, 1)
                    return
                pos, h, t, kc, w = it
                if it is L.batch[pos][0]:
                    pe.wait_ge(qx_loaded[pos % 2], 48 * (2 * g + pos // 2 + 1))
                if pos == 0 and h == t == 0:
                    pe.wait_ge(k_loaded[u][kc], 48 * (g // 2 + 1))
                diagonal = kc == L.order[pos]
                ins = nc.tensor.matmul(out[:, 0:w], qx_st[0:ROWS, pos % 2, h, t * P:(t + 1) * P],
                                       k_st[0:ROWS, u, h, kc * CH:kc * CH + w], start=True, stop=not diagonal)
                if diagonal:
                    ins = nc.tensor.matmul(out[:, w - P:w], K.ident_bf[:, :], K.mask_qk[:, :], start=False, stop=True)
                ins.then_inc(mx_ready, 1)

            def stream_item(g, u, i):
                mine = L.group(0, i) == 0
                item(L.group(g, i), u if mine else 1 - u, item_count(g, i), L.items[i], slot(i))

            def scores(g, u, s, between=lambda p: None):
                pos, kt = L.steps[s]
                m = L.mid(s)
                masked = kt >= L.order[pos] * TT
                if kt == 0:
                    pe.wait_ge(q_loaded[pos % 2], 64 * (2 * g + pos // 2 + 1))
                for p in range(2):
                    pe.wait_ge(exp_done, exp_count(g, 2 * s + p - 1))
                    for h in (2 * p, 2 * p + 1):
                        out = st[p][:, h % 2, :]
                        ins = nc.tensor.matmul(out[:, m:], k_st[0:MROWS, u, h, kt * P:(kt + 1) * P],
                                               q_st[0:MROWS, pos % 2, h, m:], start=True, stop=not masked)
                        if masked:
                            ins = nc.tensor.matmul(out[:, m:m + P], K.ident_bf[:, :], K.mask_kq[:, :], start=False, stop=True)
                    ins.then_inc(st_ready, 1)
                    between(p)

            def product(g, u, s, between):
                pos, kt = L.steps[s]
                m = L.mid(s)
                end = s == L.last[pos]
                if s == 0:
                    pe.wait_ge(v_loaded[u], 16 * (g // 2 + 1))
                if kt == 0:
                    pe.wait_ge(o_copied, 2 * (QC * g + pos) + 1)
                pe.wait_ge(exp_done, exp_count(g, 2 * s + 2))
                for h in range(GH):
                    rows = slice(h * HD, (h + 1) * HD)
                    ins = nc.tensor.matmul(o_ps[rows, m:], v_sb[:, u, kt, rows], prob[:, s % BUF, h, m:],
                                           start=(kt == 0), stop=end)
                if L.direct(s):
                    between(2)
                    for h in range(GH):
                        ins = nc.tensor.matmul(r_ps[h * HD:(h + 1) * HD, m:], K.ones[:, 0:HD], prob[:, s % BUF, h, m:],
                                               start=(kt == 0), stop=end and pos == QC - 1)
                ins.then_inc(pv_done, 1)
                between(3 if L.direct(s) else 2)
                if end and pos == QC - 1:
                    pe.wait_ge(pv_done, pv_count(g, s + 1))
                    pe.sem_inc(o_ready, 1)

            def total(g, pos):
                n = sum(s <= L.last[pos] for s in L.adds)
                pe.wait_ge(pool_added, add_count(g, n))
                for h in range(GH):
                    ins = nc.tensor.matmul(r_ps[h * HD:(h + 1) * HD, :], K.ones[:, 0:HD], psum_k[:, pos % 2, h, :],
                                           start=False, stop=True)
                ins.then_inc(o_ready, 1)

            def body(g, u, more):
                for s in range(1, L.NS + 1):
                    if s - 2 in L.last[:-1]:
                        total(g, L.last.index(s - 2))
                    items = L.stream(s, more)

                    at = L.places(len(items), 4 if L.direct(s - 1) else 3)

                    def between(place):
                        for i, p in zip(items, at):
                            if p == place:
                                stream_item(g, u, i)

                    if s < L.NS:
                        scores(g, u, s, between)
                    elif more:
                        scores(g + 1, 1 - u, 0)
                    product(g, u, s - 1, between)

            for j, it in enumerate(L.opening):
                item(0, 0, j, it, j % 2)
            scores(0, 0, 0)
            per_group(nc.tensor, body)


def phase_project(nc, K, x, wada, wproj, bproj):
    with ExitStack() as ctx:
        def sb(name, shape, dt=F32):
            return ctx.enter_context(nc.sbuf_tensor(name, shape, dt))

        def pb(name, shape):
            return ctx.enter_context(nc.psum_tensor(name, shape, F32))

        def sem(name):
            return ctx.enter_context(nc.semaphore(name))

        M0, M1 = M_GTA, M_GTM + KT
        ada = sb("ada2", [P, KT, (M1 - M0) * P])
        w_raw = sb("p_raw", [P, KT, D])
        w_hi = sb("p_hi", [P, KT, D], F32R)
        w_lo = sb("p_lo", [P, KT, D], F32R)
        bias = sb("p_bias", [1, D])
        bias_hi = sb("p_bias_hi", [1, D], F32R)
        bias_lo = sb("p_bias_lo", [1, D], F32R)
        one_row = sb("p_one_row", [1, P], F32R)
        one_sc = sb("p_one_sc", [P, BATCH, KT])
        diag = sb("p_diag", [P, 2, P])
        gate = K.gate
        o_in = sb("o_in", [P, 2, KT, CH])
        o_hi = sb("o_hi", [P, KT, CH], F32R)
        o_lo = sb("o_lo", [P, KT, CH], F32R)
        xs = sb("p_xs", [P, 2, TT, D])
        gated = sb("p_gated", [P, 2, D])
        xn = sb("p_xn", [P, TT, D])
        y32 = sb("p_y32", [P, 2, CH])
        xm_hi = sb("p_xm_hi", [P, KT, CH], F32R)
        xm_lo = sb("p_xm_lo", [P, KT, CH], F32R)
        bst = sb("p_bst", [P, TT, 6])
        mv = sb("p_mv", [P, TT, 2])
        ve = sb("p_ve", [P, TT])
        sd = sb("p_sd", [P, TT])
        rstd = sb("p_rstd", [P, TT])
        tmp = sb("p_tmp", [P, TT])
        tp = [pb(f"p_tp{i}", [P, CH]) for i in range(2)]
        acc = [pb(f"p_acc{i}", [P, D]) for i in range(TT)]
        misc = pb("p_misc", [P, CH])
        gps = pb("p_gps", [P, D])

        w_loaded = sem("p_w_loaded")
        ada_loaded = sem("p_ada_loaded")
        w_hi_ready = sem("p_w_hi_ready")
        w_split = sem("p_w_split")
        mod_ready = sem("p_mod_ready")
        diag_ready = sem("p_diag_ready")
        gate_ready = sem("p_gate_ready")
        gate_done = sem("p_gate_done")
        chain = sem("p_dve_chain")
        o_loaded = [sem(f"p_o_loaded{u}") for u in range(2)]
        x_loaded = [sem(f"p_x_loaded{u}") for u in range(2)]
        o_free = sem("p_o_free")
        hi_ready = sem("p_hi_ready")
        lo_ready = sem("p_lo_ready")
        acc_ready = sem("p_acc_ready")
        acc_free = sem("p_acc_free")
        x2_ready = sem("p_x2_ready")
        x2_stored = [sem(f"p_x2_stored{u}") for u in range(2)]
        x_free = sem("p_x_free")
        var_ready = sem("p_var_ready")
        sd_ready = sem("p_sd_ready")
        xn_ready = sem("p_xn_ready")
        tp_ready = sem("p_tp_ready")
        tp_free = sem("p_tp_free")
        xm_ready = sem("p_xm_ready")
        xm_stored = sem("p_xm_stored")
        xm_free = sem("p_xm_free")
        held = sem("c_wait_carrier")
        block = ctx.enter_context(nc.Block())

        @block.sync
        def _(sp):
            sp.dma_start(bias[:, :], bproj.rearrange("(a n) -> a n", a=1)).then_inc(w_loaded, 16)
            sp.dma_start(w_raw[:, :, :], wproj.rearrange("(t p) n -> p t n", p=P)).then_inc(w_loaded, 16)
            with nc.sync.Fori(0, NCH // 2) as i:
                for u in range(2):
                    n = 2 * i + u
                    b = n // (NCH // BATCH)
                    await_count(sp, held, o_free, n + 1)
                    sp.dma_start(o_in[:, u, :, :],
                                 K.o[bass.ds(b * KT, KT), :, bass.ds((n % (NCH // BATCH)) * CH, CH)].rearrange("g p n -> p g n")).then_inc(o_loaded[u], 16)
                    await_count(sp, held, x_free, n + 1)
                    sp.dma_start(xs[:, u, :, :],
                                 x[bass.ds(n * CH, CH), :].rearrange("(t p) d -> p t d", p=P)).then_inc(x_loaded[u], 16)

        @block.gpsimd
        def _(pool):
            pool.dma_start(ada[:, :, :], wada[:, M0 * P:M1 * P].rearrange("(t p) n -> p t n", p=P)).then_inc(ada_loaded, 16)

            def body(n, u):
                for t in range(KT):
                    pool.wait_ge(hi_ready, KT * n + t + 1)
                    if t == 0:
                        pool.wait_ge(acc_ready, TT * n + 1)
                    nc.gpsimd.tensor_tensor(o_lo[:, t, :], o_in[:, u, t, :], raw(o_hi[:, t, :]), ALU.subtract).then_inc(lo_ready, 1)
                pool.wait_ge(lo_ready, KT * (n + 1))
                pool.sem_inc(o_free, 1)

            pool.sem_inc(o_free, 2)
            with nc.gpsimd.Fori(0, NCH // 2) as i:
                for u in range(2):
                    body(2 * i + u, u)

        @block.scalar
        def _(act):
            act.wait_ge(w_loaded, 32)
            nc.scalar.activation(bias_hi[:, :], bias[:, :], ACT.Copy).then_inc(w_hi_ready, 1)
            nc.scalar.activation(w_hi[:, :, :], w_raw[:, :, :], ACT.Copy).then_inc(w_hi_ready, 1)

            def high(n, u):
                act.wait_ge(o_loaded[u], 16 * (n // 2) + 16)
                act.wait_ge(acc_ready, TT * n + 1)
                for t in range(KT):
                    nc.scalar.activation(o_hi[:, t, :], o_in[:, u, t, :], ACT.Copy).then_inc(hi_ready, 1)

            def body(n, u, more):
                if more:
                    high(n + 1, 1 - u)
                act.wait_ge(var_ready, n + 1)
                nc.scalar.activation(sd[:, :], ve[:, :], ACT.Sqrt).then_inc(sd_ready, 1)
                act.wait_ge(x2_ready, n + 1)
                act.dma_start(K.x2[bass.ds(n * CH, CH), :].rearrange("(t p) d -> p t d", p=P),
                              xs[:, u, :, :]).then_inc(x2_stored[u], 16)
                act.wait_ge(xm_ready, 2 * KT * (n + 1))
                for hl, t in enumerate((xm_hi, xm_lo)):
                    act.dma_start(K.xm2[hl, :, bass.ds(n * CH, CH)].rearrange("(t p) n -> p t n", p=P),
                                  raw(t[:, :, :])).then_inc(xm_stored, 16)
                act.wait_ge(x2_stored[u], 16 * (n // 2) + 16)
                act.sem_inc(x_free, 1)
                act.wait_ge(xm_stored, 32 * (n + 1))
                act.sem_inc(xm_free, 1)

            act.sem_inc(x_free, 2)
            act.sem_inc(xm_free, 1)
            high(0, 0)
            wave(nc.scalar, body, NCH // 2)

        @block.vector
        def _(dve):
            links = [0]

            def link(ins):
                links[0] += 1
                ins.then_inc(chain, 1)
                dve.wait_ge(chain, links[0])

            link(nc.vector.memset(raw(one_row[:, :]), 1.0))
            dve.wait_ge(w_hi_ready, 1)
            link(nc.vector.tensor_tensor(bias_lo[:, :], bias[:, :], raw(bias_hi[:, :]), ALU.subtract))
            dve.wait_ge(w_hi_ready, 2)
            nc.vector.tensor_tensor(w_lo[:, :, :], w_raw[:, :, :], raw(w_hi[:, :, :]), ALU.subtract).then_inc(w_split, 1)
            dve.wait_ge(mod_ready, 1)
            mod_ps = misc[:, 0:(M1 - M0) * BATCH].rearrange("p (m b) -> p b m", b=BATCH)
            for b in range(BATCH):
                link(nc.vector.tensor_tensor(K.mod[:, b, M0:M1], mod_ps[:, b, :], K.vcol[:, V_BADA + M0:V_BADA + M1], ALU.add))
                link(nc.vector.tensor_scalar(one_sc[:, b, :], K.mod[:, b, M_SCM:M_SCM + KT], 1.0, None, ALU.add))
                link(nc.vector.tensor_tensor(K.aff2[:, b, 0, :], one_sc[:, b, :], K.vcol[:, V_G2:V_G2 + KT], ALU.mult))
                link(nc.vector.tensor_tensor(K.aff2[:, b, 1, :], one_sc[:, b, :], K.vcol[:, V_BE2:V_BE2 + KT], ALU.mult))
                link(nc.vector.tensor_tensor(K.aff2[:, b, 1, :], K.aff2[:, b, 1, :], K.mod[:, b, M_SHM:M_SHM + KT], ALU.add))
            n = 0
            for which, m in enumerate((M_GTA, M_GTM)):
                for b in range(BATCH):
                    for t in range(KT):
                        if n >= 2:
                            dve.wait_ge(gate_ready, n - 1)
                        nc.vector.tensor_scalar(diag[:, n % 2, :], K.ident[:, :], K.mod[:, b, m + t:m + t + 1], None,
                                                ALU.mult).then_inc(diag_ready, 1)
                        n += 1
                    dve.wait_ge(gate_ready, n)
                    nc.vector.tensor_copy(gate[:, which, b, :], gps[:, :]).then_inc(gate_done, 1)
            dve.wait_ge(gate_done, 2 * BATCH)
            dve.sem_inc(tp_free, 2)
            dve.sem_inc(acc_free, TT)
            base = links[0]
            CHAINS = 2 + 5

            def body(n, u, more):
                at = [0]
                b = n // (NCH // BATCH)

                def lk(ins):
                    at[0] += 1
                    ins.then_inc(chain, 1)
                    dve.wait_ge(chain, n * CHAINS + base + at[0])

                def of_batch(t, *rest):
                    return t[(slice(None), *((b if isinstance(b, int) else bass.ds(b, 1)) if r is None else r for r in rest))]

                dve.wait_ge(x_loaded[u], 16 * (n // 2) + 16)
                for t in range(TT):
                    dve.wait_ge(acc_ready, TT * n + t + 1 + 1)
                    nc.vector.tensor_tensor(gated[:, t % 2, :], acc[t][:, :], of_batch(gate, 0, None, slice(None)),
                                            ALU.mult).then_inc(acc_free, 1)
                    dve.wait_ge(acc_free, TT * n + t + 1 + TT)
                    ins = nc.vector.tensor_tensor(xs[:, u, t, :], gated[:, t % 2, :], xs[:, u, t, :], ALU.add)
                ins.then_inc(x2_ready, 1)
                dve.wait_ge(x2_ready, n + 1)
                for t in range(TT - 1):
                    nc.vector.bn_stats(bst[:, t, :], xs[:, u, t, :])
                lk(nc.vector.bn_stats(bst[:, TT - 1, :], xs[:, u, TT - 1, :]))
                dve.sem_inc(held, 1)
                for t in range(TT - 1):
                    nc.vector.bn_aggr(mv[:, t, :], bst[:, t, :])
                lk(nc.vector.bn_aggr(mv[:, TT - 1, :], bst[:, TT - 1, :]))
                nc.vector.tensor_scalar(ve[:, :], mv[:, :, 1], EPS, None, ALU.add).then_inc(var_ready, 1)
                dve.wait_ge(sd_ready, n + 1)
                newton_rstd(nc, dve, lk, ve[:, :], sd[:, :], rstd[:, :], tmp[:, :])
                for t in range(TT):
                    nc.vector.tensor_scalar(xn[:, t, :], xs[:, u, t, :], mv[:, t, 0:1], rstd[:, t:t + 1],
                                            ALU.subtract, ALU.mult).then_inc(xn_ready, 1)
                for t in range(KT):
                    dve.wait_ge(tp_ready, n * KT + t + 1)
                    nc.vector.tensor_scalar(y32[:, t % 2, :], tp[t % 2][:, :], of_batch(K.aff2, None, 0, slice(t, t + 1)),
                                            of_batch(K.aff2, None, 1, slice(t, t + 1)), ALU.mult, ALU.add).then_inc(tp_free, 1)
                    dve.wait_ge(tp_free, n * KT + t + 1 + 2)
                    if t == 0:
                        dve.wait_ge(xm_free, n + 1)
                    nc.vector.tensor_copy(xm_hi[:, t, :], y32[:, t % 2, :]).then_inc(xm_ready, 1)
                    dve.wait_ge(xm_ready, 2 * (n * KT + t) + 1)
                    nc.vector.tensor_tensor(xm_lo[:, t, :], y32[:, t % 2, :], raw(xm_hi[:, t, :]),
                                            ALU.subtract).then_inc(xm_ready, 1)

            wave(nc.vector, body, NCH // 2)

        @block.tensor
        def _(pe):
            pe.sem_inc(acc_ready, 1)
            pe.wait_ge(ada_loaded, 16)
            for m in range(M1 - M0):
                for t in range(KT):
                    ins = nc.tensor.matmul(misc[:, m * BATCH:(m + 1) * BATCH], ada[:, t, m * P:(m + 1) * P],
                                           K.cond_t[:, t, :], start=(t == 0), stop=(t == KT - 1))
            ins.then_inc(mod_ready, 1)
            for n in range(2 * BATCH * KT):
                pe.wait_ge(diag_ready, n + 1)
                if n % KT == 0 and n:
                    pe.wait_ge(gate_done, n // KT)
                nc.tensor.matmul(gps[:, (n % KT) * P:(n % KT + 1) * P], K.ones[:, :], diag[:, n % 2, :],
                                 start=True, stop=True).then_inc(gate_ready, 1)
            pe.wait_ge(w_split, 1)

            def project(n):
                for s in range(TT):
                    pe.wait_ge(acc_free, TT * n + s + 1)
                    if s == 0:
                        pe.wait_ge(lo_ready, KT * (n + 1))
                    cols = slice(s * P, (s + 1) * P)
                    nc.tensor.matmul(acc[s][:, :], one_row[:, :], bias_hi[:, :], start=True, stop=False)
                    nc.tensor.matmul(acc[s][:, :], one_row[:, :], bias_lo[:, :], start=False, stop=False)
                    for t in range(KT):
                        for k, (a, b) in enumerate(terms(o_hi[:, t, cols], o_lo[:, t, cols], w_hi[:, t, :], w_lo[:, t, :])):
                            ins = nc.tensor.matmul(acc[s][:, :], a, b, start=False, stop=(t == KT - 1 and k == 2))
                    ins.then_inc(acc_ready, 1)

            def body(n, u, more):
                if more:
                    project(n + 1)
                for t in range(KT):
                    pe.wait_ge(tp_free, n * KT + t + 1)
                    if t == 0:
                        pe.wait_ge(xn_ready, TT * (n + 1))
                    for s in range(TT):
                        ins = nc.tensor.transpose(tp[t % 2][:, s * P:(s + 1) * P], xn[:, s, t * P:(t + 1) * P], K.ident[:, :])
                    ins.then_inc(tp_ready, 1)

            project(0)
            wave(nc.tensor, body, NCH // 2)


def phase_mlp(nc, K, w1, w2, b2, out):
    with ExitStack() as ctx:
        def sb(name, shape, dt=F32):
            return ctx.enter_context(nc.sbuf_tensor(name, shape, dt))

        def pb(name, shape):
            return ctx.enter_context(nc.psum_tensor(name, shape, F32))

        def sem(name):
            return ctx.enter_context(nc.semaphore(name))

        PIECE = CH
        NP = HID // PIECE
        LAG = 2
        w1_hi = sb("w1_hi", [P, NP, KT, PIECE], F32R)
        w1_lo = sb("w1_lo", [P, NP, KT, PIECE], F32R)
        w2_hi = sb("w2_hi", [P, NP, KT, D], F32R)
        w2_lo = sb("w2_lo", [P, NP, KT, D], F32R)
        bias = sb("m_bias", [1, D])
        bias_hi = sb("m_bias_hi", [1, D], F32R)
        bias_lo = sb("m_bias_lo", [1, D], F32R)
        one_row = sb("m_one_row", [1, P], F32R)
        xm = sb("m_xm", [P, 2, 2, KT, CH], F32R)
        xs = sb("m_xs", [P, TT, D])
        g32 = sb("m_g32", [P, 2, CH])
        g_hi = sb("m_g_hi", [P, 4, CH], F32R)
        g_lo = sb("m_g_lo", [P, 4, CH], F32R)
        gated = sb("m_gated", [P, 1, D])
        hid = [pb(f"m_hid{i}", [P, CH]) for i in range(4)]
        acc = [pb(f"m_acc{i}", [P, D]) for i in range(TT)]

        b_loaded = sem("m_b_loaded")
        w_loaded = [sem(f"m_w_loaded{u}") for u in range(2)]
        w_hi_ready = sem("m_w_hi_ready")
        w_split = sem("m_w_split")
        bias_ready = sem("m_bias_ready")
        xm_loaded = [sem(f"m_xm_loaded{u}") for u in range(2)]
        x_loaded = sem("m_x_loaded")
        hid_ready = sem("m_hid_ready")
        hid_free = sem("m_hid_free")
        g_hi_ready = sem("m_g_hi_ready")
        g_ready = sem("m_g_ready")
        used = sem("m_used")
        acc_ready = sem("m_acc_ready")
        acc_free = sem("m_acc_free")
        out_ready = sem("m_out_ready")
        out_stored = sem("m_out_stored")
        held = sem("m_wait_carrier")
        block = ctx.enter_context(nc.Block())

        def staged(i):
            return xs[:, i % 2 * 2:i % 2 * 2 + 2, :]

        def piece(i, w1_part, w2_part):
            half = slice(i % 2 * 2, i % 2 * 2 + 2)
            return (w1_part if i % 4 < 2 else w2_part)[:, i // 4, half, :]

        @block.sync
        def _(sp):
            def load_piece(i):
                k, half = i // 4, i % 2 * 2 * P
                src = w1[half:half + 2 * P, k * PIECE:(k + 1) * PIECE] if i % 4 < 2 else \
                    w2[k * CH + half:k * CH + half + 2 * P, :]
                sp.dma_start(staged(i), src.rearrange("(t p) n -> p t n", p=P)).then_inc(w_loaded[i % 2], 16)

            def load_xm(n, u):
                sp.dma_start(raw(xm[:, u, :, :, :]), K.xm2[:, :, bass.ds(n * CH, CH)]
                             .rearrange("a (t p) n -> p a t n", p=P)).then_inc(xm_loaded[u], 16)

            def load_x(n):
                sp.dma_start(xs[:, :, :], K.x2[bass.ds(n * CH, CH), :].rearrange("(t p) d -> p t d", p=P)).then_inc(x_loaded, 16)

            load_piece(0)
            load_piece(1)
            load_xm(0, 0)
            sp.dma_start(bias[:, :], b2.rearrange("(a n) -> a n", a=1)).then_inc(b_loaded, 16)
            for i in range(2, 4 * NP):
                await_count(sp, held, w_split, i - 1)
                load_piece(i)
            await_count(sp, held, w_split, 4 * NP)
            load_x(0)

            def body(n, u, more):
                if more:
                    await_count(sp, held, hid_ready, HT * (n + 2))
                    load_xm(n + 1, 1 - u)
                await_count(sp, held, out_ready, TT * (n + 1))
                sp.dma_start(out[bass.ds(n * CH, CH), :].rearrange("(t p) d -> p t d", p=P), xs[:, :, :]).then_inc(out_stored, 16)
                await_count(sp, held, out_stored, 16 * (n + 1))
                if more:
                    load_x(n + 1)

            wave(nc.sync, body, NCH // 2)

        @block.gpsimd
        def _(pool):
            pass

        @block.scalar
        def _(act):
            def high(i):
                act.wait_ge(w_loaded[i % 2], 16 * (i // 2 + 1))
                nc.scalar.activation(piece(i, w1_hi, w2_hi), staged(i), ACT.Copy).then_inc(w_hi_ready, 1)

            def tile(n, j):
                act.wait_ge(hid_ready, HT * (n + 2) + j + 1)
                act.wait_ge(g_ready, HT * n + j + 1)
                nc.scalar.activation(g32[:, j % 2, :], hid[j % 4][:, :], ACT.Gelu,
                                     bias=K.vcol[:, V_B1 + j:V_B1 + j + 1]).then_inc(hid_free, 1)
                act.wait_ge(hid_free, HT * n + j + 1 + 4)
                act.wait_ge(used, HT * n + j + 1)
                nc.scalar.activation(g_hi[:, j % 4, :], g32[:, j % 2, :], ACT.Copy).then_inc(g_hi_ready, 1)

            for i in range(4):
                high(i)
            act.wait_ge(b_loaded, 16)
            nc.scalar.activation(bias_hi[:, :], bias[:, :], ACT.Copy).then_inc(bias_ready, 1)
            for j in range(HT):
                if j // KT < NP - 1:
                    high(j + 4)
                tile(0, j)
            with nc.scalar.Fori(1, NCH) as n:
                for j in range(HT):
                    tile(n, j)

        @block.vector
        def _(dve):
            def low(i):
                dve.wait_ge(w_hi_ready, i + 1)
                nc.vector.tensor_tensor(piece(i, w1_lo, w2_lo), staged(i), raw(piece(i, w1_hi, w2_hi)), ALU.subtract).then_inc(w_split, 1)

            def tile(n, j):
                dve.wait_ge(g_hi_ready, HT * n + j + 1)
                nc.vector.tensor_tensor(g_lo[:, j % 4, :], g32[:, j % 2, :], raw(g_hi[:, j % 4, :]),
                                        ALU.subtract).then_inc(g_ready, 1)

            def finish(n, gate):
                dve.wait_ge(x_loaded, 16 * (n + 1))
                for s in range(TT):
                    dve.wait_ge(acc_ready, TT * n + s + 1)
                    nc.vector.tensor_tensor(gated[:, 0, :], acc[s][:, :], gate, ALU.mult).then_inc(acc_free, 1)
                    dve.wait_ge(acc_free, TT * n + s + 1 + TT)
                    nc.vector.tensor_tensor(xs[:, s, :], gated[:, 0, :], xs[:, s, :], ALU.add).then_inc(out_ready, 1)
                    dve.wait_ge(out_ready, TT * n + s + 1)

            nc.vector.memset(raw(one_row[:, :]), 1.0).then_inc(bias_ready, 1)
            for i in range(4):
                low(i)
            dve.wait_ge(bias_ready, 2)
            nc.vector.tensor_tensor(bias_lo[:, :], bias[:, :], raw(bias_hi[:, :]), ALU.subtract).then_inc(bias_ready, 1)
            dve.sem_inc(hid_free, 4)
            dve.sem_inc(g_ready, 2)
            dve.sem_inc(acc_free, TT)
            for j in range(HT):
                if j // KT < NP - 1:
                    low(j + 4)
                tile(0, j)
            finish(0, K.gate[:, 1, 0, :])
            with nc.vector.Fori(1, NCH) as n:
                for j in range(HT):
                    tile(n, j)
                finish(n, K.gate[:, 1, bass.ds(n // (NCH // BATCH), 1), :])

        @block.tensor
        def _(pe):
            pe.sem_inc(used, 4)
            pe.sem_inc(hid_ready, 2 * HT)

            def multiply(n, j):
                if j % KT == 0:
                    pe.wait_ge(w_split, 4 * (j // KT) + 4)
                if j == 0:
                    pe.wait_ge(bias_ready, 3)
                    for s in range(TT):
                        pe.wait_ge(acc_free, TT * n + s + 1)
                        nc.tensor.matmul(acc[s][:, :], one_row[:, :], bias_hi[:, :], start=True, stop=False)
                        nc.tensor.matmul(acc[s][:, :], one_row[:, :], bias_lo[:, :], start=False, stop=False)
                pe.wait_ge(g_ready, HT * n + j + 1 + 2)
                for s in range(TT):
                    cols = slice(s * P, (s + 1) * P)
                    for k, (a, b) in enumerate(terms(g_hi[:, j % 4, cols], g_lo[:, j % 4, cols],
                                                     w2_hi[:, j // KT, j % KT, :], w2_lo[:, j // KT, j % KT, :])):
                        ins = nc.tensor.matmul(acc[s][:, :], a, b, start=False, stop=(j == HT - 1 and k == 2))
                    if j == HT - 1:
                        ins.then_inc(acc_ready, 1)
                if j < HT - 1:
                    ins.then_inc(used, 1)
                else:
                    pe.wait_ge(acc_ready, TT * (n + 1))
                    pe.sem_inc(used, 1)

            def body(n, u, more):
                pe.wait_ge(xm_loaded[u], 16 * (n // 2) + 16)
                for j in range(HT + LAG):
                    if j < HT:
                        if j % KT == 0:
                            pe.wait_ge(w_split, 4 * (j // KT) + 2)
                        pe.wait_ge(hid_free, HT * n + j + 1)
                        cols = slice((j % KT) * P, (j % KT + 1) * P)
                        for t in range(KT):
                            for k, (a, b) in enumerate(terms(w1_hi[:, j // KT, t, cols], w1_lo[:, j // KT, t, cols],
                                                             xm[:, u, 0, t, :], xm[:, u, 1, t, :])):
                                ins = nc.tensor.matmul(hid[j % 4][:, :], a, b, start=(t == 0 and k == 0),
                                                       stop=(t == KT - 1 and k == 2))
                        ins.then_inc(hid_ready, 1)
                    if j >= LAG:
                        multiply(n, j - LAG)

            with nc.tensor.Fori(0, NCH // 2) as i:
                for u in range(2):
                    body(2 * i + u, u, True)


def build(nc, x, cond, wqkv, wproj, bproj, w1, b1, w2, b2, g1, be1, g2, be2, wada, bada, out, phases="abcd"):
    x = x.rearrange("b t d -> (b t) d")
    out = out.rearrange("b t d -> (b t) d")
    vecs = [(V_BADA, bada), (V_G1, g1), (V_BE1, be1), (V_G2, g2), (V_BE2, be2), (V_B1, b1)]
    with ExitStack() as ctx:
        K = Common(nc, ctx)
        phase_qkv(nc, K, x, cond, wada, bada, vecs, wqkv)
        if "b" in phases:
            phase_attention(nc, K)
        if "c" in phases:
            phase_project(nc, K, x, wada, wproj, bproj)
        if "d" in phases:
            phase_mlp(nc, K, w1, w2, b2, out)


_INS = ['x', 'cond_1024', 'L0_cond_Wqkv', 'L0_cond_Wproj', 'L0_cond_bproj', 'L0_cond_W1', 'L0_cond_b1',
        'L0_cond_W2', 'L0_cond_b2', 'L0_cond_g1', 'L0_cond_be1', 'L0_cond_g2', 'L0_cond_be2',
        'L0_cond_Wada', 'L0_cond_bada']
_OUTS = [((2, 2048, 512), 'float32')]


def kernel(**inputs):
    import numpy as _np
    import concourse.bacc as _bacc
    from concourse import mybir as _mybir
    from concourse.bass_utils import run_bass_kernel_spmd as _run

    nc = _bacc.Bacc("TRN2", target_bir_lowering=False, num_devices=1)
    arrays, args = {}, []
    for name in _INS:
        a = _np.ascontiguousarray(inputs[name])
        arrays[f"in_{name}_dram"] = a
        args.append(nc.dram_tensor(f"in_{name}_dram", a.shape, _mybir.dt.from_np(a.dtype), kind="ExternalInput").ap())
    for i, (shape, dtype) in enumerate(_OUTS):
        dt = _mybir.dt.from_np(_np.dtype(dtype))
        args.append(nc.dram_tensor(f"out_{i}_dram", shape, dt, kind="ExternalOutput").ap())
    build(nc, *args)
    r = _run(nc, [arrays], core_ids=[0])
    return r.results[0]["out_0_dram"]
```

```python
from contextlib import ExitStack

import concourse.bass as bass
from concourse import mybir

F32 = mybir.dt.float32
F32R = mybir.dt.float32r
BF16 = mybir.dt.bfloat16
ACT = mybir.ActivationFunctionType
ALU = mybir.AluOpType
AX = mybir.AxisListType

P = 128
BATCH, SEQ, D = 2, 2048, 512
HEADS, HD = 16, 32
HID = 4 * D
TOK = BATCH * SEQ
KT = D // P
HT = HID // P
CH = 512
NCH = TOK // CH
TT = CH // P
GH = P // HD
NG = BATCH * HEADS // GH
KEYT = SEQ // P
QC = SEQ // CH
SCALE = float(HD) ** -0.5
EPS = 1e-5
NEG = -1e30
LOWEST = -3e38

V_BADA, V_G1, V_BE1, V_G2, V_BE2, V_B1 = 0, 24, 28, 32, 36, 40
V_ROWS = 56
M_SHA, M_SCA, M_GTA, M_SHM, M_SCM, M_GTM = 0, 4, 8, 12, 16, 20


def raw(ap):
    return ap.bitcast(F32)


def terms(a_hi, a_lo, b_hi, b_lo):
    return ((a_hi, b_hi), (a_lo, b_hi), (a_hi, b_lo))


def await_count(eng, carrier, sem, value):
    eng.wait_ge(sem, value)
    eng.sem_inc(carrier, 1)


class Common:

    def __init__(self, nc, ctx):
        def sb(name, shape, dt=F32):
            return ctx.enter_context(nc.sbuf_tensor(name, shape, dt))

        def dram(name, shape):
            return nc.dram_tensor(name, shape, F32, kind="Internal").ap()

        self.ident = sb("ident", [P, P])
        self.ident_bf = sb("ident_bf", [P, P], BF16)
        self.mask_qk = sb("mask_qk", [P, P], BF16)
        self.mask_kq = sb("mask_kq", [P, P], BF16)
        self.ones = sb("ones", [P, P])
        self.vcol = sb("vcol", [P, V_ROWS])
        self.cond_t = sb("cond_t", [P, KT, BATCH])
        self.mod = sb("mod", [P, BATCH, 24])
        self.aff1 = sb("aff1", [P, BATCH, 2, KT])
        self.aff2 = sb("aff2", [P, BATCH, 2, KT])
        self.gate = sb("gate", [P, 2, BATCH, D])
        self.qk = dram("qk_scratch", (2, 2, D, TOK))
        self.v = dram("v_scratch", (TOK, D))
        self.m = dram("m_scratch", (QC, 2, GH * CH))
        self.o = dram("o_scratch", (NG, P, SEQ))
        self.x2 = dram("x2_scratch", (TOK, D))
        self.xm2 = dram("xm2_scratch", (D, TOK))


def wave(eng, body, chunks, peel=2):
    with eng.Fori(0, (chunks - peel) // 2) as i:
        for u in range(2):
            body(2 * i + u, u, peel)
    for n in range(chunks - peel, chunks):
        body(n, n % 2, chunks - 1 - n)


def newton_rstd(nc, dve, link, ve, sd, r, t):
    link(nc.vector.reciprocal(r, sd))
    link(nc.vector.tensor_tensor(t, r, r, ALU.mult))
    link(nc.vector.tensor_tensor(t, t, ve, ALU.mult))
    link(nc.vector.tensor_scalar(t, t, -0.5, 1.5, ALU.mult, ALU.add))
    link(nc.vector.tensor_tensor(r, r, t, ALU.mult))


def phase_qkv(nc, K, x, cond, wada, bada, vecs, wqkv):
    with ExitStack() as ctx:
        def sb(name, shape, dt=F32):
            return ctx.enter_context(nc.sbuf_tensor(name, shape, dt))

        def pb(name, shape):
            return ctx.enter_context(nc.psum_tensor(name, shape, F32))

        def sem(name):
            return ctx.enter_context(nc.semaphore(name))

        AHEAD = 5
        NT = 3 * D // P
        w_raw = sb("w_raw", [P, KT, 3 * D])
        w_hi = sb("w_hi", [P, KT, 3 * D], F32R)
        w_lo = sb("w_lo", [P, KT, 3 * D], F32R)
        ada = sb("ada", [P, KT, 2 * D])
        vrow = sb("vrow", [V_ROWS, P])
        cnd = sb("cnd", [BATCH, 3, D])
        xs = sb("xs", [P, 2, TT, D])
        xn = sb("xn", [P, TT, D])
        y32 = sb("y32", [P, 2, CH])
        xm_hi = sb("xm_hi", [P, 2, KT, CH], F32R)
        xm_lo = sb("xm_lo", [P, 2, KT, CH], F32R)
        st_hi = sb("st_hi", [P, 2, KT, CH], F32R)
        st_lo = sb("st_lo", [P, 2, KT, CH], F32R)
        st_v = sb("st_v", [P, TT, D])
        bst = sb("bst", [P, TT, 6])
        mv = sb("mv", [P, TT, 2])
        ve = sb("ve", [P, TT])
        sd = sb("sd", [P, TT])
        rstd = sb("rstd", [P, TT])
        tmp = sb("tmp", [P, TT])
        one_sc = sb("one_sc", [P, BATCH, KT])
        tp = [pb(f"tp{i}", [P, CH]) for i in range(2)]
        acc = [pb(f"acc{i}", [P, CH]) for i in range(4)]
        misc = pb("misc", [P, CH])

        c_ready = sem("a_constants_ready")
        v_loaded = sem("a_vectors_loaded")
        ada_loaded = sem("a_ada_loaded")
        w_loaded = [sem(f"a_w_loaded_{n}") for n in "qkv"]
        w_hi_ready = sem("a_w_hi_ready")
        w_split = [sem(f"a_w_split_{n}") for n in "qkv"]
        silu_e = sem("a_silu_exp_ready")
        silu_r = sem("a_silu_ready")
        small_pe = sem("a_small_pe")
        small_dve = sem("a_small_dve")
        x_loaded = [sem(f"a_x_loaded{u}") for u in range(2)]
        x_free = sem("a_x_free")
        var_ready = sem("a_var_ready")
        sd_ready = sem("a_sd_ready")
        xn_ready = sem("a_xn_ready")
        tp_ready = sem("a_tp_ready")
        tp_free = sem("a_tp_free")
        xm_ready = sem("a_xm_ready")
        acc_ready = sem("a_acc_ready")
        acc_free = sem("a_acc_free")
        hi_ready = sem("a_hi_ready")
        v_ready = sem("a_v_ready")
        qk_stored = [sem(f"a_{n}_stored") for n in "qk"]
        v_stored = sem("a_v_stored")
        first_chain = sem("a_dve_first_chain")
        chain = sem("a_dve_chain")
        held = sem("a_wait_carrier")
        block = ctx.enter_context(nc.Block())

        def part(w):
            return slice(w * D, (w + 1) * D)

        @block.sync
        def _(sp):
            sp.dma_start(cnd[:, 0, :], cond).then_inc(v_loaded, 16)
            for at, v in vecs:
                n = v.shape[0] // P
                sp.dma_start(vrow[at:at + n, :], v.rearrange("(t p) -> t p", p=P)).then_inc(v_loaded, 16)
            sp.dma_start(ada[:, :, :], wada[:, 0:2 * D].rearrange("(t p) n -> p t n", p=P)).then_inc(ada_loaded, 16)

            def load_x(n, u):
                sp.dma_start(xs[:, u, :, :], x[bass.ds(n * CH, CH), :].rearrange("(t p) d -> p t d", p=P)).then_inc(x_loaded[u], 16)

            load_x(0, 0)
            sp.wait_ge(ada_loaded, 16)
            for w in range(3):
                if w == 1:
                    sp.wait_ge(w_loaded[0], 16)
                sp.dma_start(w_raw[:, :, part(w)], wqkv[:, part(w)].rearrange("(t p) n -> p t n", p=P)).then_inc(w_loaded[w], 16)
            load_x(1, 1)
            with nc.sync.Fori(1, NCH // 2) as i:
                for u in range(2):
                    n = 2 * i + u
                    await_count(sp, held, x_free, n - 1)
                    load_x(n, u)

        @block.gpsimd
        def _(pool):
            nc.gpsimd.memset(K.ident[:, :], 0.0).then_inc(c_ready, 1)
            nc.gpsimd.memset(K.ident_bf[:, :], 0.0).then_inc(c_ready, 1)
            nc.gpsimd.memset(K.mask_qk[:, :], 0.0).then_inc(c_ready, 1)
            nc.gpsimd.memset(K.mask_kq[:, :], 0.0).then_inc(c_ready, 1)
            nc.gpsimd.memset(K.ones[:, :], 1.0).then_inc(c_ready, 1)
            pool.wait_ge(c_ready, 5)
            for m in (K.ident, K.ident_bf):
                nc.gpsimd.affine_select(out=m[:, :], in_=m[:, :], compare_op=ALU.not_equal, fill=1.0, base=0,
                                        pattern=[[-1, P]], channel_multiplier=1).then_inc(c_ready, 1)
            for m, step in ((K.mask_qk, 1), (K.mask_kq, -1)):
                nc.gpsimd.affine_select(out=m[:, :], in_=m[:, :], compare_op=ALU.is_ge, fill=NEG, base=0,
                                        pattern=[[-step, P]], channel_multiplier=step).then_inc(c_ready, 1)
            pool.wait_ge(w_hi_ready, 2)
            nc.gpsimd.tensor_tensor(w_lo[:, :, part(1)], w_raw[:, :, part(1)], raw(w_hi[:, :, part(1)]), ALU.subtract).then_inc(w_split[1], 1)

        @block.scalar
        def _(act):
            act.wait_ge(v_loaded, 16 * (1 + len(vecs)))
            nc.scalar.activation(cnd[:, 1, :], cnd[:, 0, :], ACT.Exp, scale=-1.0).then_inc(silu_e, 1)
            act.wait_ge(var_ready, 1)
            nc.scalar.activation(sd[:, :], ve[:, :], ACT.Sqrt).then_inc(sd_ready, 1)
            for w in range(3):
                act.wait_ge(w_loaded[w], 16)
                nc.scalar.activation(w_hi[:, :, part(w)], w_raw[:, :, part(w)], ACT.Copy).then_inc(w_hi_ready, 1)

            def std(n):
                act.wait_ge(var_ready, n + 1)
                nc.scalar.activation(sd[:, :], ve[:, :], ACT.Sqrt).then_inc(sd_ready, 1)

            def body(n, u, more):
                if more:
                    std(n + 1)
                for j in range(2 * KT):
                    act.wait_ge(acc_ready, NT * n + j + 1 + 1)
                    nc.scalar.activation(st_hi[:, j // KT, j % KT, :], acc[j % 4][:, :], ACT.Copy).then_inc(hi_ready, 1)
                    if j == KT:
                        store_qk(n, 0)
                store_qk(n, 1)
                act.wait_ge(v_ready, n + 1)
                act.dma_start(K.v[bass.ds(n * CH, CH), :].rearrange("(t p) d -> p t d", p=P),
                              st_v[:, :, :]).then_inc(v_stored, 16)
                for half in range(2):
                    act.wait_ge(qk_stored[half], 32 * (n + 1))
                act.wait_ge(v_stored, 16 * (n + 1))

            def store_qk(n, half):
                act.wait_ge(acc_free, NT * n + KT * (half + 1) + 4)
                for part, st in enumerate((st_hi, st_lo)):
                    act.dma_start(K.qk[half, part, :, bass.ds(n * CH, CH)].rearrange("(t p) n -> p t n", p=P),
                                  raw(st[:, half, :, :])).then_inc(qk_stored[half], 16)

            wave(nc.scalar, body, NCH)

        @block.vector
        def _(dve):
            links = [0]

            def link(ins):
                links[0] += 1
                ins.then_inc(first_chain, 1)
                dve.wait_ge(first_chain, links[0])

            dve.sem_inc(tp_free, 2)
            dve.sem_inc(acc_free, 4)

            dve.wait_ge(silu_e, 1)
            link(nc.vector.tensor_scalar(cnd[:, 2, :], cnd[:, 1, :], 1.0, None, ALU.add))
            link(nc.vector.reciprocal(cnd[:, 1, :], cnd[:, 2, :]))
            nc.vector.tensor_tensor(cnd[:, 2, :], cnd[:, 1, :], cnd[:, 0, :], ALU.mult).then_inc(silu_r, 1)
            dve.wait_ge(small_pe, 1)
            nc.vector.tensor_copy(K.vcol[:, :], misc[:, 0:V_ROWS]).then_inc(small_dve, 1)
            dve.wait_ge(small_pe, 2)
            nc.vector.tensor_copy(K.cond_t[:, :, :], misc[:, 64:64 + KT * BATCH].rearrange("p (t b) -> p t b", b=BATCH)).then_inc(small_dve, 1)
            CHAINS = 7

            def norm(n, u):
                at = [0]

                def lk(ins):
                    at[0] += 1
                    ins.then_inc(chain, 1)
                    dve.wait_ge(chain, n * CHAINS + at[0])

                dve.wait_ge(x_loaded[u], (n // 2) * 16 + 16)
                for t in range(TT - 1):
                    nc.vector.bn_stats(bst[:, t, :], xs[:, u, t, :])
                lk(nc.vector.bn_stats(bst[:, TT - 1, :], xs[:, u, TT - 1, :]))
                dve.sem_inc(held, 1)
                for t in range(TT - 1):
                    nc.vector.bn_aggr(mv[:, t, :], bst[:, t, :])
                lk(nc.vector.bn_aggr(mv[:, TT - 1, :], bst[:, TT - 1, :]))
                nc.vector.tensor_scalar(ve[:, :], mv[:, :, 1], EPS, None, ALU.add).then_inc(var_ready, 1)
                dve.wait_ge(sd_ready, n + 1)
                newton_rstd(nc, dve, lk, ve[:, :], sd[:, :], rstd[:, :], tmp[:, :])
                dve.wait_ge(tp_ready, n * KT + 1)
                for t in range(TT):
                    nc.vector.tensor_scalar(xn[:, t, :], xs[:, u, t, :], mv[:, t, 0:1], rstd[:, t:t + 1],
                                            ALU.subtract, ALU.mult).then_inc(xn_ready, 1)
                dve.wait_ge(xn_ready, TT * (n + 1))
                dve.sem_inc(x_free, 1)

            def modulate(n, u, t):
                b = n // (NCH // BATCH)
                dve.wait_ge(tp_ready, n * KT + t + 1 + 1)
                nc.vector.tensor_scalar(y32[:, t % 2, :], tp[t % 2][:, :], aff(b, 0, t), aff(b, 1, t),
                                        ALU.mult, ALU.add).then_inc(tp_free, 1)
                dve.wait_ge(tp_free, n * KT + t + 1 + 2)
                nc.vector.tensor_copy(xm_hi[:, u, t, :], y32[:, t % 2, :]).then_inc(xm_ready, 1)
                dve.wait_ge(xm_ready, 2 * (n * KT + t) + 1)
                nc.vector.tensor_tensor(xm_lo[:, u, t, :], y32[:, t % 2, :], raw(xm_hi[:, u, t, :]),
                                        ALU.subtract).then_inc(xm_ready, 1)

            def aff(b, which, t):
                if isinstance(b, int):
                    return K.aff1[:, b, which, t:t + 1]
                return K.aff1[:, bass.ds(b, 1), which, t:t + 1]

            def body(n, u, more):
                if more:
                    norm(n + 1, 1 - u)
                    dve.wait_ge(acc_ready, NT * n + 1)
                for j in range(NT):
                    if more and 0 <= j - AHEAD < KT:
                        modulate(n + 1, 1 - u, j - AHEAD)
                    if j < 2 * KT:
                        dve.wait_ge(hi_ready, 2 * KT * n + j + 1)
                        nc.vector.tensor_tensor(st_lo[:, j // KT, j % KT, :], acc[j % 4][:, :],
                                                raw(st_hi[:, j // KT, j % KT, :]), ALU.subtract).then_inc(acc_free, 1)
                    else:
                        dve.wait_ge(acc_ready, NT * n + j + 1 + 1)
                        ins = nc.vector.tensor_copy(st_v[:, j - 2 * KT, :], acc[j % 4][:, :])
                        ins.then_inc(acc_free, 1)
                dve.wait_ge(acc_free, NT * (n + 1) + 4)
                dve.sem_inc(v_ready, 1)

            def w_low(w):
                dve.wait_ge(w_hi_ready, w + 1)
                nc.vector.tensor_tensor(w_lo[:, :, part(w)], w_raw[:, :, part(w)], raw(w_hi[:, :, part(w)]), ALU.subtract).then_inc(w_split[w], 1)

            norm(0, 0)
            w_low(0)
            dve.wait_ge(small_dve, 1)
            dve.wait_ge(small_pe, 3)
            mod_ps = misc[:, 128:128 + 8 * BATCH].rearrange("p (m b) -> p b m", b=BATCH)
            for b in range(BATCH):
                link(nc.vector.tensor_tensor(K.mod[:, b, 0:8], mod_ps[:, b, :], K.vcol[:, V_BADA:V_BADA + 8], ALU.add))
                link(nc.vector.tensor_scalar(one_sc[:, b, :], K.mod[:, b, M_SCA:M_SCA + KT], 1.0, None, ALU.add))
                link(nc.vector.tensor_tensor(K.aff1[:, b, 0, :], one_sc[:, b, :], K.vcol[:, V_G1:V_G1 + KT], ALU.mult))
                link(nc.vector.tensor_tensor(K.aff1[:, b, 1, :], one_sc[:, b, :], K.vcol[:, V_BE1:V_BE1 + KT], ALU.mult))
                link(nc.vector.tensor_tensor(K.aff1[:, b, 1, :], K.aff1[:, b, 1, :], K.mod[:, b, M_SHA:M_SHA + KT], ALU.add))
            for t in range(KT):
                modulate(0, 0, t)
            w_low(2)
            wave(nc.vector, body, NCH)

        @block.tensor
        def _(pe):
            pe.wait_ge(c_ready, 9)
            pe.wait_ge(v_loaded, 16 * (1 + len(vecs)))
            nc.tensor.transpose(misc[:, 0:V_ROWS], vrow[:, :], K.ident[0:V_ROWS, 0:V_ROWS]).then_inc(small_pe, 1)
            pe.wait_ge(silu_r, 1)
            pe.wait_ge(small_dve, 1)
            for t in range(KT):
                ins = nc.tensor.transpose(misc[:, 64 + t * BATCH:64 + (t + 1) * BATCH], cnd[:, 2, t * P:(t + 1) * P],
                                          K.ident[0:BATCH, 0:BATCH])
            ins.then_inc(small_pe, 1)
            pe.wait_ge(small_dve, 2)
            pe.wait_ge(ada_loaded, 16)
            for m in range(8):
                for t in range(KT):
                    ins = nc.tensor.matmul(misc[:, 128 + m * BATCH:128 + (m + 1) * BATCH], ada[:, t, m * P:(m + 1) * P],
                                           K.cond_t[:, t, :], start=(t == 0), stop=(t == KT - 1))
            ins.then_inc(small_pe, 1)
            pe.sem_inc(tp_ready, 1)
            pe.sem_inc(acc_ready, 1)

            def turn(n, t):
                pe.wait_ge(tp_free, n * KT + t + 1)
                if t == 0:
                    pe.wait_ge(xn_ready, TT * (n + 1))
                for s in range(TT):
                    ins = nc.tensor.transpose(tp[t % 2][:, s * P:(s + 1) * P], xn[:, s, t * P:(t + 1) * P], K.ident[:, :])
                ins.then_inc(tp_ready, 1)

            def body(n, u, more):
                pe.wait_ge(xm_ready, 2 * KT * (n + 1))
                for j in range(NT):
                    if more and 0 <= j - AHEAD < KT:
                        turn(n + 1, j - AHEAD)
                    pe.wait_ge(acc_free, NT * n + j + 1)
                    if j % KT == 0:
                        pe.wait_ge(w_split[j // KT], 1)
                    for t in range(KT):
                        if j < 2 * KT:
                            cols = slice(j * P, (j + 1) * P)
                            ops = terms(w_hi[:, t, cols], w_lo[:, t, cols], xm_hi[:, u, t, :], xm_lo[:, u, t, :])
                        else:
                            cols = slice((j - 2 * KT) * P, (j - 2 * KT + 1) * P)
                            ops = terms(xm_hi[:, u, t, cols], xm_lo[:, u, t, cols], w_hi[:, t, 2 * D:], w_lo[:, t, 2 * D:])
                        for k, (a, b) in enumerate(ops):
                            ins = nc.tensor.matmul(acc[j % 4][:, :], a, b, start=(t == 0 and k == 0),
                                                   stop=(t == KT - 1 and k == 2))
                    ins.then_inc(acc_ready, 1)

            for t in range(KT):
                turn(0, t)
            wave(nc.tensor, body, NCH)


class Plan:

    DIRECT = 3

    def __init__(self):
        self.order = list(range(QC))[::-1]
        self.steps = [(pos, kt) for pos, c in enumerate(self.order) for kt in range((c + 1) * TT)]
        self.NS = len(self.steps)
        self.last = [self.steps.index((pos, (c + 1) * TT - 1)) for pos, c in enumerate(self.order)]
        LATER = 3
        self.batch = [[(pos, h, t, kc, min(CH, (c * TT + t + 1) * P - kc * CH))
                       for kc in range(c + 1)[::-1] for h in range(GH) for t in range(TT)]
                      for pos, c in enumerate(self.order)]
        self.opening = self.batch[0] + [0]
        self.items = []
        for pos in (*range(1, QC), 0):
            start = len(self.items)
            self.items += self.batch[pos]
            if pos != 1:
                self.items.insert(start + (LATER if pos else 0), (pos or QC) - 1)
        self.items.append(0)
        self.NI = len(self.items)
        self.adds, done = [], 0
        self.released = []
        for s, (pos, kt) in enumerate(self.steps):
            if self.direct(s):
                self.released.append(done)
                continue
            if kt == 1:
                self.released.append(done + 1)
            else:
                done += 1
                self.adds.append(s)
                self.released.append(done)
        self.NA = done
        weight = [self.width(s) + (P if self.steps[s][0] == 0 else 0) for s in range(self.NS)]
        FROM, TO = 2, self.NS - 5
        span = sum(weight[FROM:TO])
        EXTRA = 100
        price = [P if isinstance(it, int) else it[4] + EXTRA for it in self.items]
        total, spent, at, passed = sum(price), 0, 0, 0
        self.items_at = [[] for _ in self.steps]
        for s in range(FROM, TO):
            passed += weight[s]
            while at < self.NI - 1 and (spent + price[at] / 2) * span <= passed * total:
                self.items_at[s].append(at)
                spent += price[at]
                at += 1
        self.items_at[TO - 1] += range(at, self.NI - 1)
        self.items_at[TO].append(self.NI - 1)

    def direct(self, s):
        pos, kt = self.steps[s]
        return pos == QC - 1 or kt % self.DIRECT == 0

    def mid(self, s):
        pos, kt = self.steps[s]
        return max(0, kt - self.order[pos] * TT) * P

    def width(self, s):
        return CH - self.mid(s)

    def place(self, rank, sums):
        return min((0, 2, 3, GH, GH + 1)[min(rank, 4)], GH + 1 if sums else GH)

    def stream(self, s, more):
        if s >= self.NS:
            return []
        return [i for i in self.items_at[s] if more or self.group(0, i) == 0]

    def group(self, g, i):
        it = self.items[i]
        return g + (1 if (it if isinstance(it, int) else it[0]) == 0 else 0)

    def through(self, pos):
        return self.items.index(self.batch[pos][-1]) + 1


def phase_attention(nc, K, wada):
    L = Plan()
    ROWS, MROWS = 3 * HD, 3 * HD + 2
    BUF = 4
    RING = 3
    INV = 4
    M0, M1 = M_GTA, M_GTM + KT
    MOD_AT, LOAD_AT = (25, 28, 34, 37), (28, 31)
    EACH = 6
    MROW = GH * TT
    with ExitStack() as ctx:
        def sb(name, shape, dt=F32):
            return ctx.enter_context(nc.sbuf_tensor(name, shape, dt))

        def pb(name, shape):
            return ctx.enter_context(nc.psum_tensor(name, shape, F32))

        def sem(name):
            return ctx.enter_context(nc.semaphore(name))

        k_st = sb("k_st", [P, 2, GH, SEQ], F32R)
        q_st = sb("q_st", [P, 2, GH, CH], F32R)
        qx_st = sb("qx_st", [P, 2, GH, CH], F32R)
        v_sb = sb("v_sb", [P, 2, KEYT, P])
        prob = sb("prob", [P, BUF, GH, CH])
        psum_k = sb("psum_k", [P, 2, GH, CH])
        o_raw = sb("o_raw", [P, 2, 2, CH])
        o_sb = sb("o_sb", [P, 2, CH])
        one_sc = sb("b_one_sc", [P, BATCH, KT])
        ada = sb("ada2", [P, 2, KT, KT * P])
        part = sb("part", [P, 2, MROW, QC])
        mcol = sb("mcol", [P, 2, MROW])
        m_hi = sb("m_hi", [MROW, 2, P], F32R)
        m_lo = sb("m_lo", [MROW, 2, P], F32R)
        st = [pb(f"st{i}", [P, CH]) for i in range(RING)]
        mx = [pb(f"mx{i}", [P, CH]) for i in range(RING)]
        o_ps = pb("o_ps", [P, CH])
        r_ps = pb("r_ps", [P, CH])

        ring = mx + st

        ones_ready = sem("b_ones_ready")
        k_loaded = [[sem(f"b_k_loaded{u}{kc}") for kc in range(QC)] for u in range(2)]
        v_loaded = [sem(f"b_v_loaded{u}") for u in range(2)]
        q_loaded = [sem(f"b_q_loaded{u}") for u in range(2)]
        qx_loaded = [sem(f"b_qx_loaded{u}") for u in range(2)]
        m_ready = sem("b_m_ready")
        m_stored = sem("b_m_stored")
        mx_ready = sem("b_mx_ready")
        mx_free = sem("b_mx_free")
        mcol_ready = sem("b_mcol_ready")
        st_ready = sem("b_st_ready")
        exp_done = sem("b_exp_done")
        pv_done = sem("b_pv_done")
        pool_added = sem("b_pool_added")
        o_ready = sem("b_o_ready")
        o_copied = sem("b_o_copied")
        inverted = sem("b_inverted")
        o_done = sem("b_o_done")
        o_stored = [sem(f"b_o_stored{u}") for u in range(2)]
        o_sb_free = sem("b_o_sb_free")
        ada_loaded = [sem(f"b_ada_loaded{u}") for u in range(2)]
        mod_ready = sem("b_mod_ready")
        chain = sem("b_dve_chain")
        held = sem("b_wait_carrier")
        block = ctx.enter_context(nc.Block())

        def st_count(g, tiles):
            return GH * L.NS * g + tiles + 1

        def exp_count(g, tiles):
            return GH * L.NS * g + tiles + 1

        def pv_count(g, steps):
            return L.NS * g + steps + BUF

        def add_count(g, n):
            return L.NA * g + n + L.NA

        def item_count(g, n):
            return len(L.opening) + L.NI * g + n

        def before(i):
            return max(0, i - RING + 1)

        def o_reuse(g, pos):
            return QC * g + 1 + (1 if pos == 2 else 0)

        def per_group(eng, body):
            with eng.Fori(0, NG // 2 - 1) as i:
                for u in range(2):
                    body(2 * i + u, u, True)
            body(NG - 2, 0, True)
            body(NG - 1, 1, False)

        @block.sync
        def _(sp):
            def place(g):
                return g // (HEADS // GH), g % (HEADS // GH)

            def load_k(g, u, kc):
                b, gg = place(g)
                cols = slice(kc * CH, (kc + 1) * CH)
                for row, hl in enumerate((0, 1, 0)):
                    sp.dma_start(raw(k_st[row * HD:(row + 1) * HD, u, :, cols]),
                                 K.qk[1, hl, bass.ds(gg * P, P), bass.ds(b * SEQ + kc * CH, CH)]
                                 .rearrange("(h r) n -> r h n", r=HD)).then_inc(k_loaded[u][kc], 16)

            def load_queries(g, pos, dst, loaded):
                b, gg = place(g)
                for row, hl in enumerate((0, 0, 1)):
                    sp.dma_start(raw(dst[row * HD:(row + 1) * HD, pos % 2, :, :]),
                                 K.qk[0, hl, bass.ds(gg * P, P), bass.ds(b * SEQ + L.order[pos] * CH, CH)]
                                 .rearrange("(h r) n -> r h n", r=HD)).then_inc(loaded[pos % 2], 16)

            def load_qx(g, pos):
                load_queries(g, pos, qx_st, qx_loaded)

            def load_v(g, u):
                b, gg = place(g)
                sp.dma_start(v_sb[:, u, :, :],
                             K.v[bass.ds(b * SEQ, SEQ), bass.ds(gg * P, P)].rearrange("(t p) d -> p t d", p=P)).then_inc(v_loaded[u], 16)

            def store_m_load_q(g, pos):
                load_queries(g, pos, q_st, q_loaded)
                await_count(sp, held, m_ready, 2 * (QC * g + pos + 1))
                for hl, t in enumerate((m_hi, m_lo)):
                    sp.dma_start(K.m[pos, hl, :].rearrange("(r n) -> r n", n=P), raw(t[:, pos % 2, :])).then_inc(m_stored, 16)
                await_count(sp, held, m_stored, 32 * (QC * g + pos + 1) + 64)
                sp.dma_start(raw(q_st[ROWS:MROWS, pos % 2, :, :]),
                             K.m[pos, :, :].rearrange("a (h n) -> a h n", h=GH)).then_inc(q_loaded[pos % 2], 16)

            def jobs_done(g, pos):
                await_count(sp, held, mx_ready, item_count(g, L.through(pos)))

            def steps_done(g, pos):
                await_count(sp, held, st_ready, st_count(g, GH * (L.last[pos] + 1)))

            def store_o(g, pos):
                await_count(sp, held, o_done, QC * g + pos + 1 + 2)
                c = L.order[pos]
                sp.dma_start(K.o[bass.ds(g, 1), :, c * CH:(c + 1) * CH].rearrange("g r n -> (g r) n"),
                             o_sb[:, pos % 2, :]).then_inc(o_stored[pos % 2], 16)

            def stored_o(g, pos):
                await_count(sp, held, o_stored[pos % 2], 16 * (2 * g + pos // 2 + 1))
                sp.sem_inc(o_sb_free, 1)

            sp.sem_inc(m_stored, 64)
            load_qx(0, 0)
            for kc in range(QC)[::-1]:
                load_k(0, 0, kc)
            load_qx(0, 1)
            load_v(0, 0)
            await_count(sp, held, mx_ready, len(L.batch[0]))
            load_qx(0, 2)
            store_m_load_q(0, 0)

            def body(g, u, more):
                if more:
                    await_count(sp, held, st_ready, st_count(g, 0))
                    for kc in range(QC)[::-1]:
                        load_k(g + 1, 1 - u, kc)
                    await_count(sp, held, pv_done, pv_count(g, 0))
                    load_v(g + 1, 1 - u)
                jobs_done(g, 1)
                load_qx(g, 3)
                store_m_load_q(g, 1)
                jobs_done(g, 2)
                if more:
                    load_qx(g + 1, 0)
                steps_done(g, 0)
                store_m_load_q(g, 2)
                store_o(g, 0)
                jobs_done(g, 3)
                if more:
                    load_qx(g + 1, 1)
                stored_o(g, 0)
                steps_done(g, 1)
                store_m_load_q(g, 3)
                store_o(g, 1)
                if more:
                    jobs_done(g, 0)
                    load_qx(g + 1, 2)
                    steps_done(g, 2)
                    store_m_load_q(g + 1, 0)
                stored_o(g, 1)
                store_o(g, 2)
                stored_o(g, 2)
                store_o(g, 3)
                stored_o(g, 3)

            per_group(nc.sync, body)

        @block.gpsimd
        def _(pool):
            nc.gpsimd.memset(raw(k_st[ROWS:MROWS, :, :, :]), 1.0).then_inc(ones_ready, 1)
            pool.sem_inc(pool_added, L.NA)

            def body(g, u, more):
                for n, s in enumerate(L.adds):
                    pos, kt = L.steps[s]
                    m = L.mid(s)
                    dst = psum_k[:, pos % 2, :, m:]
                    pool.wait_ge(exp_done, exp_count(g, GH * (s + 1)))
                    if kt == 2:
                        pool.wait_ge(o_ready, o_reuse(g, pos))
                        src = prob[:, (s - 1) % BUF, :, m:]
                    else:
                        pool.wait_ge(pool_added, add_count(g, n))
                        src = dst
                    nc.gpsimd.tensor_tensor(dst, src, prob[:, s % BUF, :, m:], ALU.add).then_inc(pool_added, 1)

            per_group(nc.gpsimd, body)

        @block.scalar
        def _(act):
            act.sem_inc(exp_done, 1)
            act.sem_inc(o_done, 2)
            act.sem_inc(o_copied, 1)

            def exps(g, s):
                m = L.mid(s)
                act.wait_ge(pv_done, pv_count(g, s + 1 - BUF))
                n = L.released[s - BUF] if s >= BUF else L.released[s - BUF] - L.NA
                act.wait_ge(pool_added, add_count(g, n))
                for h in range(GH):
                    n = GH * s + h
                    act.wait_ge(st_ready, st_count(g, n + 1))
                    nc.scalar.activation(prob[:, s % BUF, h, m:], st[n % RING][:, m:], ACT.Exp, scale=SCALE).then_inc(exp_done, 1)

            def load_ada(n):
                act.dma_start(ada[:, n % 2, :, :], wada[:, (M0 + n * KT) * P:(M0 + (n + 1) * KT) * P]
                              .rearrange("(t p) n -> p t n", p=P)).then_inc(ada_loaded[n % 2], 16)

            def copy(g, pos):
                act.wait_ge(pv_done, pv_count(g, L.last[pos] + 1))
                act.wait_ge(o_done, QC * g + pos + 1)
                nc.scalar.activation(o_raw[:, pos % 2, 0, :], o_ps[:, :], ACT.Copy).then_inc(o_copied, 1)
                act.wait_ge(o_ready, QC * g + pos + 1 + 1)
                nc.scalar.activation(o_raw[:, pos % 2, 1, :], r_ps[:, :], ACT.Copy).then_inc(o_copied, 1)

            def body(g, u, more):
                for s in range(1, L.NS + 1):
                    if s < L.NS:
                        exps(g, s)
                    elif more:
                        exps(g + 1, 0)
                    if not more and s in LOAD_AT:
                        n = LOAD_AT.index(s) + 2
                        act.wait_ge(mod_ready, n - 1)
                        load_ada(n)
                    if s - 1 in L.last:
                        copy(g, L.last.index(s - 1))

            load_ada(0)
            load_ada(1)
            exps(0, 0)
            per_group(nc.scalar, body)

        @block.vector
        def _(dve):
            dve.sem_inc(mx_free, 2)

            def item(g, pre, it, bank):
                if isinstance(it, int):
                    return turn(g, pre, it, bank)
                pos, h, t, kc, w = it
                dve.wait_ge(mx_ready, pre + 1)
                nc.vector.tensor_reduce(part[:, pos % 2, h * TT + t, kc:kc + 1], bank[:, 0:w], AX.X, ALU.max).then_inc(mx_free, 1)
                if it is L.batch[pos][-1]:
                    dve.wait_ge(mx_free, pre + 1 + 2)
                    nc.vector.tensor_reduce(mcol[:, pos % 2, :], part[:, pos % 2, :, 0:L.order[pos] + 1],
                                            AX.X, ALU.max).then_inc(mcol_ready, 1)

            def turn(g, pre, pos, bank):
                n = QC * g + pos
                dve.wait_ge(mx_ready, pre + 1)
                dve.wait_ge(m_stored, 32 * n + 32)
                m = bank[0:MROW, 0:P]
                nc.vector.tensor_scalar(m_hi[:, pos % 2, :], m, -1.0, None, ALU.mult).then_inc(m_ready, 1)
                dve.wait_ge(m_ready, 2 * n + 1)
                nc.vector.scalar_tensor_tensor(out=m_lo[:, pos % 2, :], in0=m, scalar=-1.0, in1=raw(m_hi[:, pos % 2, :]),
                                               op0=ALU.mult, op1=ALU.subtract).then_inc(m_ready, 1)
                dve.wait_ge(m_ready, 2 * n + 2)
                dve.sem_inc(mx_free, 1)

            def invert(g, pos, j):
                r = o_raw[:, pos % 2, 1, j * CH // INV:(j + 1) * CH // INV]
                dve.wait_ge(o_copied, 2 * (QC * g + pos) + 2 + 1)
                nc.vector.reciprocal(r, r).then_inc(inverted, 1)

            def finish(g, pos):
                dve.wait_ge(inverted, INV * (QC * g + pos + 1))
                dve.wait_ge(o_sb_free, QC * g + pos + 1)
                nc.vector.tensor_tensor(o_sb[:, pos % 2, :], o_raw[:, pos % 2, 0, :], o_raw[:, pos % 2, 1, :],
                                        ALU.mult).then_inc(o_done, 1)

            def body(g, u, more):
                for s in range(1, L.NS + 2):
                    for pos in range(QC - 1):
                        j = s - 2 - L.last[pos]
                        if 0 <= j < INV:
                            invert(g, pos, j)
                        if j == INV:
                            finish(g, pos)
                    items = L.stream(s, more)
                    for i in items:
                        item(L.group(g, i), item_count(g, i), L.items[i], mx[i % RING])
                for j in range(INV):
                    invert(g, QC - 1, j)
                finish(g, QC - 1)

            dve.sem_inc(o_sb_free, 2)
            for j, it in enumerate(L.opening):
                item(0, j, it, ring[j % len(ring)])
            per_group(nc.vector, body)
            dve.wait_ge(mod_ready, (M1 - M0) // KT)
            mod_ps = mx[0][:, 0:(M1 - M0) * BATCH].rearrange("p (m b) -> p b m", b=BATCH)
            links = [0]

            def link(ins):
                links[0] += 1
                ins.then_inc(chain, 1)
                dve.wait_ge(chain, links[0])

            for b in range(BATCH):
                link(nc.vector.tensor_tensor(K.mod[:, b, M0:M1], mod_ps[:, b, :], K.vcol[:, V_BADA + M0:V_BADA + M1], ALU.add))
                link(nc.vector.tensor_scalar(one_sc[:, b, :], K.mod[:, b, M_SCM:M_SCM + KT], 1.0, None, ALU.add))
                link(nc.vector.tensor_tensor(K.aff2[:, b, 0, :], one_sc[:, b, :], K.vcol[:, V_G2:V_G2 + KT], ALU.mult))
                link(nc.vector.tensor_tensor(K.aff2[:, b, 1, :], one_sc[:, b, :], K.vcol[:, V_BE2:V_BE2 + KT], ALU.mult))
                link(nc.vector.tensor_tensor(K.aff2[:, b, 1, :], K.aff2[:, b, 1, :], K.mod[:, b, M_SHM:M_SHM + KT], ALU.add))

        @block.tensor
        def _(pe):
            pe.sem_inc(st_ready, 1)
            pe.sem_inc(pv_done, BUF)
            pe.sem_inc(o_ready, 1)

            def item(g, u, pre, it, out, free):
                if not isinstance(free, int) or free > 0:
                    pe.wait_ge(mx_free, free)
                if isinstance(it, int):
                    pe.wait_ge(mcol_ready, QC * g + it + 1)
                    nc.tensor.transpose(out[0:MROW, 0:P], mcol[:, it % 2, :], K.ident[:, :]).then_inc(mx_ready, 1)
                    return
                pos, h, t, kc, w = it
                if it is L.batch[pos][0]:
                    pe.wait_ge(qx_loaded[pos % 2], 48 * (2 * g + pos // 2 + 1))
                if pos == 0 and h == t == 0:
                    pe.wait_ge(k_loaded[u][kc], 48 * (g // 2 + 1))
                diagonal = kc == L.order[pos]
                ins = nc.tensor.matmul(out[:, 0:w], qx_st[0:ROWS, pos % 2, h, t * P:(t + 1) * P],
                                       k_st[0:ROWS, u, h, kc * CH:kc * CH + w], start=True, stop=not diagonal)
                if diagonal:
                    ins = nc.tensor.matmul(out[:, w - P:w], K.ident_bf[:, :], K.mask_qk[:, :], start=False, stop=True)
                ins.then_inc(mx_ready, 1)

            def stream_item(g, u, i):
                mine = L.group(0, i) == 0
                item(L.group(g, i), u if mine else 1 - u, item_count(g, i), L.items[i], mx[i % RING], item_count(g, before(i)) + 2)

            def scores(g, u, s, between=lambda part: None):
                pos, kt = L.steps[s]
                m = L.mid(s)
                masked = kt >= L.order[pos] * TT
                if kt == 0:
                    pe.wait_ge(q_loaded[pos % 2], 64 * (2 * g + pos // 2 + 1))
                for h in range(GH):
                    n = GH * s + h
                    pe.wait_ge(exp_done, exp_count(g, before(n)))
                    out = st[n % RING]
                    ins = nc.tensor.matmul(out[:, m:], k_st[0:MROWS, u, h, kt * P:(kt + 1) * P],
                                           q_st[0:MROWS, pos % 2, h, m:], start=True, stop=not masked)
                    if masked:
                        ins = nc.tensor.matmul(out[:, m:m + P], K.ident_bf[:, :], K.mask_kq[:, :], start=False, stop=True)
                    ins.then_inc(st_ready, 1)
                    between(h)

            def product(g, u, s, between):
                pos, kt = L.steps[s]
                m = L.mid(s)
                end = s == L.last[pos]
                if s == 0:
                    pe.wait_ge(v_loaded[u], 16 * (g // 2 + 1))
                if kt == 0:
                    pe.wait_ge(o_copied, 2 * (QC * g + pos) + 1)
                pe.wait_ge(exp_done, exp_count(g, GH * (s + 1)))
                for h in range(GH):
                    rows = slice(h * HD, (h + 1) * HD)
                    ins = nc.tensor.matmul(o_ps[rows, m:], v_sb[:, u, kt, rows], prob[:, s % BUF, h, m:],
                                           start=(kt == 0), stop=end)
                if L.direct(s):
                    between(GH)
                    for h in range(GH):
                        ins = nc.tensor.matmul(r_ps[h * HD:(h + 1) * HD, m:], K.ones[:, 0:HD], prob[:, s % BUF, h, m:],
                                               start=(kt == 0), stop=end and pos == QC - 1)
                ins.then_inc(pv_done, 1)
                between(GH + 1 if L.direct(s) else GH)
                if end and pos == QC - 1:
                    pe.wait_ge(pv_done, pv_count(g, s + 1))
                    pe.sem_inc(o_ready, 1)

            def total(g, pos):
                n = sum(s <= L.last[pos] for s in L.adds)
                pe.wait_ge(pool_added, add_count(g, n))
                for h in range(GH):
                    ins = nc.tensor.matmul(r_ps[h * HD:(h + 1) * HD, :], K.ones[:, 0:HD], psum_k[:, pos % 2, h, :],
                                           start=False, stop=True)
                ins.then_inc(o_ready, 1)

            def modulation(s):
                for n, at in enumerate(MOD_AT):
                    for j in range((s - at) * EACH, min((s - at + 1) * EACH, KT * KT)):
                        if j < 0:
                            continue
                        if j == 0:
                            pe.wait_ge(ada_loaded[n % 2], 16 * (n // 2 + 1))
                        if n == j == 0:
                            pe.wait_ge(mx_free, item_count(NG - 1, L.through(QC - 1) + 1) + 2)
                        m, t = j // KT, j % KT
                        ins = nc.tensor.matmul(mx[0][:, (n * KT + m) * BATCH:(n * KT + m + 1) * BATCH],
                                               ada[:, n % 2, t, m * P:(m + 1) * P], K.cond_t[:, t, :],
                                               start=(t == 0), stop=(t == KT - 1))
                        if j == KT * KT - 1:
                            ins.then_inc(mod_ready, 1)

            def body(g, u, more):
                for s in range(1, L.NS + 1):
                    if s - 2 in L.last[:-1]:
                        total(g, L.last.index(s - 2))
                    items = L.stream(s, more)


                    def between(part):
                        for rank, i in enumerate(items):
                            if L.place(rank, L.direct(s - 1)) == part:
                                stream_item(g, u, i)

                    if s < L.NS:
                        scores(g, u, s, between)
                    elif more:
                        scores(g + 1, 1 - u, 0)
                    product(g, u, s - 1, between)
                    if not more:
                        modulation(s)

            for j, it in enumerate(L.opening):
                item(0, 0, j, it, ring[j % len(ring)], (j - len(ring) + 1 + 2) * (j >= len(ring)))
            pe.wait_ge(mx_free, len(L.opening) + 2)
            pe.wait_ge(ones_ready, 1)
            scores(0, 0, 0)
            per_group(nc.tensor, body)


def phase_project(nc, K, x, wproj, bproj):
    with ExitStack() as ctx:
        def sb(name, shape, dt=F32):
            return ctx.enter_context(nc.sbuf_tensor(name, shape, dt))

        def pb(name, shape):
            return ctx.enter_context(nc.psum_tensor(name, shape, F32))

        def sem(name):
            return ctx.enter_context(nc.semaphore(name))

        w_raw = sb("p_raw", [P, KT, D])
        w_hi = sb("p_hi", [P, KT, D], F32R)
        w_lo = sb("p_lo", [P, KT, D], F32R)
        bias = sb("p_bias", [1, D])
        bias_hi = sb("p_bias_hi", [1, D], F32R)
        bias_lo = sb("p_bias_lo", [1, D], F32R)
        one_row = sb("p_one_row", [1, P], F32R)
        diag = sb("p_diag", [P, 2, P])
        gate = K.gate
        o_in = sb("o_in", [P, 2, KT, CH])
        o_hi = sb("o_hi", [P, 2, KT, CH], F32R)
        o_lo = sb("o_lo", [P, 2, KT, CH], F32R)
        xs = sb("p_xs", [P, 2, TT, D])
        gated = sb("p_gated", [P, TT, D])
        xn = sb("p_xn", [P, TT, D])
        y = sb("p_y", [P, 2, KT, CH])
        bst = sb("p_bst", [P, TT, 6])
        mv = sb("p_mv", [P, TT, 2])
        ve = sb("p_ve", [P, TT])
        sd = sb("p_sd", [P, TT])
        rstd = sb("p_rstd", [P, TT])
        tmp = sb("p_tmp", [P, TT])
        tp = [pb(f"p_tp{i}", [P, CH]) for i in range(2)]
        acc = [pb(f"p_acc{i}", [P, D]) for i in range(TT)]
        gps = pb("p_gps", [P, D])

        w_loaded = sem("p_w_loaded")
        w_hi_ready = sem("p_w_hi_ready")
        w_split = sem("p_w_split")
        diag_ready = sem("p_diag_ready")
        gate_ready = sem("p_gate_ready")
        gate_done = sem("p_gate_done")
        chain = sem("p_dve_chain")
        o_loaded = [sem(f"p_o_loaded{u}") for u in range(2)]
        x_loaded = [sem(f"p_x_loaded{u}") for u in range(2)]
        hi_ready = sem("p_hi_ready")
        lo_ready = sem("p_lo_ready")
        acc_ready = sem("p_acc_ready")
        acc_free = sem("p_acc_free")
        x2_ready = sem("p_x2_ready")
        x2_stored = [sem(f"p_x2_stored{u}") for u in range(2)]
        var_ready = sem("p_var_ready")
        sd_ready = sem("p_sd_ready")
        xn_ready = sem("p_xn_ready")
        tp_ready = sem("p_tp_ready")
        y_ready = sem("p_y_ready")
        y_stored = [sem(f"p_y_stored{u}") for u in range(2)]
        held = sem("c_wait_carrier")
        block = ctx.enter_context(nc.Block())

        @block.sync
        def _(sp):
            sp.dma_start(bias[:, :], bproj.rearrange("(a n) -> a n", a=1)).then_inc(w_loaded, 16)
            sp.dma_start(w_raw[:, :, :], wproj.rearrange("(t p) n -> p t n", p=P)).then_inc(w_loaded, 16)

            def load_o(n, u):
                b = n // (NCH // BATCH)
                sp.dma_start(o_in[:, u, :, :],
                             K.o[bass.ds(b * KT, KT), :, bass.ds((n % (NCH // BATCH)) * CH, CH)].rearrange("g p n -> p g n")).then_inc(o_loaded[u], 16)

            def load_x(n, u):
                sp.dma_start(xs[:, u, :, :], x[bass.ds(n * CH, CH), :].rearrange("(t p) d -> p t d", p=P)).then_inc(x_loaded[u], 16)

            def store_x2(n, u):
                await_count(sp, held, x2_ready, TT * (n + 1))
                sp.dma_start(K.x2[bass.ds(n * CH, CH), :].rearrange("(t p) d -> p t d", p=P), xs[:, u, :, :]).then_inc(x2_stored[u], 16)

            def body(n, u, left):
                if left > 2:
                    await_count(sp, held, lo_ready, KT * (n + 2))
                    load_o(n + 3, 1 - u)
                if left > 1:
                    await_count(sp, held, xn_ready, TT * (n + 1))
                    await_count(sp, held, x2_stored[u], 16 * (n // 2) + 16)
                    load_x(n + 2, u)
                if left:
                    store_x2(n + 1, 1 - u)
                await_count(sp, held, y_ready, KT * (n + 1) + 2)
                sp.dma_start(K.xm2[:, bass.ds(n * CH, CH)].rearrange("(t p) n -> p t n", p=P), y[:, u, :, :]).then_inc(y_stored[u], 16)

            for u in range(2):
                load_o(u, u)
                load_x(u, u)
            for u in range(2):
                sp.sem_inc(y_stored[u], 16)
            await_count(sp, held, lo_ready, KT)
            load_o(2, 0)
            store_x2(0, 0)
            wave(nc.sync, body, NCH, 4)
            for u in range(2):
                sp.wait_ge(x2_stored[u], 16 * NCH // 2)
                sp.wait_ge(y_stored[u], 16 * NCH // 2 + 16)

        @block.gpsimd
        def _(pool):
            def low(n, u):
                for t in range(KT):
                    pool.wait_ge(hi_ready, KT * n + t + 1)
                    nc.gpsimd.tensor_tensor(o_lo[:, u, t, :], o_in[:, u, t, :], raw(o_hi[:, u, t, :]), ALU.subtract).then_inc(lo_ready, 1)

            def add(n, u):
                pool.wait_ge(x_loaded[u], 16 * (n // 2) + 16)
                for t in range(TT):
                    pool.wait_ge(acc_free, TT * n + t + 1)
                    nc.gpsimd.tensor_tensor(xs[:, u, t, :], gated[:, t, :], xs[:, u, t, :], ALU.add).then_inc(x2_ready, 1)

            def body(n, u, left):
                if left:
                    add(n + 1, 1 - u)
                if left > 2:
                    low(n + 3, 1 - u)

            low(0, 0)
            low(1, 1)
            add(0, 0)
            low(2, 0)
            wave(nc.gpsimd, body, NCH, 4)

        @block.scalar
        def _(act):
            act.wait_ge(w_loaded, 32)
            nc.scalar.activation(bias_hi[:, :], bias[:, :], ACT.Copy).then_inc(w_hi_ready, 1)
            nc.scalar.activation(w_hi[:, :, :], w_raw[:, :, :], ACT.Copy).then_inc(w_hi_ready, 1)

            def high(n, u):
                act.wait_ge(o_loaded[u], 16 * (n // 2) + 16)
                for t in range(KT):
                    nc.scalar.activation(o_hi[:, u, t, :], o_in[:, u, t, :], ACT.Copy).then_inc(hi_ready, 1)

            def std(n):
                act.wait_ge(var_ready, n + 1)
                nc.scalar.activation(sd[:, :], ve[:, :], ACT.Sqrt).then_inc(sd_ready, 1)

            def body(n, u, left):
                if left > 2:
                    act.wait_ge(acc_ready, TT * (n + 2))
                    high(n + 3, 1 - u)
                if left:
                    std(n + 1)

            high(0, 0)
            high(1, 1)
            act.wait_ge(acc_ready, TT)
            high(2, 0)
            std(0)
            wave(nc.scalar, body, NCH, 4)

        @block.vector
        def _(dve):
            links = [0]

            def link(ins):
                links[0] += 1
                ins.then_inc(chain, 1)
                dve.wait_ge(chain, links[0])

            n = 0
            for which, m in enumerate((M_GTA, M_GTM)):
                for b in range(BATCH):
                    for t in range(KT):
                        if n >= 2:
                            dve.wait_ge(gate_ready, n - 1)
                        nc.vector.tensor_scalar(diag[:, n % 2, :], K.ident[:, :], K.mod[:, b, m + t:m + t + 1], None,
                                                ALU.mult).then_inc(diag_ready, 1)
                        n += 1
                    dve.wait_ge(gate_ready, n)
                    nc.vector.tensor_copy(gate[:, which, b, :], gps[:, :]).then_inc(gate_done, 1)
            link(nc.vector.memset(raw(one_row[:, :]), 1.0))
            dve.wait_ge(w_hi_ready, 1)
            link(nc.vector.tensor_tensor(bias_lo[:, :], bias[:, :], raw(bias_hi[:, :]), ALU.subtract))
            dve.wait_ge(w_hi_ready, 2)
            nc.vector.tensor_tensor(w_lo[:, :, :], w_raw[:, :, :], raw(w_hi[:, :, :]), ALU.subtract).then_inc(w_split, 1)
            dve.wait_ge(gate_done, 2 * BATCH)
            dve.sem_inc(y_ready, 2)
            base = links[0]
            CHAINS = 2 + 5

            def of_batch(n, t, *rest):
                b = n // (NCH // BATCH)
                return t[(slice(None), *((b if isinstance(b, int) else bass.ds(b, 1)) if r is None else r for r in rest))]

            def gating(n, u):
                for t in range(TT):
                    dve.wait_ge(acc_ready, TT * n + t + 1)
                    nc.vector.tensor_tensor(gated[:, t, :], acc[t][:, :], of_batch(n, gate, 0, None, slice(None)),
                                            ALU.mult).then_inc(acc_free, 1)

            def norm(n, u):
                at = [0]

                def lk(ins):
                    at[0] += 1
                    ins.then_inc(chain, 1)
                    dve.wait_ge(chain, n * CHAINS + base + at[0])

                for t in range(TT):
                    dve.wait_ge(x2_ready, TT * n + t + 1)
                    ins = nc.vector.bn_stats(bst[:, t, :], xs[:, u, t, :])
                lk(ins)
                dve.sem_inc(held, 1)
                for t in range(TT - 1):
                    nc.vector.bn_aggr(mv[:, t, :], bst[:, t, :])
                lk(nc.vector.bn_aggr(mv[:, TT - 1, :], bst[:, TT - 1, :]))
                nc.vector.tensor_scalar(ve[:, :], mv[:, :, 1], EPS, None, ALU.add).then_inc(var_ready, 1)
                dve.wait_ge(sd_ready, n + 1)
                newton_rstd(nc, dve, lk, ve[:, :], sd[:, :], rstd[:, :], tmp[:, :])
                for t in range(TT):
                    nc.vector.tensor_scalar(xn[:, t, :], xs[:, u, t, :], mv[:, t, 0:1], rstd[:, t:t + 1],
                                            ALU.subtract, ALU.mult).then_inc(xn_ready, 1)

            def modulate(n, u):
                dve.wait_ge(y_stored[u], 16 * (n // 2) + 16)
                for t in range(KT):
                    dve.wait_ge(tp_ready, n * KT + t + 1)
                    nc.vector.tensor_scalar(y[:, u, t, :], tp[t % 2][:, :], of_batch(n, K.aff2, None, 0, slice(t, t + 1)),
                                            of_batch(n, K.aff2, None, 1, slice(t, t + 1)), ALU.mult, ALU.add).then_inc(y_ready, 1)

            def body(n, u, left):
                if left:
                    dve.wait_ge(x2_ready, TT * (n + 1))
                    gating(n + 1, 1 - u)
                modulate(n, u)
                if left:
                    norm(n + 1, 1 - u)

            gating(0, 0)
            norm(0, 0)
            wave(nc.vector, body, NCH, 4)

        @block.tensor
        def _(pe):
            for n in range(2 * BATCH * KT):
                pe.wait_ge(diag_ready, n + 1)
                if n % KT == 0 and n:
                    pe.wait_ge(gate_done, n // KT)
                nc.tensor.matmul(gps[:, (n % KT) * P:(n % KT + 1) * P], K.ones[:, :], diag[:, n % 2, :],
                                 start=True, stop=True).then_inc(gate_ready, 1)
            pe.wait_ge(w_split, 1)

            def project(n, u, s):
                pe.wait_ge(lo_ready, KT * (n + 1))
                cols = slice(s * P, (s + 1) * P)
                nc.tensor.matmul(acc[s][:, :], one_row[:, :], bias_hi[:, :], start=True, stop=False)
                nc.tensor.matmul(acc[s][:, :], one_row[:, :], bias_lo[:, :], start=False, stop=False)
                for t in range(KT):
                    for k, (a, b) in enumerate(terms(o_hi[:, u, t, cols], o_lo[:, u, t, cols], w_hi[:, t, :], w_lo[:, t, :])):
                        ins = nc.tensor.matmul(acc[s][:, :], a, b, start=False, stop=(t == KT - 1 and k == 2))
                ins.then_inc(acc_ready, 1)

            def turn(n, t):
                pe.wait_ge(y_ready, n * KT + t + 1)
                if t == 0:
                    pe.wait_ge(xn_ready, TT * (n + 1))
                for s in range(TT):
                    ins = nc.tensor.transpose(tp[t % 2][:, s * P:(s + 1) * P], xn[:, s, t * P:(t + 1) * P], K.ident[:, :])
                ins.then_inc(tp_ready, 1)

            def body(n, u, left):
                for s in range(TT):
                    for t in range(2 * s, min(2 * s + 2, KT)):
                        turn(n, t)
                    if left > 1:
                        pe.wait_ge(acc_free, TT * (n + 1) + s + 1)
                        project(n + 2, u, s)

            for s in range(TT):
                project(0, 0, s)
            for s in range(TT):
                pe.wait_ge(acc_free, s + 1)
                project(1, 1, s)
            wave(nc.tensor, body, NCH, 4)


def phase_mlp(nc, K, w1, w2, b2, out):
    with ExitStack() as ctx:
        def sb(name, shape, dt=F32):
            return ctx.enter_context(nc.sbuf_tensor(name, shape, dt))

        def pb(name, shape):
            return ctx.enter_context(nc.psum_tensor(name, shape, F32))

        def sem(name):
            return ctx.enter_context(nc.semaphore(name))

        PIECE = CH
        NP = HID // PIECE
        LAG = 2
        w1_hi = sb("w1_hi", [P, NP, KT, PIECE], F32R)
        w1_lo = sb("w1_lo", [P, NP, KT, PIECE], F32R)
        w2_hi = sb("w2_hi", [P, NP, KT, D], F32R)
        w2_lo = sb("w2_lo", [P, NP, KT, D], F32R)
        bias = sb("m_bias", [1, D])
        bias_hi = sb("m_bias_hi", [1, D], F32R)
        bias_lo = sb("m_bias_lo", [1, D], F32R)
        one_row = sb("m_one_row", [1, P], F32R)
        gbias = sb("m_gbias", [P, BATCH, D])
        xr = sb("m_xr", [P, KT, CH])
        xm_hi = sb("m_xm_hi", [P, KT, CH], F32R)
        xm_lo = sb("m_xm_lo", [P, KT, CH], F32R)
        xs = sb("m_xs", [P, TT, D])
        g32 = sb("m_g32", [P, 2, CH])
        g_hi = sb("m_g_hi", [P, 4, CH], F32R)
        g_lo = sb("m_g_lo", [P, 4, CH], F32R)
        gated = sb("m_gated", [P, 1, D])
        hid = [pb(f"m_hid{i}", [P, CH]) for i in range(4)]
        acc = [pb(f"m_acc{i}", [P, D]) for i in range(TT)]

        b_loaded = sem("m_b_loaded")
        w_loaded = [sem(f"m_w_loaded{u}") for u in range(2)]
        w_hi_ready = sem("m_w_hi_ready")
        w_split = sem("m_w_split")
        bias_ready = sem("m_bias_ready")
        rows_ready = sem("m_bias_rows_ready")
        gbias_ready = sem("m_gbias_ready")
        x_ready = sem("m_x_ready")
        xm_loaded = sem("m_xm_loaded")
        xm_hi_ready = sem("m_xm_hi_ready")
        xm_split = sem("m_xm_split")
        x_loaded = sem("m_x_loaded")
        hid_ready = sem("m_hid_ready")
        hid_free = sem("m_hid_free")
        g_hi_ready = sem("m_g_hi_ready")
        g_ready = sem("m_g_ready")
        used = sem("m_used")
        acc_ready = sem("m_acc_ready")
        acc_free = sem("m_acc_free")
        out_ready = sem("m_out_ready")
        out_stored = sem("m_out_stored")
        held = sem("m_wait_carrier")
        block = ctx.enter_context(nc.Block())

        def staged(i):
            return xs[:, i % 2 * 2:i % 2 * 2 + 2, :]

        def piece(i, w1_part, w2_part):
            half = slice(i % 2 * 2, i % 2 * 2 + 2)
            return (w1_part if i % 4 < 2 else w2_part)[:, i // 4, half, :]

        @block.sync
        def _(sp):
            def load_piece(i):
                k, half = i // 4, i % 2 * 2 * P
                src = w1[half:half + 2 * P, k * PIECE:(k + 1) * PIECE] if i % 4 < 2 else \
                    w2[k * CH + half:k * CH + half + 2 * P, :]
                sp.dma_start(staged(i), src.rearrange("(t p) n -> p t n", p=P)).then_inc(w_loaded[i % 2], 16)

            def load_xm(n):
                sp.dma_start(xr[:, :, :], K.xm2[:, bass.ds(n * CH, CH)].rearrange("(t p) n -> p t n", p=P)).then_inc(xm_loaded, 16)

            def load_x(n):
                sp.dma_start(xs[:, :, :], K.x2[bass.ds(n * CH, CH), :].rearrange("(t p) d -> p t d", p=P)).then_inc(x_loaded, 16)

            sp.dma_start(bias[:, :], b2.rearrange("(a n) -> a n", a=1)).then_inc(b_loaded, 16)
            load_piece(0)
            load_piece(1)
            load_xm(0)
            for i in range(2, 4 * NP):
                await_count(sp, held, w_split, i - 1)
                load_piece(i)
            await_count(sp, held, w_split, 4 * NP)
            load_x(0)

            def body(n, more):
                if more:
                    await_count(sp, held, xm_split, KT * (n + 1))
                    load_xm(n + 1)
                await_count(sp, held, out_ready, TT * (n + 1))
                sp.dma_start(out[bass.ds(n * CH, CH), :].rearrange("(t p) d -> p t d", p=P), xs[:, :, :]).then_inc(out_stored, 16)
                await_count(sp, held, out_stored, 16 * (n + 1))
                if more:
                    load_x(n + 1)

            with nc.sync.Fori(0, NCH - 1) as n:
                body(n, True)
            body(NCH - 1, False)

        @block.gpsimd
        def _(pool):
            pass

        @block.scalar
        def _(act):
            def high(i):
                act.wait_ge(w_loaded[i % 2], 16 * (i // 2 + 1))
                nc.scalar.activation(piece(i, w1_hi, w2_hi), staged(i), ACT.Copy).then_inc(w_hi_ready, 1)

            def tile(n, j):
                act.wait_ge(hid_ready, HT * n + j + 1)
                act.wait_ge(g_ready, HT * n + j + 1)
                nc.scalar.activation(g32[:, j % 2, :], hid[j % 4][:, :], ACT.Gelu,
                                     bias=K.vcol[:, V_B1 + j:V_B1 + j + 1]).then_inc(hid_free, 1)
                act.wait_ge(hid_free, HT * n + j + 1 + 4)
                act.wait_ge(used, HT * n + j + 1)
                nc.scalar.activation(g_hi[:, j % 4, :], g32[:, j % 2, :], ACT.Copy).then_inc(g_hi_ready, 1)

            def xm_high(n):
                act.wait_ge(xm_loaded, 16 * (n + 1))
                for t in range(KT):
                    nc.scalar.activation(xm_hi[:, t, :], xr[:, t, :], ACT.Copy).then_inc(xm_hi_ready, 1)

            act.wait_ge(b_loaded, 16)
            nc.scalar.activation(bias_hi[:, :], bias[:, :], ACT.Copy).then_inc(bias_ready, 1)
            for i in range(2):
                high(i)
            xm_high(0)
            for i in range(2, 4):
                high(i)
            for j in range(HT):
                if j // KT < NP - 1:
                    high(j + 4)
                tile(0, j)
            xm_high(1)
            with nc.scalar.Fori(1, NCH - 1) as n:
                for j in range(HT):
                    tile(n, j)
                xm_high(n + 1)
            for j in range(HT):
                tile(NCH - 1, j)

        @block.vector
        def _(dve):
            def low(i):
                dve.wait_ge(w_hi_ready, i + 1)
                nc.vector.tensor_tensor(piece(i, w1_lo, w2_lo), staged(i), raw(piece(i, w1_hi, w2_hi)), ALU.subtract).then_inc(w_split, 1)

            def tile(n, j):
                dve.wait_ge(g_hi_ready, HT * n + j + 1)
                nc.vector.tensor_tensor(g_lo[:, j % 4, :], g32[:, j % 2, :], raw(g_hi[:, j % 4, :]),
                                        ALU.subtract).then_inc(g_ready, 1)

            def xm_low(n):
                for t in range(KT):
                    dve.wait_ge(xm_hi_ready, KT * n + t + 1)
                    nc.vector.tensor_tensor(xm_lo[:, t, :], xr[:, t, :], raw(xm_hi[:, t, :]), ALU.subtract).then_inc(xm_split, 1)

            def finish(n, gate, gated_bias):
                dve.wait_ge(x_loaded, 16 * (n + 1))
                for s in range(TT):
                    nc.vector.tensor_tensor(xs[:, s, :], gated_bias, xs[:, s, :], ALU.add).then_inc(x_ready, 1)
                dve.wait_ge(x_ready, TT * (n + 1))
                for s in range(TT):
                    dve.wait_ge(acc_ready, TT * n + s + 1)
                    nc.vector.tensor_tensor(gated[:, 0, :], acc[s][:, :], gate, ALU.mult).then_inc(acc_free, 1)
                    dve.wait_ge(acc_free, TT * n + s + 1 + TT)
                    nc.vector.tensor_tensor(xs[:, s, :], gated[:, 0, :], xs[:, s, :], ALU.add).then_inc(out_ready, 1)
                    dve.wait_ge(out_ready, TT * n + s + 1)

            nc.vector.memset(raw(one_row[:, :]), 1.0).then_inc(bias_ready, 1)
            dve.wait_ge(bias_ready, 2)
            nc.vector.tensor_tensor(bias_lo[:, :], bias[:, :], raw(bias_hi[:, :]), ALU.subtract).then_inc(bias_ready, 1)
            for i in range(2):
                low(i)
            xm_low(0)
            for i in range(2, 4):
                low(i)
            dve.sem_inc(hid_free, 4)
            dve.sem_inc(g_ready, 2)
            dve.wait_ge(rows_ready, 1)
            for b in range(BATCH):
                nc.vector.tensor_tensor(gbias[:, b, :], acc[0][:, :], K.gate[:, 1, b, :], ALU.mult).then_inc(gbias_ready, 1)
            dve.wait_ge(gbias_ready, BATCH)
            dve.sem_inc(acc_free, TT)
            for j in range(HT):
                if j // KT < NP - 1:
                    low(j + 4)
                tile(0, j)
            xm_low(1)
            finish(0, K.gate[:, 1, 0, :], gbias[:, 0, :])
            with nc.vector.Fori(1, NCH - 1) as n:
                for j in range(HT):
                    tile(n, j)
                xm_low(n + 1)
                b = n // (NCH // BATCH)
                finish(n, K.gate[:, 1, bass.ds(b, 1), :], gbias[:, bass.ds(b, 1), :])
            for j in range(HT):
                tile(NCH - 1, j)
            finish(NCH - 1, K.gate[:, 1, BATCH - 1, :], gbias[:, BATCH - 1, :])

        @block.tensor
        def _(pe):
            pe.sem_inc(used, 4)
            pe.wait_ge(bias_ready, 3)
            nc.tensor.matmul(acc[0][:, :], one_row[:, :], bias_hi[:, :], start=True, stop=False)
            nc.tensor.matmul(acc[0][:, :], one_row[:, :], bias_lo[:, :], start=False, stop=True).then_inc(rows_ready, 1)

            def multiply(n, j):
                if j % KT == 0:
                    pe.wait_ge(w_split, 4 * (j // KT) + 4)
                pe.wait_ge(g_ready, HT * n + j + 1 + 2)
                for s in range(TT):
                    if j == 0:
                        pe.wait_ge(acc_free, TT * n + s + 1)
                    cols = slice(s * P, (s + 1) * P)
                    for k, (a, b) in enumerate(terms(g_hi[:, j % 4, cols], g_lo[:, j % 4, cols],
                                                     w2_hi[:, j // KT, j % KT, :], w2_lo[:, j // KT, j % KT, :])):
                        ins = nc.tensor.matmul(acc[s][:, :], a, b, start=(j == 0 and k == 0), stop=(j == HT - 1 and k == 2))
                    if j == HT - 1:
                        ins.then_inc(acc_ready, 1)
                if j < HT - 1:
                    ins.then_inc(used, 1)
                else:
                    pe.wait_ge(acc_ready, TT * (n + 1))
                    pe.sem_inc(used, 1)

            with nc.tensor.Fori(0, NCH) as n:
                for j in range(HT + LAG):
                    if j < HT:
                        if j % KT == 0:
                            pe.wait_ge(w_split, 4 * (j // KT) + 2)
                        pe.wait_ge(hid_free, HT * n + j + 1)
                        cols = slice((j % KT) * P, (j % KT + 1) * P)
                        for t in range(KT):
                            if j == 0:
                                pe.wait_ge(xm_split, KT * n + t + 1)
                            for k, (a, b) in enumerate(terms(w1_hi[:, j // KT, t, cols], w1_lo[:, j // KT, t, cols],
                                                             xm_hi[:, t, :], xm_lo[:, t, :])):
                                ins = nc.tensor.matmul(hid[j % 4][:, :], a, b, start=(t == 0 and k == 0),
                                                       stop=(t == KT - 1 and k == 2))
                        ins.then_inc(hid_ready, 1)
                    if j >= LAG:
                        multiply(n, j - LAG)


def build(nc, x, cond, wqkv, wproj, bproj, w1, b1, w2, b2, g1, be1, g2, be2, wada, bada, out, phases="abcd"):
    x = x.rearrange("b t d -> (b t) d")
    out = out.rearrange("b t d -> (b t) d")
    vecs = [(V_BADA, bada), (V_G1, g1), (V_BE1, be1), (V_G2, g2), (V_BE2, be2), (V_B1, b1)]
    with ExitStack() as ctx:
        K = Common(nc, ctx)
        phase_qkv(nc, K, x, cond, wada, bada, vecs, wqkv)
        if "b" in phases:
            phase_attention(nc, K, wada)
        if "c" in phases:
            phase_project(nc, K, x, wproj, bproj)
        if "d" in phases:
            phase_mlp(nc, K, w1, w2, b2, out)


_INS = ['x', 'cond_1024', 'L0_cond_Wqkv', 'L0_cond_Wproj', 'L0_cond_bproj', 'L0_cond_W1', 'L0_cond_b1',
        'L0_cond_W2', 'L0_cond_b2', 'L0_cond_g1', 'L0_cond_be1', 'L0_cond_g2', 'L0_cond_be2',
        'L0_cond_Wada', 'L0_cond_bada']
_OUTS = [((2, 2048, 512), 'float32')]


def kernel(**inputs):
    import numpy as _np
    import concourse.bacc as _bacc
    from concourse import mybir as _mybir
    from concourse.bass_utils import run_bass_kernel_spmd as _run

    nc = _bacc.Bacc("TRN2", target_bir_lowering=False, num_devices=1)
    arrays, args = {}, []
    for name in _INS:
        a = _np.ascontiguousarray(inputs[name])
        arrays[f"in_{name}_dram"] = a
        args.append(nc.dram_tensor(f"in_{name}_dram", a.shape, _mybir.dt.from_np(a.dtype), kind="ExternalInput").ap())
    for i, (shape, dtype) in enumerate(_OUTS):
        dt = _mybir.dt.from_np(_np.dtype(dtype))
        args.append(nc.dram_tensor(f"out_{i}_dram", shape, dt, kind="ExternalOutput").ap())
    build(nc, *args)
    r = _run(nc, [arrays], core_ids=[0])
    return r.results[0]["out_0_dram"]
```
